# Optimizing a Trainium2 kernel written in Bass

```python
import numpy as np
import jax
import jax.numpy as jnp

def _softmax(x, axis=-1):
    return jax.nn.softmax(x, axis=axis)

def _gelu(x):
    return jax.nn.gelu(x, approximate=True)

def _silu(x):
    return jax.nn.silu(x)

def _sigmoid(x):
    return jax.nn.sigmoid(x)

def _layernorm(x, axis=-1, eps=1e-05):
    m = jnp.mean(x, axis=axis, keepdims=True)
    v = jnp.var(x, axis=axis, keepdims=True)
    return (x - m) / jnp.sqrt(v + eps)

def _scatter_add(tgt, idx, src, axis=0):
    return tgt.at[idx].add(src)

def _segment_sum(src, seg, n):
    return jax.ops.segment_sum(src, seg, n)
kernel_name = 'mk_vit_tower_cls_d1_tok_img768_r4_961a9b'

def setup_inputs(seed: int=0):
    np.random.seed(seed)
    _w = jnp.asarray

    def _rec_inputs():
        import jax
        import jax.numpy as jnp
        _rk = jax.random.key(seed)
        x = -0.000596345 + 1.00056 * jax.random.normal(jax.random.fold_in(_rk, 1), (4, 3, 64, 64), jnp.float32)
        cls_tok = 0.02 * jax.random.normal(jax.random.fold_in(_rk, 5), (1, 1, 192), jnp.float32)
        return (x, cls_tok)
    x, cls_tok = _rec_inputs()

    def _L0_tok_setup():
        import jax, jax.numpy as jnp
        import numpy as np
        B = 16
        IMG = 64
        CH = 3
        EMBED = 64
        GP = 16
        PRE = [1, 2, 4]
        N_LEVELS = 3
        FUSED = EMBED * N_LEVELS

        def hilbert_flat_indices(n):
            t = np.arange(n * n, dtype=np.int64)
            x = np.zeros(n * n, dtype=np.int64)
            y = np.zeros(n * n, dtype=np.int64)
            s = 1
            while s < n:
                rx = 1 & t // 2
                ry = 1 & (t ^ rx)
                swap = ry == 0
                flip = swap & (rx == 1)
                x = np.where(flip, s - 1 - x, x)
                y = np.where(flip, s - 1 - y, y)
                x2 = np.where(swap, y, x)
                y2 = np.where(swap, x, y)
                x, y = (x2, y2)
                x = x + s * rx
                y = y + s * ry
                t = t // 4
                s *= 2
            return y * n + x

        def _level(x, idx, W, b, p, gp):
            Bsz, C, H, _ = x.shape
            h = H // p
            t = x.reshape(Bsz, C, h, p, h, p).transpose(0, 2, 4, 3, 5, 1).reshape(Bsz, h * h, p * p * C)
            t = t[:, idx]
            t = t.reshape(Bsz, h * h // gp, gp * p * p * C)
            return t @ W.T + b

        def _interp_linear(x, n_out):
            L = x.shape[1]
            pos = (jnp.arange(n_out, dtype=jnp.float32) + 0.5) * (L / n_out) - 0.5
            pos = jnp.clip(pos, 0.0, L - 1)
            i0 = jnp.floor(pos).astype(jnp.int32)
            i1 = jnp.minimum(i0 + 1, L - 1)
            w = (pos - i0).astype(x.dtype)
            return x[:, i0] * (1.0 - w)[None, :, None] + x[:, i1] * w[None, :, None]
        key = jax.random.key(seed)
        ks = jax.random.split(key, 9)
        inp = {'x': jax.random.normal(ks[0], (B, CH, IMG, IMG), jnp.float32)}
        for i, p in enumerate(PRE):
            din = CH * p * p * GP
            inp[f'W{i}'] = jax.random.normal(ks[1 + 2 * i], (EMBED, din), jnp.float32) * din ** (-0.5)
            inp[f'b{i}'] = jax.random.normal(ks[2 + 2 * i], (EMBED,), jnp.float32) * 0.02
        inp['Wf'] = jax.random.normal(ks[7], (FUSED, FUSED), jnp.float32) * FUSED ** (-0.5)
        inp['bf'] = jax.random.normal(ks[8], (FUSED,), jnp.float32) * 0.02
        for i, p in enumerate(PRE):
            inp[f'idx{i}'] = jnp.asarray(hilbert_flat_indices(IMG // p), jnp.int32)
        return inp
    _L0_tok_all = _L0_tok_setup()
    _L0_tok_in = {k: v for k, v in _L0_tok_all.items() if k in ('W0', 'b0', 'W1', 'b1', 'W2', 'b2', 'Wf', 'bf', 'idx0', 'idx1', 'idx2')}
    del _L0_tok_all

    def _L0_attn_setup():
        import jax, jax.numpy as jnp
        import numpy as np
        B, T, D, H = (4, 1024, 192, 12)
        K, V, LR = (D // 2, D, 16)
        HK, HV = (K // H, V // H)
        EPS = 1e-05
        GATE_LOGIT_NORMALIZER = 16.0
        SCALE = HK ** (-0.5)

        def _gla_forward(x, Wq, Wk, Wv, Wgk1, Wgk2, bgk2, Wg, o_norm_w, Wo):
            b, t, _ = x.shape
            q = (x @ Wq).reshape(b, t, H, HK) * SCALE
            kk = (x @ Wk).reshape(b, t, H, HK)
            v = (x @ Wv).reshape(b, t, H, HV)
            gk = jax.nn.log_sigmoid(x @ Wgk1 @ Wgk2 + bgk2) / GATE_LOGIT_NORMALIZER
            gk = gk.reshape(b, t, H, HK)
            qs, ks, vs, gs = (jnp.moveaxis(a, 1, 0) for a in (q, kk, v, gk))

            def step(S, inp):
                q_t, k_t, v_t, g_t = inp
                S = S * jnp.exp(g_t)[..., None] + k_t[..., None] * v_t[..., None, :]
                o_t = jnp.einsum('bhk,bhkv->bhv', q_t, S)
                return (S, o_t)
            S0 = jnp.zeros((b, H, HK, HV), x.dtype)
            _, o = jax.lax.scan(step, S0, (qs, ks, vs, gs))
            o = jnp.moveaxis(o, 0, 1)
            g = (x @ Wg).reshape(b, t, H, HV)
            rms = o * jax.lax.rsqrt(jnp.mean(o * o, axis=-1, keepdims=True) + EPS) * o_norm_w
            o = rms * (g * jax.nn.sigmoid(g))
            return o.reshape(b, t, V) @ Wo
        key = jax.random.key(seed)
        k = jax.random.split(key, 9)

        def w(kk, shape, fan_in):
            return jax.random.normal(kk, shape, jnp.float32) * fan_in ** (-0.5)
        return {'x': jax.random.normal(k[0], (B, T, D), jnp.float32), 'Wq': w(k[1], (D, K), D), 'Wk': w(k[2], (D, K), D), 'Wv': w(k[3], (D, V), D), 'Wgk1': w(k[4], (D, LR), D), 'Wgk2': w(k[5], (LR, K), LR), 'bgk2': jnp.zeros((K,), jnp.float32), 'Wg': w(k[6], (D, V), D), 'o_norm_w': jnp.ones((HV,), jnp.float32), 'Wo': w(k[7], (V, D), V)}
    _L0_attn_all = _L0_attn_setup()
    _L0_attn_in = {k: v for k, v in _L0_attn_all.items() if k in ('Wq', 'Wk', 'Wv', 'Wgk1', 'Wgk2', 'bgk2', 'Wg', 'o_norm_w', 'Wo')}
    del _L0_attn_all

    def _L0_ffn_setup():
        import jax, jax.numpy as jnp
        import numpy as np
        B_SZ, S, D = (8, 128, 192)
        H = 12
        N_EXP = 8
        RANK = 16
        ALPHA = 32
        TOP_K = 2
        key = jax.random.key(seed)
        ks = jax.random.split(key, 9)
        x = jax.random.normal(ks[0], (B_SZ, S, D), jnp.float32)
        W_qkv = jax.random.normal(ks[1], (3 * D, D), jnp.float32) * 0.02
        b_qkv = jnp.zeros((3 * D,), jnp.float32)
        W_gate = jax.random.normal(ks[2], (N_EXP, D), jnp.float32) * 0.02
        b_gate = jnp.zeros((N_EXP,), jnp.float32)
        A = jax.random.normal(ks[3], (N_EXP, RANK, D), jnp.float32) * 0.02
        B_lora = jax.random.normal(ks[4], (N_EXP, 3 * D, RANK), jnp.float32) * 0.02
        W_proj = jax.random.normal(ks[5], (D, D), jnp.float32) * 0.02
        b_proj = jnp.zeros((D,), jnp.float32)
        return {'x': x, 'W_qkv': W_qkv, 'b_qkv': b_qkv, 'W_gate': W_gate, 'b_gate': b_gate, 'A': A, 'B_lora': B_lora, 'W_proj': W_proj, 'b_proj': b_proj}
    _L0_ffn_all = _L0_ffn_setup()
    _L0_ffn_in = {k: v for k, v in _L0_ffn_all.items() if k in ('W_qkv', 'b_qkv', 'W_gate', 'b_gate', 'A', 'B_lora', 'W_proj', 'b_proj')}
    del _L0_ffn_all
    return {'x': x, 'cls_tok': cls_tok, 'L0_tok_W0': _L0_tok_in['W0'], 'L0_tok_b0': _L0_tok_in['b0'], 'L0_tok_W1': _L0_tok_in['W1'], 'L0_tok_b1': _L0_tok_in['b1'], 'L0_tok_W2': _L0_tok_in['W2'], 'L0_tok_b2': _L0_tok_in['b2'], 'L0_tok_Wf': _L0_tok_in['Wf'], 'L0_tok_bf': _L0_tok_in['bf'], 'L0_tok_idx0': _L0_tok_in['idx0'], 'L0_tok_idx1': _L0_tok_in['idx1'], 'L0_tok_idx2': _L0_tok_in['idx2'], 'L0_attn_Wq': _L0_attn_in['Wq'], 'L0_attn_Wk': _L0_attn_in['Wk'], 'L0_attn_Wv': _L0_attn_in['Wv'], 'L0_attn_Wgk1': _L0_attn_in['Wgk1'], 'L0_attn_Wgk2': _L0_attn_in['Wgk2'], 'L0_attn_bgk2': _L0_attn_in['bgk2'], 'L0_attn_Wg': _L0_attn_in['Wg'], 'L0_attn_o_norm_w': _L0_attn_in['o_norm_w'], 'L0_attn_Wo': _L0_attn_in['Wo'], 'L0_ffn_W_qkv': _L0_ffn_in['W_qkv'], 'L0_ffn_b_qkv': _L0_ffn_in['b_qkv'], 'L0_ffn_W_gate': _L0_ffn_in['W_gate'], 'L0_ffn_b_gate': _L0_ffn_in['b_gate'], 'L0_ffn_A': _L0_ffn_in['A'], 'L0_ffn_B_lora': _L0_ffn_in['B_lora'], 'L0_ffn_W_proj': _L0_ffn_in['W_proj'], 'L0_ffn_b_proj': _L0_ffn_in['b_proj']}

def reference(x, cls_tok, L0_tok_W0, L0_tok_b0, L0_tok_W1, L0_tok_b1, L0_tok_W2, L0_tok_b2, L0_tok_Wf, L0_tok_bf, L0_tok_idx0, L0_tok_idx1, L0_tok_idx2, L0_attn_Wq, L0_attn_Wk, L0_attn_Wv, L0_attn_Wgk1, L0_attn_Wgk2, L0_attn_bgk2, L0_attn_Wg, L0_attn_o_norm_w, L0_attn_Wo, L0_ffn_W_qkv, L0_ffn_b_qkv, L0_ffn_W_gate, L0_ffn_b_gate, L0_ffn_A, L0_ffn_B_lora, L0_ffn_W_proj, L0_ffn_b_proj):
    import jax
    import jax.numpy as jnp

    def _L0_tok_ref(x, W0, b0, W1, b1, W2, b2, Wf, bf, idx0, idx1, idx2):
        import jax, jax.numpy as jnp
        import numpy as np
        B = 16
        IMG = 64
        CH = 3
        EMBED = 64
        GP = 16
        PRE = [1, 2, 4]
        N_LEVELS = 3
        FUSED = EMBED * N_LEVELS

        def hilbert_flat_indices(n):
            t = np.arange(n * n, dtype=np.int64)
            x = np.zeros(n * n, dtype=np.int64)
            y = np.zeros(n * n, dtype=np.int64)
            s = 1
            while s < n:
                rx = 1 & t // 2
                ry = 1 & (t ^ rx)
                swap = ry == 0
                flip = swap & (rx == 1)
                x = np.where(flip, s - 1 - x, x)
                y = np.where(flip, s - 1 - y, y)
                x2 = np.where(swap, y, x)
                y2 = np.where(swap, x, y)
                x, y = (x2, y2)
                x = x + s * rx
                y = y + s * ry
                t = t // 4
                s *= 2
            return y * n + x

        def _level(x, idx, W, b, p, gp):
            Bsz, C, H, _ = x.shape
            h = H // p
            t = x.reshape(Bsz, C, h, p, h, p).transpose(0, 2, 4, 3, 5, 1).reshape(Bsz, h * h, p * p * C)
            t = t[:, idx]
            t = t.reshape(Bsz, h * h // gp, gp * p * p * C)
            return t @ W.T + b

        def _interp_linear(x, n_out):
            L = x.shape[1]
            pos = (jnp.arange(n_out, dtype=jnp.float32) + 0.5) * (L / n_out) - 0.5
            pos = jnp.clip(pos, 0.0, L - 1)
            i0 = jnp.floor(pos).astype(jnp.int32)
            i1 = jnp.minimum(i0 + 1, L - 1)
            w = (pos - i0).astype(x.dtype)
            return x[:, i0] * (1.0 - w)[None, :, None] + x[:, i1] * w[None, :, None]
        Ws = [(idx0, W0, b0, PRE[0]), (idx1, W1, b1, PRE[1]), (idx2, W2, b2, PRE[2])]
        outs = [_level(x, idx, W, b, p, GP) for idx, W, b, p in Ws]
        n_tokens = outs[0].shape[1]
        outs = [outs[0]] + [_interp_linear(o, n_tokens) for o in outs[1:]]
        y = jnp.concatenate(outs, axis=-1)
        return y @ Wf.T + bf

    def _L0_attn_ref(x, Wq, Wk, Wv, Wgk1, Wgk2, bgk2, Wg, o_norm_w, Wo):
        import jax, jax.numpy as jnp
        import numpy as np
        B, T, D, H = (4, 1024, 192, 12)
        K, V, LR = (D // 2, D, 16)
        HK, HV = (K // H, V // H)
        EPS = 1e-05
        GATE_LOGIT_NORMALIZER = 16.0
        SCALE = HK ** (-0.5)

        def _gla_forward(x, Wq, Wk, Wv, Wgk1, Wgk2, bgk2, Wg, o_norm_w, Wo):
            b, t, _ = x.shape
            q = (x @ Wq).reshape(b, t, H, HK) * SCALE
            kk = (x @ Wk).reshape(b, t, H, HK)
            v = (x @ Wv).reshape(b, t, H, HV)
            gk = jax.nn.log_sigmoid(x @ Wgk1 @ Wgk2 + bgk2) / GATE_LOGIT_NORMALIZER
            gk = gk.reshape(b, t, H, HK)
            qs, ks, vs, gs = (jnp.moveaxis(a, 1, 0) for a in (q, kk, v, gk))

            def step(S, inp):
                q_t, k_t, v_t, g_t = inp
                S = S * jnp.exp(g_t)[..., None] + k_t[..., None] * v_t[..., None, :]
                o_t = jnp.einsum('bhk,bhkv->bhv', q_t, S)
                return (S, o_t)
            S0 = jnp.zeros((b, H, HK, HV), x.dtype)
            _, o = jax.lax.scan(step, S0, (qs, ks, vs, gs))
            o = jnp.moveaxis(o, 0, 1)
            g = (x @ Wg).reshape(b, t, H, HV)
            rms = o * jax.lax.rsqrt(jnp.mean(o * o, axis=-1, keepdims=True) + EPS) * o_norm_w
            o = rms * (g * jax.nn.sigmoid(g))
            return o.reshape(b, t, V) @ Wo
        return _gla_forward(x, Wq, Wk, Wv, Wgk1, Wgk2, bgk2, Wg, o_norm_w, Wo)

    def _L0_ffn_ref(x, W_qkv, b_qkv, W_gate, b_gate, A, B_lora, W_proj, b_proj):
        import jax, jax.numpy as jnp
        import numpy as np
        B_SZ, S, D = (8, 128, 192)
        H = 12
        N_EXP = 8
        RANK = 16
        ALPHA = 32
        TOP_K = 2
        b, s, d = x.shape
        n_exp, rank = (A.shape[0], A.shape[1])
        scaling = ALPHA / rank
        head_dim = d // H
        scale = head_dim ** (-0.5)
        t = b * s
        x_flat = x.reshape(t, d)
        qkv_base = x @ W_qkv.T + b_qkv
        logits = x_flat @ W_gate.T + b_gate
        router_probs = jax.nn.softmax(logits, axis=-1)
        top_k_weights, top_k_indices = jax.lax.top_k(router_probs, TOP_K)
        a_down = jnp.einsum('td,nrd->tnr', x_flat, A)
        expert_out = jnp.einsum('tnr,nor->tno', a_down, B_lora) * scaling
        dispatch = jnp.zeros((t, n_exp), x.dtype).at[jnp.arange(t)[:, None], top_k_indices].add(top_k_weights)
        sparse_out = jnp.einsum('tno,tn->to', expert_out, dispatch)
        qkv = qkv_base + sparse_out.reshape(b, s, 3 * d)
        qkv = qkv.reshape(b, s, 3, H, head_dim).transpose(2, 0, 3, 1, 4)
        q, k, v = (qkv[0], qkv[1], qkv[2])
        attn = jax.nn.softmax(jnp.einsum('bhqd,bhkd->bhqk', q, k) * scale, axis=-1)
        out = jnp.einsum('bhqk,bhkd->bhqd', attn, v)
        out = out.transpose(0, 2, 1, 3).reshape(b, s, d)
        return out @ W_proj.T + b_proj
    h = _L0_tok_ref(x, L0_tok_W0, L0_tok_b0, L0_tok_W1, L0_tok_b1, L0_tok_W2, L0_tok_b2, L0_tok_Wf, L0_tok_bf, L0_tok_idx0, L0_tok_idx1, L0_tok_idx2)
    h = jnp.concatenate([jnp.broadcast_to(cls_tok, (h.shape[0], 1, h.shape[2])), h], axis=1)
    h = h + _L0_attn_ref(_layernorm(h, axis=-1), L0_attn_Wq, L0_attn_Wk, L0_attn_Wv, L0_attn_Wgk1, L0_attn_Wgk2, L0_attn_bgk2, L0_attn_Wg, L0_attn_o_norm_w, L0_attn_Wo)
    h = h + _L0_ffn_ref(_layernorm(h, axis=-1), L0_ffn_W_qkv, L0_ffn_b_qkv, L0_ffn_W_gate, L0_ffn_b_gate, L0_ffn_A, L0_ffn_B_lora, L0_ffn_W_proj, L0_ffn_b_proj)
    return h

_drawn_inputs = setup_inputs


def setup_inputs(seed=0):
    import zlib

    import numpy as np

    out = dict(_drawn_inputs(seed))
    spreads = {'L0_attn_bgk2': (0.0, 0.287),
     'L0_attn_o_norm_w': (1.0, 0.2),
     'L0_ffn_b_qkv': (0.0, 0.354),
     'L0_ffn_b_gate': (0.0, 0.8),
     'L0_ffn_b_proj': (0.0, 0.1)}
    factors = {'L0_tok_b0': 2.684,
     'L0_ffn_W_qkv': 4.731,
     'L0_ffn_W_gate': 8.0,
     'L0_ffn_A': 8.0,
     'L0_ffn_B_lora': 8.0}
    for name, (base, spread) in spreads.items():
        noise = np.random.default_rng([zlib.crc32(name.encode()), seed]).standard_normal(out[name].shape)
        drawn = base * np.exp(spread * noise) if base else spread * noise
        out[name] = jnp.asarray(drawn.astype(out[name].dtype))
    for name, factor in factors.items():
        out[name] = (out[name] * factor).astype(out[name].dtype)
    return out
```

```python
from contextlib import ExitStack

import numpy as np

import concourse.bass as bass
from concourse import mybir

F32 = mybir.dt.float32
F16 = mybir.dt.float16
I32 = mybir.dt.int32
U32 = mybir.dt.uint32
ALU = mybir.AluOpType
ACT = mybir.ActivationFunctionType
AX = mybir.AxisListType

B, IMG, CH = 4, 64, 3
D, H = 192, 12
HALF = D // 2
HK, HV = D // 2 // H, D // H
HD = D // H
E = 64
GP = 16
NTOK = IMG * IMG // GP
TS = 128
NC = NTOK // TS
T = NTOK + 1
NT1, NT2 = NTOK // 4, NTOK // 16
NEXP, RANK = 8, 16
NR = NEXP * RANK
CW = B * TS
BANK = 512
EPS = 1e-5
GATE_NORM = 16.0
Q_SCALE = float(HK) ** -0.5
ATT_SCALE = float(HD) ** -0.5
LORA_SCALE = 32.0 / RANK
HH = H // 2

PACKS = {
    "p128": [("ident", 128), ("cls", D), ("eps", 1), ("interp1", 2 * NC * TS), ("causal", TS),
             ("b_gate", NEXP), ("tie", NEXP), ("b_proj", D), ("b_v", D), ("B_qk", 2 * D), ("B_v", D), ("ones_h", H * H)],
    "p96": [("Wq", 2 * HALF), ("Wk", 2 * HALF), ("Wv", 2 * D), ("Wg", 2 * D), ("b_gk", 1), ("o_norm", 1),
            ("blockdiag", D), ("headcol", H), ("head_mean", HALF), ("restart", CW), ("Wo", 2 * D),
            ("W_ga", 2 * (NEXP + NR)), ("W_qk", 2 * 2 * D), ("W_v", 2 * D), ("b_qk", 4),
            ("cls_heads", 2 * H), ("W_proj", 2 * D)],
    "p65": [("b0", 128), ("b1", 128), ("b2", 128), ("Wf0", D), ("Wf1", D), ("Wf2", D), ("W0", 4 * 48),
            ("W1", 2 * HALF), ("W2", 8 * HALF), ("Wgk1", D), ("Wgk2", HALF), ("interp2", B * NC * TS),
            ("to_heads", D)],
}
ROWS = {"p128": 128, "p96": 96, "p65": 65}


def offsets(pack):
    at, n = {}, 0
    for name, cols in PACKS[pack]:
        at[name] = (n, cols)
        n += cols
    return at, n

PRE = {i: [("qk", m) for m in range(4)] + ([("vc",)] if i == 0 else []) + [("v",), ("cq",)]
       + [("max", c, hd) for hd in range(H) for c in range(NC)] + [("mT",), ("ck",)] for i in range(B)}
POST = [("rbc", 0), ("rbc", 1), ("proj",)]


def schedule():
    plan = [[[] for _ in range(H)] for _ in range(B)]
    for i in range(B):
        if i:
            plan[i][1] += [(i - 1, key) for key in POST]
        if i + 1 < B:
            pre = [(i + 1, key) for key in PRE[i + 1]]
            early = 4 + 2
            plan[i][1] += pre[0:early]
            pre = pre[early:]
            first = 5
            per = -(-len(pre) // (H - first))
            for hd in range(first, H):
                plan[i][hd] += pre[0:per]
                pre = pre[per:]
    return plan


SCHEDULE = schedule()
LAST = [(B - 1, key) for key in POST] + [(B - 1, ("pc",))]
WORK = [(0, key) for key in PRE[0]] + [use for image in SCHEDULE for uses in image for use in uses] + LAST


def work_index(i, key):
    return WORK.index((i, key))


def work_bank(i, key):
    return 6 + work_index(i, key) % 2


def build(nc, pix0, pix1, pix2, index, p128, p96, p65, out):
    n_cols = {p: offsets(p)[1] for p in PACKS}
    with ExitStack() as ctx:
        def sb(name, shape, dt=F32):
            return ctx.enter_context(nc.sbuf_tensor(name, shape, dt))

        packed = {p: sb(p + "_sb", [ROWS[p], n_cols[p]]) for p in PACKS}

        def w(pack, name, rows=None):
            a, n = offsets(pack)[0][name]
            return packed[pack][0:rows or ROWS[pack], a:a + n]

        ident = w("p128", "ident")
        ident96 = ident[0:HALF, 0:HALF]
        cls_rows = w("p128", "cls")
        interp1 = w("p128", "interp1").rearrange("p (a c t) -> p a c t", a=2, c=NC)
        causal = w("p128", "causal")
        eps = w("p128", "eps")
        b_gate = w("p128", "b_gate")
        tie = w("p128", "tie")
        b_proj = w("p128", "b_proj")
        B_qk = w("p128", "B_qk")
        B_v = w("p128", "B_v")
        ones_h = w("p128", "ones_h").rearrange("p (h m) -> p h m", h=H)
        Wq = w("p96", "Wq").rearrange("p (i n) -> p i n", i=2)
        Wk = w("p96", "Wk").rearrange("p (i n) -> p i n", i=2)
        Wv = w("p96", "Wv").rearrange("p (i n) -> p i n", i=2)
        Wg = w("p96", "Wg").rearrange("p (i n) -> p i n", i=2)
        b_gk = w("p96", "b_gk")
        o_norm = w("p96", "o_norm")
        blockdiag = w("p96", "blockdiag")
        headcol = w("p96", "headcol")
        head_mean = w("p96", "head_mean")
        restart = w("p96", "restart")
        Wo = w("p96", "Wo").rearrange("p (i n) -> p i n", i=2)
        W_ga = w("p96", "W_ga").rearrange("p (i n) -> p i n", i=2)
        W_qk = w("p96", "W_qk").rearrange("p (i n) -> p i n", i=2)
        W_v = w("p96", "W_v").rearrange("p (i n) -> p i n", i=2)
        b_qk = w("p96", "b_qk")
        b_v = w("p128", "b_v")
        cls_heads = w("p96", "cls_heads").rearrange("p (i n) -> p i n", i=2)
        W_proj = w("p96", "W_proj").rearrange("p (i n) -> p i n", i=2)
        b_rep = [w("p65", f"b{i}", 65 if i == 2 else E) for i in range(3)]
        Wf = [w("p65", f"Wf{i}", 65 if i == 2 else E) for i in range(3)]
        W0 = w("p65", "W0", E).rearrange("p (i n) -> p i n", i=2)
        W1 = w("p65", "W1", E).rearrange("p (i n) -> p i n", i=2)
        W2 = w("p65", "W2", E).rearrange("p (i n) -> p i n", i=8)
        Wgk1 = w("p65", "Wgk1", 16).rearrange("p (i n) -> p i n", i=2)
        Wgk2 = w("p65", "Wgk2", 16)
        interp2 = w("p65", "interp2", E).rearrange("p (b c t) -> p b c t", b=B, c=NC)
        to_heads = w("p65", "to_heads", H).rearrange("p (i n) -> p i n", i=2)

        idx = sb("idx", [128, 2 + 8 + NC * GP], I32)
        G2 = sb("G2", [128, 2, B * 48])
        G1 = sb("G1", [128, 8, B * 12])
        G0 = sb("G0", [128, NC, GP, B * CH])
        Gp = sb("Gp", [128, 6 * D])
        G0p = Gp[:, 0:2 * D].rearrange("p (c b j d) -> p c b j d", c=NC, b=B, j=GP)
        G1p = Gp[:, 2 * D:4 * D].rearrange("p (b k d) -> p b k d", b=B, k=8)
        G2p = Gp[:, 4 * D:6 * D].rearrange("p (b k d) -> p b k d", b=B, k=2)
        wT = Gp[:, 0:B * T].rearrange("p (b t) -> p b t", b=B)
        M = sb("M", [HALF, 12, D])
        xT2 = M[:, :, :].rearrange("p a n -> p (a n)")[:, 0:2 * B * T].rearrange("p (a b t) -> p a b t", a=2, b=B)
        bias_h = sb("bias_h", [128, D])
        T2t = sb("T2t", [HALF, 8, B, NT2])
        T1t = sb("T1t", [HALF, 2, B, NT1])
        Z1 = sb("Z1", [128, 2, D])
        Z2 = sb("Z2", [E, D])
        T0t = sb("T0t", [HALF, NC, 2, TS])
        Wgk = sb("Wgk", [HALF, 2, HALF])
        h = sb("h", [128, NC, B, D])
        h1 = sb("h1", [128, NC, B, D])
        h1_cls = sb("h1_cls", [B, D])
        stats = sb("stats", [128, 6, B, 6])
        moments = sb("moments", [128, 6, B, 2])
        ln_var = sb("ln_var", [128, 6, B])
        rstd = sb("rstd", [128, 6, B])
        xh_tiles = sb("xh_tiles", [128, 2 + NC * B, D])
        xh = [xh_tiles[:, 0:1, :], xh_tiles[:, 1:2, :]] + [xh_tiles[:, 2 + B * c:2 + B * (c + 1), :] for c in (0, 1, 0, 1)]
        xT_cls = sb("xT_cls", [HALF, 2, 128])
        xT = sb("xT", [HALF, 2, CW])
        q_cls = sb("q_cls", [HALF, 8])
        S0 = sb("S0", [HALF, D])
        shared = sb("shared", [128, 7 * CW + 4 * CW + 7 * (2 * CW + 8)])
        place = [0]

        def early(shape):
            n = int(np.prod(shape[1:]))
            t = shared[0:shape[0], place[0]:place[0] + n]
            place[0] += n
            return t

        late_place = [0]

        def late(shape, dt=F32):
            n = int(np.prod(shape[1:]))
            words = n if dt == F32 else n // 2
            t = shared[0:shape[0], late_place[0]:late_place[0] + words]
            late_place[0] += words
            return t if dt == F32 else t.bitcast(dt)

        zm = early([HALF, CW])
        za = early([HALF, CW])
        zl = early([HALF, CW])
        Gs = early([HALF, CW])
        Gc = early([HALF, CW])
        Eq = early([HALF, CW])
        Ek = early([HALF, CW])
        decay = sb("decay", [HALF, NC, 3, B])
        qt = early([HALF, NC * CW]).rearrange("p (c n) -> p c n", c=NC)
        kt = early([HALF, NC * CW]).rearrange("p (c n) -> p c n", c=NC)
        arena = sb("arena", [128, B * 2 * H * T // 2])
        qm = arena[0:HALF, 0:H * CW].rearrange("p (h c) -> p h c", h=H)
        Vp = arena[:, H * CW:H * CW + NC * B * H * 32].rearrange("p (c b h e) -> p c b h e", c=NC, b=B, h=H)
        A = arena[:, H * CW + NC * B * H * 32:H * CW + NC * B * H * 32 + 16 * TS].rearrange("p (n h t) -> p n h t", n=4, h=4)
        stack = arena[0:48, :].bitcast(F16).rearrange("p (b s h t) -> p b s h t", b=B, s=2, h=H)
        Sc = sb("Sc", [HALF, NC, B, D])
        sel = Sc[0:H].rearrange("p c b n -> p (c b n)")[:, 0:H * TS // 2].bitcast(F16).rearrange("p (h t) -> p h t", h=H)
        S1 = sb("S1", [HALF, B, D])
        ktok = sb("ktok", [128, B, HALF])
        NORMW = 2 * CW + 2 * 4
        def norm_buf():
            t = early([HALF, NORMW])
            return [t[:, 0:2 * CW].rearrange("p (i n) -> p i n", i=2)] * NC + [t[:, 2 * CW:NORMW].rearrange("p (i n) -> p i n", i=2)]

        g_log, g_abs, g_raw, g_w, o_sq, o_ln, yT = (norm_buf() for _ in range(7))
        GW = NEXP + NR
        logits = sb("logits", [128, 3, B, NEXP])
        pr = sb("pr", [128, 3, 6, B, NEXP])
        sm = sb("sm", [128, 3, 8, B])
        disp = sb("disp", [128, 3, B, NEXP])
        aw = late([128, NC, B, NR]).rearrange("p (c b n) -> p c b n", c=NC, b=B)
        aw_cls = sb("aw_cls", [B, NR])
        x2_cls = sb("x2_cls", [HALF, 2, B])
        w_cls = sb("w_cls", [NR, B])
        qk_hi = late([HALF, 2, 4, T], F16).rearrange("p (a m t) -> p a m t", a=2, m=4)
        qk_lo = late([HALF, 2, 4, T], F16).rearrange("p (a m t) -> p a m t", a=2, m=4)
        cls_qk = sb("cls_qk", [HALF, 2, 2, 2, H], F16)
        x_rep = sb("x_rep", [HALF, 2, H])
        w_rep = sb("w_rep", [NR, H])
        v2 = late([128, 2, 2, H, 32]).rearrange("p (a c h e) -> p a c h e", a=2, c=2, h=H)
        v_cls = late([HALF, D])
        mx = sb("mx", [128, 2, 2, H])
        mx_cls = sb("mx_cls", [H, 2])
        neg_m = T1t[0:H].rearrange("p a b n -> p (a b n)")[:, 0:T].bitcast(F16).rearrange("p (a t) -> p a t", a=2)
        pT = late([128, 4, 2, T]).rearrange("p (n c t) -> p n c t", n=4, c=2)
        p_cls = late([HALF, 2, T]).rearrange("p (a t) -> p a t", a=2)
        s_clsk = late([H, T])
        den_l = late([H, T])
        den_r = late([H, T])
        r_bc = late([HALF, 2, T]).rearrange("p (a t) -> p a t", a=2)
        oT = late([HALF, B, 2, T]).rearrange("p (b a t) -> p b a t", b=B, a=2)
        res = late([128, NC, B, D]).rearrange("p (c b n) -> p c b n", c=NC, b=B)
        res_cls = G2[0:B, 0, :]
        fin = h
        fin_cls = G2[0:B, 1, :]
        PS = ctx.enter_context(nc.psum_tensor("PS", [128, 8, BANK], F32))
        bounce = nc.dram_tensor("bounce", (B, 2, 4 * HALF, T), F16, kind="Internal").ap()

        NAMES = (
            "weights_a weights_b weights_c idx_loaded gathered_coarse gathered0 gathered1 dve_chain act_chain "
            "cls_cols pads_zero perm_done moments_done rstd_done xh_done cls_T xT_cls_evac bias_done bias_evac M_done "
            "M_evac Wgk_done Wgk_evac cls_proj cls_qk_evac S0_done o_cls g_read g_log g_logsig o_square "
            "ms_done o_log weight_log weight y_done wo_done h1_done coarse_T T2_evac T1_evac Z_done Z1_evac Z2_evac "
            "T0_done T0_evac h_mm h_evac xh_T xT_evac_a xT_evac_v z_done z_read z_log Gc_done decays "
            "q_done k_done qt_done kt_done qm_done v_done v_evac Sin_done sc_done A_done av_done kT_done kT_evac "
            "kv_done S1_done g_done xT2_evac ga_done logits_sub logits_exp disp_done aw_done aw_T wT_evac "
            "reps_done work_full work_free qk_hi_done bounced_out bounced stacked cls_qk_done sT_done p_done "
            "pv_done den_log den_rec p_cls_in p_cls_done neg_m_done v2_ready o_free oT_done res_done fin_done stored"
        ).split()
        s = {n: ctx.enter_context(nc.semaphore(n)) for n in NAMES}
        block = ctx.enter_context(nc.Block())

        SC_BANKS = (0, 3, 6, 7)
        NG = B * (H // 4)
        o_ps = PS[0:HALF, 1:3, :]
        NORM = {
            2: (PS[0:HALF, 2, 0:8].rearrange("p (i n) -> p i n", i=2), PS[0:HALF, 4, 0:8].rearrange("p (i n) -> p i n", i=2),
                PS[0:HALF, 3, 0:8].rearrange("p (i n) -> p i n", i=2)),
            0: (o_ps, PS[0:HALF, 4:6, :], PS[0:HALF, 6:8, :]),
            1: (o_ps, PS[0:HALF, 4:6, :], PS[0:HALF, 6:8, :]),
        }
        TURN = {2: 1, 0: 2, 1: 3}

        def padded(t):
            return bass.AP(t.tensor, t.offset, [list(t.ap[0]), [64, H // 2], [48, 2], [1, HV]])

        def heads(t):
            return t.rearrange("p (a e v) -> p a e v", a=H // 2, e=2)

        def bc(t, shape):
            return t.to_broadcast(shape)

        @block.sync
        def _(sp):
            n128, n96, n65 = (offsets(p)[0] for p in ("p128", "p96", "p65"))
            sp.dma_start(idx[:, :], index).then_inc(s["idx_loaded"], 16)
            a = n128["interp1"][0]
            sp.dma_start(packed["p128"][:, 0:a], p128[:, 0:a]).then_inc(s["weights_a"], 16)
            b = n65["interp2"][0]
            sp.dma_start(packed["p65"][:, 0:b], p65[:, 0:b]).then_inc(s["weights_a"], 16)
            c = n96["W_ga"][0]
            sp.dma_start(packed["p96"][:, 0:c], p96[:, 0:c]).then_inc(s["weights_b"], 16)
            sp.dma_start(packed["p128"][:, a:], p128[:, a:]).then_inc(s["weights_b"], 16)
            sp.dma_start(packed["p65"][:, b:], p65[:, b:]).then_inc(s["weights_c"], 16)
            sp.dma_start(packed["p96"][:, c:], p96[:, c:]).then_inc(s["weights_c"], 16)
            def store(i):
                sp.wait_ge(s["fin_done"], i + 1)
                sp.dma_start(out[i, 1:T, :].rearrange("(c t) n -> t c n", c=NC), fin[:, :, i, :]).then_inc(s["stored"], 16)

            for i in range(B):
                if i >= 2:
                    store(i - 2)
                for part, t in ((0, qk_hi), (1, qk_lo)):
                    if part == 0:
                        sp.wait_ge(s["qk_hi_done"], 4 * (i + 1))
                    else:
                        sp.wait_ge(s["bounced_out"], i + 1)
                    sp.dma_start(bounce[i, part].rearrange("(m p) c -> p m c", m=4), t[:, i % 2]).then_inc(s["bounced"], 16)
                sp.wait_ge(s["bounced"], 32 * (i + 1))
                for side, parts in ((0, (0, 0, 1)), (1, (0, 1, 0))):
                    for slot, part in enumerate(parts):
                        src = bounce[i, part, side * D:(side + 1) * D, :].rearrange("(h d) c -> d h c", d=HD)
                        sp.dma_start(stack[HD * slot:HD * (slot + 1), i, side], src).then_inc(s["stacked"], 16)
            store(B - 2)
            store(B - 1)
            sp.wait_ge(s["fin_done"], B + 1)
            sp.dma_start(out[:, 0, :], fin_cls).then_inc(s["stored"], 16)
            sp.wait_ge(s["stored"], 16 * (B + 1))

        @block.gpsimd
        def _(pool):
            pool.wait_ge(s["idx_loaded"], 16)

            def gather(dst, table, col, sem):
                pool.indirect_dma_start(dst, None, table, bass.IndirectOffsetOnAxis(ap=idx[:, col:col + 1].bitcast(U32), axis=0)
                                        ).then_inc(s[sem], 16)

            for k in range(2):
                gather(G2[:, k, :], pix2, k, "gathered_coarse")
            for k in range(8):
                gather(G1[:, k, :], pix1, 2 + k, "gathered_coarse")
            for c in range(NC):
                for j in range(GP):
                    gather(G0[:, c, j, :], pix0, 10 + c * GP + j, f"gathered{c}")
            pool.wait_ge(s["weights_b"], 32)
            pool.wait_ge(s["h1_done"], 1 + 2 * NC)
            pool.tensor_tensor(res_cls, h1_cls[:, :], b_proj[0:B, :], ALU.add).then_inc(s["res_done"], 1)
            for c in range(NC):
                for i in range(B):
                    pool.tensor_tensor(res[:, c, i, :], h1[:, c, i, :], b_proj, ALU.add).then_inc(s["res_done"], 1)

        @block.scalar
        def _(act):
            chain = [0]

            def link(ins):
                chain[0] += 1
                ins.then_inc(s["act_chain"], 1)
                act.wait_ge(s["act_chain"], chain[0])

            def layer_norm(k, rows, n):
                act.wait_ge(s["moments_done"], k + 1)
                link(act.activation(ln_var[0:rows, k, 0:n], moments[0:rows, k, 0:n, 1], ACT.Ln,
                                    bias=eps[0:rows], scale=1.0))
                act.activation(rstd[0:rows, k, 0:n], ln_var[0:rows, k, 0:n], ACT.Exp, scale=-0.5
                               ).then_inc(s["rstd_done"], 1)

            def gate_parts(j):
                _, g_psum, _ = NORM[j]
                if j == 1:
                    act.wait_ge(s["y_done"], 2)
                act.activation(g_raw[j], g_psum, ACT.Copy).then_inc(s["g_read"], 1)
                act.wait_ge(s["g_read"], TURN[j])
                link(act.activation(g_abs[j], g_raw[j], ACT.Abs))
                link(act.activation(g_abs[j], g_abs[j], ACT.Exp, scale=-1.0))
                act.activation(g_abs[j], g_abs[j], ACT.Ln, bias=1.0).then_inc(s["g_log"], 1)

            def norm(j):
                o_psum, _, ms_psum = NORM[j]
                t = TURN[j]
                act.activation(o_sq[j], o_psum, ACT.Square).then_inc(s["o_square"], 1)
                act.wait_ge(s["ms_done"], t)
                act.activation(o_ln[j], ms_psum, ACT.Ln, bias=eps[0:HALF], scale=1.0).then_inc(s["o_log"], 1)
                act.wait_ge(s["weight_log"], t)
                act.activation(o_sq[j], g_w[j], ACT.Exp).then_inc(s["weight"], 1)

            def route(k, rows, n, slot_g):
                act.wait_ge(s["logits_sub"], k + 1)
                act.activation(pr[0:rows, slot_g, 0, 0:n, :], pr[0:rows, slot_g, 0, 0:n, :], ACT.Exp).then_inc(s["logits_exp"], 1)

            act.preload_act_table_set("natural_log_exp_and_others")
            act.wait_ge(s["weights_a"], 32)
            layer_norm(0, 128, 1)
            for i in range(1, 6, 2):
                act.wait_ge(s["M_done"], i + 1)
                act.activation(M[:, 2 * i:2 * i + 2, :], PS[0:HALF, 2 + i, 0:2 * D].rearrange("p (a n) -> p a n", a=2),
                               ACT.Copy).then_inc(s["M_evac"], 1)
            act.wait_ge(s["weights_b"], 32)
            act.wait_ge(s["cls_proj"], 1)
            gate_parts(2)
            act.wait_ge(s["o_cls"], 1)
            norm(2)
            layer_norm(1, B, 1)
            route(0, B, 1, 2)

            act.wait_ge(s["coarse_T"], 1)
            act.activation(T2t[:, :, :, :], PS[0:HALF, 4, :].rearrange("p (b j n) -> p j b n", b=B, j=8), ACT.Copy).then_inc(s["T2_evac"], 1)
            act.wait_ge(s["Z_done"], 1)
            act.activation(Z1[:, :, :], PS[:, 6, 0:2 * D].rearrange("p (a n) -> p a n", a=2), ACT.Copy).then_inc(s["Z1_evac"], 1)

            def tokens(c):
                act.wait_ge(s["T0_done"], c + 1)
                act.activation(T0t[:, c], PS[0:HALF, 4, 0:2 * TS].rearrange("p (a n) -> p a n", a=2), ACT.Copy).then_inc(s["T0_evac"], 1)
                layer_norm(2 + c, 128, B)
                act.wait_ge(s["xh_T"], c + 1)
                if c:
                    act.wait_ge(s["v_done"], 2 * c)
                    act.wait_ge(s["k_done"], c)
                    act.wait_ge(s["g_done"], c)
                act.activation(xT[:, 0, :], PS[0:HALF, 7, :], ACT.Copy).then_inc(s["xT_evac_a"], 1)

            def decays(c):
                act.wait_ge(s["z_done"], c + 1)
                act.activation(zm[:, :], PS[0:HALF, 3, :], ACT.Identity, bias=b_gk, scale=1.0).then_inc(s["z_read"], 1)
                act.wait_ge(s["z_read"], c + 1)
                link(act.activation(za[:, :], zm[:, :], ACT.Abs))
                link(act.activation(za[:, :], za[:, :], ACT.Exp, scale=-1.0))
                act.activation(zl[:, :], za[:, :], ACT.Ln, bias=1.0).then_inc(s["z_log"], 1)
                act.wait_ge(s["Gc_done"], c + 1)
                if c:
                    act.wait_ge(s["qt_done"], c)
                    act.wait_ge(s["kt_done"], c)
                act.activation(Eq[:, :], Gc[:, :], ACT.Exp, scale=1.0 / GATE_NORM).then_inc(s["decays"], 1)
                act.activation(Ek[:, :], Gc[:, :], ACT.Exp, scale=-1.0 / GATE_NORM).then_inc(s["decays"], 1)
                by_image = Gs[:, :].rearrange("p (b t) -> p b t", b=B)
                about = Gc[:, :].rearrange("p (b t) -> p b t", b=B)
                act.activation(decay[:, c, 0, :], by_image[:, :, TS // 2 - 1], ACT.Exp, scale=1.0 / GATE_NORM)
                act.activation(decay[:, c, 1, :], about[:, :, TS - 1], ACT.Exp, scale=1.0 / GATE_NORM)
                act.activation(decay[:, c, 2, :], by_image[:, :, TS - 1], ACT.Exp, scale=1.0 / GATE_NORM).then_inc(s["decays"], 1)

            def values(c):
                for i in range(B):
                    act.wait_ge(s["v_done"], 2 * c + i // 2 + 1)
                    if c == 0 and i == 0:
                        act.wait_ge(s["pads_zero"], 1)
                    v = PS[:, 6 + i // 2, (i % 2) * D:(i % 2 + 1) * D]
                    act.activation(padded(Vp[:, c, i]), heads(v), ACT.Copy).then_inc(s["v_evac"], 1)

            def project(c):
                decays(c)
                act.wait_ge(s["g_done"], c + 1)
                gate_parts(c)
                values(c)

            tokens(0)
            project(0)
            act.wait_ge(s["kT_done"], 1)
            act.activation(ktok[:, :, :], PS[:, 0, 0:B * HALF].rearrange("p (b n) -> p b n", b=B), ACT.Copy).then_inc(s["kT_evac"], 1)
            tokens(1)
            act.wait_ge(s["av_done"], NG)
            norm(0)
            project(1)
            act.wait_ge(s["av_done"], 2 * NG)

            def chunk_in(c):
                if c == 0:
                    act.wait_ge(s["h_mm"], 2 * NC)
                    act.wait_ge(s["reps_done"], 1)
                    for half in range(2):
                        act.activation(xT2[:, half, :, 0], x2_cls[:, half, :], ACT.Copy)
                    act.activation(wT[:, :, 0], w_cls[:, :], ACT.Copy).then_inc(s["cls_cols"], 1)
                layer_norm(4 + c, 128, B)
                act.wait_ge(s["xh_T"], 2 + c + 1)
                act.activation(xT2[:, 0, :, 1 + c * TS:1 + (c + 1) * TS], PS[0:HALF, 4, :].rearrange("p (b n) -> p b n", b=B),
                               ACT.Copy).then_inc(s["xT_evac_a"], 1)
                route(1 + c, 128, B, c)
                act.wait_ge(s["aw_T"], 1 + c + 1)
                act.activation(wT[:, :, 1 + c * TS:1 + (c + 1) * TS], PS[:, 0, :].rearrange("p (b n) -> p b n", b=B),
                               ACT.Copy).then_inc(s["wT_evac"], 1)

            norm(1)
            for c in range(NC):
                chunk_in(c)

            def high_parts(i):
                for m in range(4):
                    act.wait_ge(s["work_full"], work_index(i, ("qk", m)) + 1)
                    if i >= 2 and m == 0:
                        act.wait_ge(s["bounced"], 32 * (i - 1))
                    act.activation(qk_hi[:, i % 2, m, :], PS[0:HALF, work_bank(i, ("qk", m)), 0:T], ACT.Identity,
                                   bias=b_qk[:, m:m + 1], scale=1.0).then_inc(s["qk_hi_done"], 1)

            def cls_probs(i):
                act.wait_ge(s["p_cls_in"], i + 1)
                act.wait_ge(s["pads_zero"], 2)
                if i >= 2:
                    act.wait_ge(s["pv_done"], H * (i - 1))
                act.activation(p_cls[0:H, i % 2, :], s_clsk[:, :], ACT.Exp, scale=ATT_SCALE).then_inc(s["p_cls_done"], 1)

            def probs(i, hd):
                n = i * H + hd
                act.wait_ge(s["sT_done"], n + 1)
                if n >= 4:
                    act.wait_ge(s["pv_done"], n - 3)
                act.activation(pT[:, n % 4], PS[:, 2 * (n % 2):2 * (n % 2) + 2, 0:T], ACT.Exp, scale=ATT_SCALE
                               ).then_inc(s["p_done"], 1)

            def denominators(i):
                act.wait_ge(s["pv_done"], H * (i + 1))
                if i >= 1:
                    act.wait_ge(s["den_rec"], i)
                link(act.activation(den_l[:, :], PS[96:96 + H, 4, 0:T], ACT.Ln))
                if i >= 1:
                    act.wait_ge(s["work_full"], work_index(i - 1, ("rbc", 1)) + 1)
                act.activation(den_r[:, :], den_l[:, :], ACT.Exp, scale=-1.0).then_inc(s["den_rec"], 1)

            high_parts(0)
            cls_probs(0)
            for i in range(B):
                for hd in range(H):
                    if hd == 2 and i + 1 < B:
                        high_parts(i + 1)
                    probs(i, hd)
                denominators(i)
                if i + 1 < B:
                    cls_probs(i + 1)

        @block.vector
        def _(dve):
            chain = [0]

            def link(ins):
                chain[0] += 1
                ins.then_inc(s["dve_chain"], 1)
                dve.wait_ge(s["dve_chain"], chain[0])

            def copy_then(out_, in_, sem):
                dve.tensor_copy(out_, in_).then_inc(s[sem], 1)

            def layer_norm(k, rows, tiles):
                for i, t in enumerate(tiles):
                    last = dve.bn_stats(stats[0:rows, k, i, :], t)
                link(last)
                for i in range(len(tiles)):
                    last = dve.bn_aggr(moments[0:rows, k, i, :], stats[0:rows, k, i, :])
                last.then_inc(s["moments_done"], 1)
                dve.wait_ge(s["moments_done"], k + 1)
                dve.wait_ge(s["rstd_done"], k + 1)
                for i, t in enumerate(tiles):
                    last = dve.tensor_scalar(xh[k][0:rows, i, :], t, moments[0:rows, k, i, 0:1], rstd[0:rows, k, i:i + 1],
                                             ALU.subtract, ALU.mult)
                last.then_inc(s["xh_done"], 1)

            def gate_logsig(j):
                dve.wait_ge(s["g_log"], TURN[j])
                if j == 1:
                    dve.wait_ge(s["weight_log"], 2)
                dve.scalar_tensor_tensor(g_log[j], g_raw[j], 0.0, g_abs[j], ALU.min, ALU.subtract).then_inc(s["g_logsig"], 1)

            def norm(j):
                o_psum, _, _ = NORM[j]
                t = TURN[j]
                dve.wait_ge(s["o_log"], t)
                dve.wait_ge(s["g_logsig"], t)
                dve.scalar_tensor_tensor(g_w[j], o_ln[j], -0.5, g_log[j], ALU.mult, ALU.add).then_inc(s["weight_log"], 1)
                dve.wait_ge(s["weight"], t)
                link(dve.scalar_tensor_tensor(g_w[j], g_raw[j], o_norm, o_sq[j], ALU.mult, ALU.mult))
                dve.tensor_tensor(yT[j], o_psum, g_w[j], ALU.mult).then_inc(s["y_done"], 1)

            dve.memset(Vp[:, :, :, :, :], 0.0).then_inc(s["pads_zero"], 1)

            dve.wait_ge(s["weights_a"], 32)
            layer_norm(0, 128, [cls_rows])
            dve.wait_ge(s["bias_done"], 1)
            copy_then(bias_h[:, :], PS[:, 1, 0:D], "bias_evac")
            dve.wait_ge(s["cls_T"], 1)
            copy_then(xT_cls[:, :, :], PS[0:HALF, 0, 0:256].rearrange("p (i n) -> p i n", i=2), "xT_cls_evac")
            for i in range(0, 6, 2):
                dve.wait_ge(s["M_done"], i + 1)
                dve.tensor_copy(M[:, 2 * i:2 * i + 2, :], PS[0:HALF, 2 + i, 0:2 * D].rearrange("p (a n) -> p a n", a=2)
                                ).then_inc(s["M_evac"], 1)
            dve.wait_ge(s["Wgk_done"], 1)
            copy_then(Wgk[:, :, :], PS[0:HALF, 0, 0:D].rearrange("p (i n) -> p i n", i=2), "Wgk_evac")
            dve.wait_ge(s["weights_b"], 32)
            dve.wait_ge(s["cls_proj"], 1)
            dve.tensor_scalar(q_cls[:, 0:4], PS[0:HALF, 1, 0:4], Q_SCALE, None, ALU.mult)
            link(dve.tensor_copy(q_cls[:, 4:8], PS[0:HALF, 1, 4:8]))
            dve.scalar_tensor_tensor(S0[:, :], PS[0:HALF, 1, 16:16 + D], q_cls[:, 4:5], blockdiag, ALU.mult, ALU.mult
                                     ).then_inc(s["S0_done"], 1)
            gate_logsig(2)
            norm(2)
            dve.wait_ge(s["wo_done"], 1)
            dve.tensor_tensor(h1_cls[:, :], PS[0:B, 0, 0:D], cls_rows[0:B, :], ALU.add).then_inc(s["h1_done"], 1)
            dve.wait_ge(s["h1_done"], 1)
            layer_norm(1, B, [h1_cls[:, :]])
            dve.wait_ge(s["cls_T"], 2)
            for half in range(2):
                last = dve.tensor_copy(x2_cls[:, half, :], PS[0:HALF, 2, half * B:(half + 1) * B])
            link(last)
            dve.tensor_copy(x_rep[:, :, :], x2_cls[:, :, 0:1].to_broadcast([HALF, 2, H])).then_inc(s["xT2_evac"], 1)
            route_events = [0]

            def route(rows, units, slot_g):
                k = route_events[0]
                route_events[0] += 1
                n = len(units)
                lg, P = logits[0:rows, slot_g, 0:n, :], [pr[0:rows, slot_g, a, 0:n, :] for a in range(6)]
                r = [sm[0:rows, slot_g, a, 0:n] for a in range(8)]

                def wide(x):
                    return x.unsqueeze(2).to_broadcast([rows, n, NEXP])

                dve.wait_ge(s["ga_done"], k + 1)
                for a, u in enumerate(units):
                    last = dve.tensor_tensor(logits[0:rows, slot_g, a, :], u[:, 0:NEXP], b_gate[0:rows], ALU.add)
                link(last)
                link(dve.tensor_reduce(r[0], lg, AX.X, ALU.max))
                dve.tensor_tensor(P[0], lg, wide(r[0]), ALU.subtract).then_inc(s["logits_sub"], 1)
                dve.wait_ge(s["logits_exp"], k + 1)
                link(dve.tensor_reduce(r[1], P[0], AX.X, ALU.add))
                link(dve.reciprocal(r[2], r[1]))
                link(dve.tensor_tensor(P[1], P[0], wide(r[2]), ALU.mult))
                chosen = []
                left = P[1]
                for turn in range(2):
                    link(dve.tensor_reduce(r[3 + 2 * turn], left, AX.X, ALU.max))
                    link(dve.tensor_tensor(P[2 + turn], left, wide(r[3 + 2 * turn]), ALU.is_ge))
                    link(dve.tensor_tensor(P[2 + turn], P[2 + turn], tie[0:rows].unsqueeze(1).to_broadcast([rows, n, NEXP]), ALU.mult))
                    link(dve.tensor_reduce(r[4 + 2 * turn], P[2 + turn], AX.X, ALU.max))
                    link(dve.tensor_tensor(P[2 + turn], P[2 + turn], wide(r[4 + 2 * turn]), ALU.is_equal))
                    chosen.append(P[2 + turn])
                    if turn == 0:
                        link(dve.scalar_tensor_tensor(P[4], P[2], -2.0, P[1], ALU.mult, ALU.add))
                        left = P[4]
                link(dve.tensor_tensor(P[5], chosen[0], chosen[1], ALU.add))
                link(dve.scalar_tensor_tensor(disp[0:rows, slot_g, 0:n, :], P[5], LORA_SCALE, P[1], ALU.mult, ALU.mult))
                for a, u in enumerate(units):
                    down = u[:, NEXP:NEXP + NR].rearrange("p (e r) -> p e r", e=NEXP)
                    weighted = aw_cls[:, :] if slot_g == 2 else aw[:, slot_g, a, :]
                    last = dve.tensor_tensor(weighted.rearrange("p (e r) -> p e r", e=NEXP), down,
                                             disp[0:rows, slot_g, a, :].unsqueeze(2).to_broadcast([rows, NEXP, RANK]), ALU.mult)
                last.then_inc(s["aw_done"], 1)

            def routed_psum(slot_g):
                if slot_g == 2:
                    return [PS[0:B, 3, 0:GW]]
                return [PS[:, 6 + i // 2, (i % 2) * GW:(i % 2 + 1) * GW] for i in range(B)]

            dve.wait_ge(s["weights_b"], 32)
            route(B, routed_psum(2), 2)
            dve.wait_ge(s["aw_T"], 1)
            link(dve.tensor_copy(w_cls[:, :], PS[:, 2, 0:B]))
            dve.tensor_copy(w_rep[:, :], w_cls[:, 0:1].to_broadcast([NR, H])).then_inc(s["reps_done"], 1)

            dve.wait_ge(s["gathered_coarse"], 16 * 10)
            dve.tensor_copy(G2p[:, :, :, :], G2[:, :, :].rearrange("p k (b d) -> p b k d", b=B))
            dve.tensor_copy(G1p[:, :, :, :], G1[:, :, :].rearrange("p k (b d) -> p b k d", b=B)).then_inc(s["perm_done"], 1)
            dve.wait_ge(s["coarse_T"], 1)
            copy_then(T1t[:, :, :, :], PS[0:HALF, 5, :].rearrange("p (b k n) -> p k b n", b=B, k=2), "T1_evac")
            dve.wait_ge(s["Z_done"], 1)
            copy_then(Z2[:, :], PS[0:E, 7, 0:D], "Z2_evac")

            def tokens(c):
                dve.wait_ge(s[f"gathered{c}"], 16 * GP)
                for i in range(B):
                    last = dve.tensor_copy(G0p[:, c, i, :, :], G0[:, c, :, CH * i:CH * (i + 1)])
                last.then_inc(s["perm_done"], 1)
                for a in range(2):
                    dve.wait_ge(s["h_mm"], 2 * c + a + 1)
                    last = dve.tensor_tensor(h[:, c, 2 * a:2 * a + 2, :], PS[:, 5 + a, 0:2 * D].rearrange("p (a n) -> p a n", a=2),
                                             bias_h[:, :].unsqueeze(1).to_broadcast([128, 2, D]), ALU.add)
                    last.then_inc(s["h_evac"], 1)
                dve.wait_ge(s["h_evac"], 2 * (c + 1))
                layer_norm(2 + c, 128, [h[:, c, i, :] for i in range(B)])
                dve.wait_ge(s["xh_T"], c + 1)
                if c:
                    dve.wait_ge(s["v_done"], 2 * c)
                    dve.wait_ge(s["k_done"], c)
                    dve.wait_ge(s["g_done"], c)
                copy_then(xT[:, 1, :], PS[0:HALF, 0, :], "xT_evac_v")

            def project(c):
                dve.wait_ge(s["z_log"], c + 1)
                link(dve.scalar_tensor_tensor(zm[:, :], zm[:, :], 0.0, zl[:, :], ALU.min, ALU.subtract))
                if c:
                    dve.wait_ge(s["decays"], 3 * c)
                link(dve.tensor_tensor_scan(Gs[:, :], restart, zm[:, :], 0.0, ALU.mult, ALU.add))
                by_image = Gs[:, :].rearrange("p (b t) -> p b t", b=B)
                middle = by_image[:, :, TS // 2 - 1:TS // 2].to_broadcast([HALF, B, TS])
                dve.tensor_tensor(Gc[:, :].rearrange("p (b t) -> p b t", b=B), by_image, middle, ALU.subtract
                                  ).then_inc(s["Gc_done"], 1)
                dve.wait_ge(s["decays"], 3 * c + 1)
                dve.wait_ge(s["q_done"], c + 1)
                dve.scalar_tensor_tensor(qt[:, c, :], PS[0:HALF, 1, :], Q_SCALE, Eq[:, :], ALU.mult, ALU.mult
                                         ).then_inc(s["qt_done"], 1)
                dve.wait_ge(s["decays"], 3 * c + 2)
                dve.wait_ge(s["k_done"], c + 1)
                dve.tensor_tensor(kt[:, c, :], PS[0:HALF, 2, :], Ek[:, :], ALU.mult).then_inc(s["kt_done"], 1)
                dve.wait_ge(s["qt_done"], c + 1)
                if c:
                    dve.wait_ge(s["sc_done"], NG * c)
                for hd in range(H):
                    dve.tensor_scalar(qm[:, hd, :], qt[:, c, :], headcol[:, hd:hd + 1], None, ALU.mult).then_inc(s["qm_done"], 1)
                dve.wait_ge(s["decays"], 3 * c + 3)
                for i in range(B):
                    state = S0[:, :] if c == 0 else S1[:, i, :]
                    last = dve.tensor_scalar(Sc[:, c, i, :], state, decay[:, c, 0, i:i + 1], None, ALU.mult)
                last.then_inc(s["Sin_done"], 1)

            def scores(c):
                for g in range(NG):
                    n = NG * c + g
                    dve.wait_ge(s["sc_done"], n + 1)
                    if n >= 4:
                        dve.wait_ge(s["av_done"], n - 3)
                    sc = PS[:, SC_BANKS[n % 4], :].rearrange("p (h t) -> p h t", h=4)
                    dve.tensor_tensor(A[:, n % 4], sc, causal.unsqueeze(1).to_broadcast([128, 4, TS]), ALU.mult
                                      ).then_inc(s["A_done"], 1)

            def h1_sum(c):
                for a, bank in ((0, 0), (1, 3)):
                    dve.wait_ge(s["wo_done"], 1 + 2 * c + a + 1)
                    dve.tensor_tensor(h1[:, c, 2 * a:2 * a + 2, :], PS[:, bank, 0:2 * D].rearrange("p (a n) -> p a n", a=2),
                                      h[:, c, 2 * a:2 * a + 2, :], ALU.add).then_inc(s["h1_done"], 1)

            tokens(0)
            project(0)
            gate_logsig(0)
            scores(0)
            for i in range(B):
                dve.wait_ge(s["kv_done"], i // 2 + 1)
                bank = (3, 0)[i // 2]
                link(dve.scalar_tensor_tensor(S1[:, i, :], PS[0:HALF, bank, (i % 2) * D:(i % 2 + 1) * D], decay[:, 0, 1, i:i + 1],
                                              blockdiag, ALU.mult, ALU.mult))
                dve.scalar_tensor_tensor(S1[:, i, :], S0[:, :], decay[:, 0, 2, i:i + 1], S1[:, i, :], ALU.mult, ALU.add
                                         ).then_inc(s["S1_done"], 1)
            dve.wait_ge(s["S1_done"], B)
            tokens(1)
            norm(0)
            project(1)
            gate_logsig(1)
            h1_sum(0)
            scores(1)
            norm(1)
            h1_sum(1)

            def chunk_in(c):
                dve.wait_ge(s["h1_done"], 1 + 2 * (c + 1))
                layer_norm(4 + c, 128, [h1[:, c, i, :] for i in range(B)])
                dve.wait_ge(s["xh_T"], 2 + c + 1)
                dve.tensor_copy(xT2[:, 1, :, 1 + c * TS:1 + (c + 1) * TS], PS[0:HALF, 5, :].rearrange("p (b n) -> p b n", b=B)
                                ).then_inc(s["xT2_evac"], 1)
                route(128, routed_psum(c), c)

            for c in range(NC):
                chunk_in(c)

            dve.wait_ge(s["wo_done"], 5)
            dve.memset(v2, 0.0)
            dve.memset(p_cls, 0.0)
            dve.memset(v_cls, 0.0)
            dve.tensor_copy(sel, ident[0:H, 0:H].unsqueeze(2).to_broadcast([H, H, TS])).then_inc(s["pads_zero"], 1)
            dve.wait_ge(s["pads_zero"], 2)

            done_T = [0]
            for n, (i, key) in enumerate(WORK):
                dve.wait_ge(s["work_full"], n + 1)
                ps = PS[:, 6 + n % 2, :]
                kind = key[0]
                if kind == "qk":
                    m = key[1]
                    dve.wait_ge(s["qk_hi_done"], 4 * i + m + 1)
                    if i >= 2 and m == 0:
                        dve.wait_ge(s["bounced"], 32 * (i - 1))
                    last = dve.scalar_tensor_tensor(qk_lo[:, i % 2, m, :], ps[0:HALF, 0:T], b_qk[:, m:m + 1],
                                                    qk_hi[:, i % 2, m, :], ALU.add, ALU.subtract)
                    last.then_inc(s["work_free"], 1)
                    if m == 3:
                        dve.wait_ge(s["work_free"], n + 1)
                        dve.engine_nop().then_inc(s["bounced_out"], 1) if False else dve.nop().then_inc(s["bounced_out"], 1)
                        if i == 0:
                            for side in range(2):
                                for part, t in ((0, qk_hi), (1, qk_lo)):
                                    for half in range(2):
                                        last = dve.tensor_tensor(cls_qk[:, side, part, half, :], cls_heads[:, half, :],
                                                                 t[:, 0, 2 * side + half, 0:1].to_broadcast([HALF, H]), ALU.mult)
                            last.then_inc(s["cls_qk_done"], 1)
                elif kind == "vc":
                    link(dve.tensor_tensor(v_cls[0:H, :], ps[0:H, 0:D], b_v[0:H, :], ALU.add))
                    dve.tensor_tensor(v_cls[0:H, :], v_cls[0:H, :], to_heads.rearrange("p i n -> p (i n)"), ALU.mult
                                      ).then_inc(s["work_free"], 1)
                elif kind == "v":
                    if i >= 2:
                        dve.wait_ge(s["pv_done"], H * (i - 1))
                    for c in range(NC):
                        last = dve.tensor_tensor(padded(v2[:, i % 2, c]), heads(ps[:, c * D:(c + 1) * D]), heads(b_v), ALU.add)
                    last.then_inc(s["work_free"], 1)
                elif kind == "cq":
                    dve.tensor_reduce(mx_cls[:, i % 2:i % 2 + 1], ps[0:H, 0:T], AX.X, ALU.max).then_inc(s["work_free"], 1)
                elif kind == "max":
                    c, hd = key[1:]
                    dve.tensor_reduce(mx[:, i % 2, c, hd:hd + 1], ps[:, 0:T], AX.X, ALU.max).then_inc(s["work_free"], 1)
                elif kind == "mT":
                    if i >= 2:
                        dve.wait_ge(s["sT_done"], H * (i - 1))
                    dve.tensor_scalar(neg_m[:, i % 2, 0:1], mx_cls[:, i % 2:i % 2 + 1], -1.0, None, ALU.mult)
                    dve.tensor_scalar(neg_m[:, i % 2, 1:T], ps[0:H, 0:NTOK], -1.0, None, ALU.mult).then_inc(s["work_free"], 1)
                elif kind == "ck":
                    if i >= 1:
                        dve.wait_ge(s["p_cls_done"], i)
                    dve.wait_ge(s["work_free"], n)
                    dve.tensor_tensor(s_clsk[:, :], ps[0:H, 0:T], neg_m[:, i % 2, :], ALU.add).then_inc(s["work_free"], 1)
                    dve.wait_ge(s["work_free"], n + 1)
                    dve.nop().then_inc(s["p_cls_in"], 1)
                elif kind == "rbc":
                    half = key[1]
                    link(dve.tensor_copy(r_bc[:, half, :], ps[0:HALF, 0:T]))
                    dve.tensor_tensor(oT[:, i, half, :], PS[0:HALF, 4 + half, 0:T], r_bc[:, half, :], ALU.mult
                                      ).then_inc(s["work_free"], 1)
                elif kind == "proj":
                    dve.wait_ge(s["res_done"], 1 + 2 * B)
                    dve.tensor_tensor(fin[:, :, i, :], ps[:, 0:2 * D].rearrange("p (c n) -> p c n", c=NC), res[:, :, i, :], ALU.add
                                      ).then_inc(s["work_free"], 1)
                    dve.wait_ge(s["work_free"], n + 1)
                    dve.nop().then_inc(s["fin_done"], 1)
                elif kind == "pc":
                    dve.tensor_tensor(fin_cls, ps[0:B, 0:D], res_cls, ALU.add).then_inc(s["fin_done"], 1)

        @block.tensor
        def _(pe):
            def halves(out_, lhs, rhs):
                for half in range(2):
                    last = pe.matmul(out_, lhs[half], rhs[half], start=(half == 0), stop=(half == 1), skip_group_check=True)
                return last

            def turn(bank_ap, x, half, sem=None):
                rows = x.partition_size() if hasattr(x, "partition_size") else None
                return pe.transpose(bank_ap, x, ident)

            pe.wait_ge(s["weights_a"], 32)
            for i in range(3):
                last = pe.matmul(PS[:, 1, 0:D], b_rep[i], Wf[i], start=(i == 0), stop=(i == 2))
            last.then_inc(s["bias_done"], 1)
            factors = [(W0[:, i, :], 0) for i in range(2)] + [(W1[:, i, :], 1) for i in range(2)] + [(W2[:, i, :], 2) for i in range(8)]
            for i, (f, level) in enumerate(factors):
                last = pe.matmul(PS[0:HALF, 2 + i // 2, (i % 2) * D:(i % 2 + 1) * D], f, Wf[level][0:E], start=True, stop=True)
                if i % 2:
                    last.then_inc(s["M_done"], 1)
            pe.wait_ge(s["xh_done"], 1)
            for half in range(2):
                last = pe.transpose(PS[0:HALF, 0, half * 128:(half + 1) * 128], xh[0][:, 0, half * HALF:(half + 1) * HALF], ident)
            last.then_inc(s["cls_T"], 1)
            pe.wait_ge(s["xT_cls_evac"], 1)
            for half in range(2):
                last = pe.matmul(PS[0:HALF, 0, half * HALF:(half + 1) * HALF], Wgk1[:, half, :], Wgk2, start=True, stop=True)
            last.then_inc(s["Wgk_done"], 1)
            pe.wait_ge(s["weights_b"], 32)
            pe.wait_ge(s["bias_evac"], 1)
            pe.wait_ge(s["M_evac"], 6)
            x4 = [xT_cls[:, i, 0:B] for i in range(2)]
            halves(PS[0:HALF, 1, 0:4], [Wq[:, i, :] for i in range(2)], x4)
            halves(PS[0:HALF, 1, 4:8], [Wk[:, i, :] for i in range(2)], x4)
            for m in range(2):
                halves(PS[0:HALF, 4, 4 * m:4 * m + 4], [Wg[:, i, m * HALF:(m + 1) * HALF] for i in range(2)], x4)
            halves(PS[0:HALF, 1, 16:16 + D], [xT_cls[:, i, 0:HALF] for i in range(2)], [Wv[:, i, :] for i in range(2)]
                   ).then_inc(s["cls_proj"], 1)
            pe.wait_ge(s["S0_done"], 1)
            for m in range(2):
                last = pe.matmul(PS[0:HALF, 2, 4 * m:4 * m + 4], S0[:, m * HALF:(m + 1) * HALF], q_cls[:, 0:4], start=True, stop=True)
            last.then_inc(s["o_cls"], 1)

            def mean_squares(j):
                _, _, ms_psum = NORM[j]
                pe.wait_ge(s["o_square"], TURN[j])
                for m in range(2):
                    last = pe.matmul(ms_psum[:, m, :], head_mean, o_sq[j][:, m, :], start=True, stop=True)
                last.then_inc(s["ms_done"], 1)

            mean_squares(2)
            pe.wait_ge(s["y_done"], 1)
            pe.wait_ge(s["Wgk_evac"], 1)
            halves(PS[0:B, 0, 0:D], [yT[2][:, i, :] for i in range(2)], [Wo[:, i, :] for i in range(2)]).then_inc(s["wo_done"], 1)
            pe.wait_ge(s["xh_done"], 2)
            for half in range(2):
                last = pe.transpose(PS[0:HALF, 2, half * B:(half + 1) * B], xh[1][0:B, 0, half * HALF:(half + 1) * HALF],
                                    ident[0:B, 0:B])
            last.then_inc(s["cls_T"], 1)
            pe.wait_ge(s["xT2_evac"], 1)
            pe.wait_ge(s["weights_c"], 32)
            pe.wait_ge(s["o_log"], 1)
            halves(PS[0:B, 3, 0:GW], [x2_cls[:, i, :] for i in range(2)], [W_ga[:, i, :] for i in range(2)]).then_inc(s["ga_done"], 1)
            pe.wait_ge(s["aw_done"], 1)
            pe.transpose(PS[:, 2, 0:B], aw_cls[:, :], ident[0:B, 0:B]).then_inc(s["aw_T"], 1)

            pe.wait_ge(s["perm_done"], 1)
            for i in range(B):
                pe.transpose(PS[0:HALF, 4, i * 128:(i + 1) * 128], G2p[:, i, :, :], ident)
            for i in range(B):
                last = pe.transpose(PS[0:HALF, 5, i * 128:(i + 1) * 128], G1p[:, i, :, :], ident)
            last.then_inc(s["coarse_T"], 1)
            pe.wait_ge(s["T1_evac"], 1)
            for a in range(2):
                for half in range(2):
                    pe.matmul(PS[:, 6, a * D:(a + 1) * D], T1t[:, half, 2 * a:2 * a + 2, :], M[:, 2 + half, :],
                              start=(half == 0), stop=(half == 1))
            pe.wait_ge(s["T2_evac"], 1)
            for j in range(8):
                last = pe.matmul(PS[0:E, 7, 0:D], T2t[:, j, :, :], M[:, 4 + j, :], start=(j == 0), stop=(j == 7))
            last.then_inc(s["Z_done"], 1)

            def tokens(c):
                pe.wait_ge(s["perm_done"], c + 2)
                if c == 0:
                    pe.wait_ge(s["T2_evac"], 1)
                else:
                    pe.wait_ge(s["g_read"], 2)
                for a in range(2):
                    last = pe.transpose(PS[0:HALF, 4, a * TS:(a + 1) * TS], G0p[:, c, 2 * a:2 * a + 2, :, :], ident)
                last.then_inc(s["T0_done"], 1)
                pe.wait_ge(s["T0_evac"], c + 1)
                if c == 0:
                    pe.wait_ge(s["Z1_evac"], 1)
                    pe.wait_ge(s["Z2_evac"], 1)
                else:
                    pe.wait_ge(s["A_done"], NG)
                for i in range(B):
                    out_ = PS[:, 5 + i // 2, (i % 2) * D:(i % 2 + 1) * D]
                    pe.matmul(out_, T0t[:, c, i // 2, :], M[:, i % 2, :], start=True, stop=False, skip_group_check=True)
                    pe.matmul(out_, interp1[:, i % 2, c, :], Z1[:, i // 2, :], start=False, stop=False, skip_group_check=True)
                    last = pe.matmul(out_, interp2[:, i, c, :], Z2[:, :], start=False, stop=True, skip_group_check=True)
                    if i % 2:
                        last.then_inc(s["h_mm"], 1)
                pe.wait_ge(s["xh_done"], 2 + c + 1)
                if c:
                    pe.wait_ge(s["S1_done"], B)
                for half in range(2):
                    for i in range(B):
                        last = pe.transpose(PS[0:HALF, (7, 0)[half], i * TS:(i + 1) * TS],
                                            xh[2 + c][:, i, half * HALF:(half + 1) * HALF], ident)
                last.then_inc(s["xh_T"], 1)

            def project(c):
                pe.wait_ge(s["xT_evac_a"], c + 1)
                pe.wait_ge(s["xT_evac_v"], c + 1)
                x = [xT[:, i, :] for i in range(2)]
                halves(PS[0:HALF, 3, :], [Wgk[:, i, :] for i in range(2)], x).then_inc(s["z_done"], 1)
                if c == 0:
                    queries_keys(c)
                pe.wait_ge(s["h_evac"], 2 * (c + 1))
                for m in range(2):
                    last = halves(PS[0:HALF, 4 + m, :], [Wg[:, i, m * HALF:(m + 1) * HALF] for i in range(2)], x)
                last.then_inc(s["g_done"], 1)
                if c:
                    pe.wait_ge(s["o_log"], 2)
                for i in range(B):
                    last = halves(PS[:, 6 + i // 2, (i % 2) * D:(i % 2 + 1) * D],
                                  [xT[:, a, i * TS:(i + 1) * TS] for a in range(2)], [Wv[:, a, :] for a in range(2)])
                    if i % 2:
                        last.then_inc(s["v_done"], 1)
                if c:
                    queries_keys(c)

            def queries_keys(c):
                x = [xT[:, i, :] for i in range(2)]
                if c:
                    pe.wait_ge(s["y_done"], 2)
                halves(PS[0:HALF, 1, :], [Wq[:, i, :] for i in range(2)], x).then_inc(s["q_done"], 1)
                halves(PS[0:HALF, 2, :], [Wk[:, i, :] for i in range(2)], x).then_inc(s["k_done"], 1)

            def linear_attention(c):
                pe.wait_ge(s["qt_done"], c + 1)
                pe.wait_ge(s["kt_done"], c + 1)
                pe.wait_ge(s["Sin_done"], c + 1)
                first = [True, True]
                for i in range(B):
                    for m in range(2):
                        pe.matmul(PS[0:HALF, 1 + m, i * TS:(i + 1) * TS], Sc[:, c, i, m * HALF:(m + 1) * HALF],
                                  qt[:, c, i * TS:(i + 1) * TS], start=first[m], stop=False, skip_group_check=True)
                        first[m] = False
                pe.wait_ge(s["z_read"], c + 1)
                pe.wait_ge(s["v_evac"], B * (c + 1))
                if c:
                    pe.wait_ge(s["h1_done"], 3)

                def scores(n):
                    g = n - NG * c
                    i, hg = g // 3, g % 3
                    pe.wait_ge(s["qm_done"], H * c + 4 * hg + 4)
                    if g >= 4:
                        pe.wait_ge(s["A_done"], n - 3)
                    pe.matmul(PS[:, SC_BANKS[n % 4], :], kt[:, c, i * TS:(i + 1) * TS],
                              qm[:, 4 * hg:4 * hg + 4, i * TS:(i + 1) * TS], start=True, stop=True).then_inc(s["sc_done"], 1)

                def values(n):
                    g = n - NG * c
                    i, hg = g // 3, g % 3
                    pe.wait_ge(s["A_done"], n + 1)
                    for a in (0, 2, 1, 3):
                        hd = 4 * hg + a
                        pair = hd // 2
                        row = 32 * (pair % 3)
                        last = pe.matmul(PS[row:row + 32, 1 + pair // 3, i * TS:(i + 1) * TS], Vp[:, c, i, hd, :], A[:, n % 4, a, :],
                                         start=False, stop=False, skip_group_check=True)
                    last.then_inc(s["av_done"], 1)

                for g in range(NG + 2):
                    if g < NG:
                        scores(NG * c + g)
                    if g >= 2:
                        values(NG * c + g - 2)

            def out_projection(c):
                pe.wait_ge(s["y_done"], 1 + c + 1)
                for i in range(B):
                    last = halves(PS[:, (0, 3)[i // 2], (i % 2) * D:(i % 2 + 1) * D],
                                  [yT[c][:, a, i * TS:(i + 1) * TS] for a in range(2)], [Wo[:, a, :] for a in range(2)])
                    if i % 2:
                        last.then_inc(s["wo_done"], 1)

            tokens(0)
            project(0)
            linear_attention(0)
            pe.wait_ge(s["A_done"], NG)
            for i in range(B):
                last = pe.transpose(PS[:, 0, i * HALF:(i + 1) * HALF], kt[:, 0, i * TS:(i + 1) * TS], ident96)
            last.then_inc(s["kT_done"], 1)
            pe.wait_ge(s["kT_evac"], 1)
            for i in range(B):
                last = pe.matmul(PS[0:HALF, (3, 0)[i // 2], (i % 2) * D:(i % 2 + 1) * D], ktok[:, i, :], padded(Vp[:, 0, i]),
                                 start=True, stop=True)
                if i % 2:
                    last.then_inc(s["kv_done"], 1)
            tokens(1)
            pe.wait_ge(s["h_evac"], 4)
            pe.wait_ge(s["xT_evac_a"], 2)
            mean_squares(0)
            project(1)
            pe.wait_ge(s["xT_evac_v"], 2)
            pe.wait_ge(s["z_read"], 2)
            out_projection(0)
            linear_attention(1)
            pe.wait_ge(s["A_done"], 2 * NG)
            mean_squares(1)
            out_projection(1)

            def chunk_in(c):
                pe.wait_ge(s["xh_done"], 4 + c + 1)
                if c == 0:
                    pe.wait_ge(s["g_read"], 3)
                else:
                    pe.wait_ge(s["xT_evac_a"], 3)
                    pe.wait_ge(s["xT2_evac"], 2)
                for half in range(2):
                    for i in range(B):
                        last = pe.transpose(PS[0:HALF, 4 + half, i * TS:(i + 1) * TS],
                                            xh[4 + c][:, i, half * HALF:(half + 1) * HALF], ident)
                last.then_inc(s["xh_T"], 1)
                pe.wait_ge(s["xT_evac_a"], 2 + c + 1)
                pe.wait_ge(s["xT2_evac"], 1 + c + 1)
                if c == 0:
                    pe.wait_ge(s["o_log"], 3)
                else:
                    pe.wait_ge(s["aw_done"], 2)
                for i in range(B):
                    last = halves(PS[:, 6 + i // 2, (i % 2) * GW:(i % 2 + 1) * GW],
                                  [xT2[:, a, i, 1 + c * TS:1 + (c + 1) * TS] for a in range(2)], [W_ga[:, a, :] for a in range(2)])
                last.then_inc(s["ga_done"], 1)
                pe.wait_ge(s["aw_done"], 1 + c + 1)
                if c == 0:
                    pe.wait_ge(s["h1_done"], 5)
                else:
                    pe.wait_ge(s["wT_evac"], 1)
                for i in range(B):
                    last = pe.transpose(PS[:, 0, i * TS:(i + 1) * TS], aw[:, c, i, :], ident)
                last.then_inc(s["aw_T"], 1)

            for c in range(NC):
                chunk_in(c)
            pe.wait_ge(s["wT_evac"], 2)
            pe.wait_ge(s["xT2_evac"], 3)
            pe.wait_ge(s["xT_evac_a"], 4)
            pe.wait_ge(s["reps_done"], 1)
            pe.wait_ge(s["cls_cols"], 1)
            pe.wait_ge(s["pads_zero"], 2)

            at = [0]

            def work(i, key):
                n = at[0]
                at[0] += 1
                assert WORK[n] == (i, key)
                if n >= 2:
                    pe.wait_ge(s["work_free"], n - 1)
                ps = PS[:, 6 + n % 2, :]
                kind = key[0]
                if kind == "qk":
                    m = key[1]
                    for half in range(2):
                        pe.matmul(ps[0:HALF, 0:T], W_qk[:, half, m * HALF:(m + 1) * HALF], xT2[:, half, i, :],
                                  start=(half == 0), stop=False)
                    last = pe.matmul(ps[0:HALF, 0:T], B_qk[:, m * HALF:(m + 1) * HALF], wT[:, i, :], start=False, stop=True)
                elif kind == "vc":
                    for half in range(2):
                        pe.matmul(ps[0:H, 0:D], x_rep[:, half, :], W_v[:, half, :], start=(half == 0), stop=False)
                    last = pe.matmul(ps[0:H, 0:D], w_rep[:, :], B_v, start=False, stop=True)
                elif kind == "v":
                    for c in range(NC):
                        cols = slice(1 + c * TS, 1 + (c + 1) * TS)
                        for half in range(2):
                            pe.matmul(ps[:, c * D:(c + 1) * D], xT2[:, half, i, cols], W_v[:, half, :], start=(half == 0), stop=False)
                        last = pe.matmul(ps[:, c * D:(c + 1) * D], wT[:, i, cols], B_v, start=False, stop=True)
                elif kind in ("cq", "ck"):
                    if kind == "cq" and i == 0:
                        pe.wait_ge(s["cls_qk_done"], 1)
                    if kind == "cq":
                        pe.wait_ge(s["bounced_out"], i + 1)
                    side = 0 if kind == "cq" else 1
                    steps = [(a, b, half) for a, b in ((0, 0), (0, 1), (1, 0)) for half in range(2)]
                    for n_, (a, b, half) in enumerate(steps):
                        t = (qk_hi, qk_lo)[b]
                        last = pe.matmul(ps[0:H, 0:T], cls_qk[:, side, a, half, :], t[:, i % 2, 2 * (1 - side) + half, :],
                                         start=(n_ == 0), stop=(n_ == len(steps) - 1))
                elif kind == "max":
                    c, hd = key[1:]
                    if c == 0 and hd == 0:
                        pe.wait_ge(s["stacked"], 96 * (i + 1))
                    last = pe.matmul(ps[:, 0:T], stack[0:48, i, 0, hd, 1 + c * TS:1 + (c + 1) * TS], stack[0:48, i, 1, hd, :],
                                     start=True, stop=True)
                elif kind == "mT":
                    pe.wait_ge(s["work_free"], n)
                    for c in range(NC):
                        last = pe.transpose(ps[0:H, c * TS:(c + 1) * TS], mx[:, i % 2, c, :], ident)
                elif kind == "rbc":
                    pe.wait_ge(s["den_rec"], i + 1)
                    last = pe.matmul(ps[0:HALF, 0:T], to_heads[:, key[1], :], den_r[:, :], start=True, stop=True)
                elif kind == "proj":
                    pe.wait_ge(s["work_free"], n)
                    for c in range(NC):
                        last = halves(ps[:, c * D:(c + 1) * D], [oT[:, i, a, 1 + c * TS:1 + (c + 1) * TS] for a in range(2)],
                                      [W_proj[:, a, :] for a in range(2)])
                elif kind == "pc":
                    last = halves(ps[0:B, 0:D], [oT[:, :, a, 0] for a in range(2)], [W_proj[:, a, :] for a in range(2)])
                last.then_inc(s["work_full"], 1)

            def key_scores(i, hd):
                n = i * H + hd
                if hd == 0:
                    pe.wait_ge(s["work_free"], work_index(i, ("mT",)) + 1)
                if n >= 2:
                    pe.wait_ge(s["p_done"], n - 1)
                for c in range(NC):
                    out_ = PS[:, 2 * (n % 2) + c, 0:T]
                    pe.matmul(out_, stack[0:48, i, 1, hd, 1 + c * TS:1 + (c + 1) * TS], stack[0:48, i, 0, hd, :], start=True, stop=False)
                    last = pe.matmul(out_, sel[:, hd, :], neg_m[:, i % 2, :], start=False, stop=True)
                last.then_inc(s["sT_done"], 1)

            def weighted_values(i, hd):
                n = i * H + hd
                if hd == 0:
                    if i:
                        pe.wait_ge(s["work_free"], work_index(i - 1, ("rbc", 1)) + 1)
                        pe.wait_ge(s["den_rec"], i)
                    pe.wait_ge(s["p_cls_done"], i + 1)
                    for m in range(2):
                        pe.matmul(PS[0:HALF, 4 + m, 0:T], v_cls[:, m * HALF:(m + 1) * HALF], p_cls[:, i % 2, :],
                                  start=True, stop=False, skip_group_check=True)
                    pe.matmul(PS[96:96 + H, 4, 0:T], ident[0:HALF, 0:H], p_cls[:, i % 2, :], start=True, stop=False,
                              skip_group_check=True)
                pe.wait_ge(s["p_done"], n + 1)
                pair = hd // 2
                row = 32 * (pair % 3)
                for c in range(NC):
                    pe.matmul(PS[row:row + 32, 4 + pair // 3, 0:T], v2[:, i % 2, c, hd, :], pT[:, n % 4, c, :],
                              start=False, stop=False, skip_group_check=True)
                    last = pe.matmul(PS[96:96 + H, 4, 0:T], ones_h[:, hd, :], pT[:, n % 4, c, :], start=False, stop=False,
                                     skip_group_check=True)
                last.then_inc(s["pv_done"], 1)

            for key in PRE[0]:
                work(0, key)
            for i in range(B):
                for hd in range(H):
                    key_scores(i, hd)
                    for j, key in SCHEDULE[i][hd]:
                        work(j, key)
                    if hd >= 2:
                        weighted_values(i, hd - 2)
                weighted_values(i, H - 2)
                weighted_values(i, H - 1)
            for j, key in LAST:
                work(j, key)


def interpolation(length, n_out):
    pos = (np.arange(n_out, dtype=np.float32) + np.float32(0.5)) * np.float32(length / n_out) - np.float32(0.5)
    pos = np.clip(pos, np.float32(0), np.float32(length - 1))
    lo = np.floor(pos).astype(np.int32)
    up = np.minimum(lo + 1, length - 1)
    frac = (pos - lo).astype(np.float32)
    m = np.zeros((length, n_out), np.float32)
    np.add.at(m, (lo, np.arange(n_out)), np.float32(1) - frac)
    np.add.at(m, (up, np.arange(n_out)), frac)
    return m

def kernel(**inputs):
    import concourse.bacc as bacc
    from concourse.bass_utils import run_bass_kernel_spmd

    a = {k.replace("L0_", ""): np.asarray(v) for k, v in inputs.items()}
    x = a["x"]
    f32 = np.float32

    def patches(p):
        n = IMG // p
        return np.ascontiguousarray(x.reshape(B, CH, n, p, n, p).transpose(2, 4, 0, 3, 5, 1).reshape(n * n, B * p * p * CH))

    index = np.concatenate([
        a["tok_idx2"].reshape(NT2, 2, 8).transpose(2, 0, 1).reshape(128, 2),
        a["tok_idx1"].reshape(NT1, 2, 8).transpose(1, 0, 2).reshape(128, 8),
        a["tok_idx0"].reshape(NC, TS, GP).transpose(1, 0, 2).reshape(128, NC * GP)], axis=1)

    def split(m):
        return m.reshape(2, HALF, -1).transpose(1, 0, 2).reshape(HALF, -1)

    def rows(v, n):
        return np.broadcast_to(v.reshape(1, -1), (n, v.size))

    i1, i2 = interpolation(NT1, NTOK), interpolation(NT2, NTOK)
    interp1 = np.zeros((2, NT1, 2, NC, TS), f32)
    for p in range(2):
        interp1[p, :, p] = i1.reshape(NT1, NC, TS)
    interp2 = np.zeros((B, NT2, B, NC, TS), f32)
    for p in range(B):
        interp2[p, :, p] = i2.reshape(NT2, NC, TS)
    W0 = np.zeros((E, 2, 2, 48), f32)
    for p in range(2):
        W0[:, p, p] = a["tok_W0"]
    WfT = a["tok_Wf"].T
    heads96 = np.arange(HALF) // HD
    ones_h = np.zeros((128, H, H), f32)
    ones_h[:, np.arange(H), np.arange(H)] = 1
    cls_heads = np.zeros((HALF, 2, H), f32)
    to_heads = np.zeros((H, 2, HALF), f32)
    for half in range(2):
        cls_heads[np.arange(HALF), half, half * HH + heads96] = 1
        to_heads[half * HH + heads96, half, np.arange(HALF)] = 1
    restart = np.ones((HALF, B, TS), f32)
    restart[:, :, 0] = 0
    lora_up = a["ffn_B_lora"].transpose(0, 2, 1).reshape(NR, 3 * D)
    W_qkvT = a["ffn_W_qkv"].T
    parts = {
        "ident": np.eye(128, dtype=f32), "cls": rows(a["cls_tok"], 128), "interp1": interp1.reshape(128, -1),
        "causal": np.triu(np.ones((TS, TS), f32)), "eps": np.full((128, 1), EPS, f32), "b_gate": rows(a["ffn_b_gate"], 128),
        "tie": rows(np.arange(NEXP, 0, -1).astype(f32), 128), "b_proj": rows(a["ffn_b_proj"], 128),
        "b_v": rows(a["ffn_b_qkv"][2 * D:], 128), "B_qk": lora_up[:, 0:2 * D], "B_v": lora_up[:, 2 * D:],
        "ones_h": ones_h.reshape(128, -1),
        "Wq": split(a["attn_Wq"]), "Wk": split(a["attn_Wk"]), "Wv": split(a["attn_Wv"]), "Wg": split(a["attn_Wg"]),
        "b_gk": a["attn_bgk2"].reshape(HALF, 1), "o_norm": np.tile(a["attn_o_norm_w"], HH).reshape(HALF, 1),
        "blockdiag": (np.arange(HALF)[:, None] // HK == np.arange(D)[None] // HV).astype(f32),
        "headcol": (np.arange(HALF)[:, None] // HK == np.arange(H)[None]).astype(f32),
        "head_mean": (heads96[:, None] == heads96[None]).astype(f32) / f32(HV), "restart": restart.reshape(HALF, -1),
        "Wo": split(a["attn_Wo"]),
        "W_ga": split(np.concatenate([a["ffn_W_gate"].T, a["ffn_A"].reshape(NR, D).T], axis=1)),
        "W_qk": split(W_qkvT[:, 0:2 * D]), "W_v": split(W_qkvT[:, 2 * D:]), "b_qk": a["ffn_b_qkv"][0:2 * D].reshape(4, HALF).T,
        "cls_heads": cls_heads.reshape(HALF, -1), "W_proj": split(a["ffn_W_proj"].T),
        "b0": np.broadcast_to(a["tok_b0"][:, None], (E, 128)), "b1": np.broadcast_to(a["tok_b1"][:, None], (E, 128)),
        "b2": np.concatenate([np.broadcast_to(a["tok_b2"][:, None], (E, 128)), np.ones((1, 128), f32)]),
        "Wf0": WfT[0:E], "Wf1": WfT[E:2 * E], "Wf2": np.concatenate([WfT[2 * E:], a["tok_bf"].reshape(1, D)]),
        "W0": W0.reshape(E, -1), "W1": a["tok_W1"],
        "W2": a["tok_W2"].reshape(E, 2, 8, 48).transpose(0, 2, 1, 3).reshape(E, -1),
        "Wgk1": a["attn_Wgk1"].T, "Wgk2": a["attn_Wgk2"], "interp2": interp2.reshape(E, -1), "to_heads": to_heads.reshape(H, -1),
    }
    arrays = {"pix0": patches(1), "pix1": patches(2), "pix2": patches(4), "index": np.ascontiguousarray(index)}
    for p, blocks in PACKS.items():
        at, n = offsets(p)
        packed = np.zeros((ROWS[p], n), f32)
        for name, cols in blocks:
            m = parts[name]
            packed[0:m.shape[0], at[name][0]:at[name][0] + cols] = m
        arrays[p] = packed

    nc = bacc.Bacc("TRN2", target_bir_lowering=False, num_devices=1)
    args = [nc.dram_tensor("in_" + n, v.shape, mybir.dt.from_np(v.dtype), kind="ExternalInput").ap() for n, v in arrays.items()]
    out = nc.dram_tensor("out_0", (B, T, D), F32, kind="ExternalOutput").ap()
    build(nc, *args, out)
    r = run_bass_kernel_spmd(nc, [{"in_" + n: v for n, v in arrays.items()}], core_ids=[0])
    return r.results[0]["out_0"]
```

```python
from contextlib import ExitStack

import numpy as np

import concourse.bass as bass
from concourse import mybir

F32 = mybir.dt.float32
F16 = mybir.dt.float16
I32 = mybir.dt.int32
U32 = mybir.dt.uint32
ALU = mybir.AluOpType
ACT = mybir.ActivationFunctionType
AX = mybir.AxisListType

B, IMG, CH = 4, 64, 3
D, H = 192, 12
HALF = D // 2
HK, HV = D // 2 // H, D // H
HD = D // H
E = 64
GP = 16
NTOK = IMG * IMG // GP
TS = 128
NC = NTOK // TS
T = NTOK + 1
NT1, NT2 = NTOK // 4, NTOK // 16
NEXP, RANK = 8, 16
NR = NEXP * RANK
CW = B * TS
BANK = 512
EPS = 1e-5
GATE_NORM = 16.0
Q_SCALE = float(HK) ** -0.5
ATT_SCALE = float(HD) ** -0.5
LORA_SCALE = 32.0 / RANK
HH = H // 2

PACKS = {
    "p128": [("ident", 128), ("cls", D), ("eps", 1), ("interp1", 2 * NC * TS), ("causal", TS),
             ("b_gate", NEXP), ("tie", NEXP), ("b_proj", D), ("b_v", D), ("B_qk", 2 * D), ("B_v", D), ("den_rows", TS), ("W_proj", H // 4 * D)],
    "p96": [("Wq", 2 * HALF), ("Wk", 2 * HALF), ("Wv", 2 * D), ("Wg", 2 * D), ("b_gk", 1), ("o_norm", 1),
            ("blockdiag", D), ("headcol", H), ("head_mean", HALF), ("restart", CW), ("Wo", 2 * D),
            ("W_ga", 2 * (NEXP + NR)), ("W_qk", 2 * 2 * D), ("W_v", 2 * D), ("b_qk", 4),
            ("cls_heads", 2 * H)],
    "p65": [("b0", 128), ("b1", 128), ("b2", 128), ("Wf0", D), ("Wf1", D), ("Wf2", D), ("W0", 4 * 48),
            ("W1", 2 * HALF), ("W2", 8 * HALF), ("Wgk1", D), ("Wgk2", HALF), ("interp2", B * NC * TS),
            ("to_heads", D)],
}
ROWS = {"p128": 128, "p96": 96, "p65": 65}


def offsets(pack):
    at, n = {}, 0
    for name, cols in PACKS[pack]:
        at[name] = (n, cols)
        n += cols
    return at, n

PAIRS = B * H
LAG = 2
SLOTS = 8
BANKS = H // 4
STEPS = PAIRS + 5
START = []
USES = [[] for _ in range(STEPS)]
RAWS = [[] for _ in range(STEPS)]
DIVIDES = [[] for _ in range(STEPS)]


def plan():
    for i in range(B):
        qk = [(i, ("qk", m)) for m in range(4)]
        maxima = [(i, ("max", c, hd)) for hd in range(H) for c in range(NC)]
        last = [(i, ("mT",)), (i, ("ck",)), (i, ("cs",))]
        first = H * (i - 1)
        if i == 0:
            START.extend(qk + [(0, ("vc",)), (0, ("v",)), (0, ("cq",)), (1, ("qk", 0)), (1, ("qk", 1))] + maxima[0:8]
                         + [(1, ("qk", 2))] + maxima[8:12] + [(1, ("qk", 3))] + maxima[12:16] + [(1, ("cq",))] + maxima[16:] + last)
        else:
            if i > 1:
                for k, use in enumerate(qk + [(i, ("cq",))]):
                    USES[first - 9 + k // 2].append(use)
            begin, steps = (first, 9) if i == 1 else (first - 2, 10)
            for k, use in enumerate(maxima):
                USES[begin + k * steps // len(maxima)].append(use)
            USES[first + 3].append((i, ("v",)))
            for k, use in enumerate(last):
                USES[begin + steps + (0, 1, 2 if i == 1 else 3)[k]].append(use)
        for b in range(BANKS):
            done = H * i + 4 * b + 3 + LAG + 1
            late = i == B - 1 and b == BANKS - 1
            RAWS[done].append((i, b))
            USES[done + (0 if late else 1)].insert(0, (i, ("den", b)))
            DIVIDES[done + (1 if late else 2)].append((i, b))
        USES[H * i + H + LAG + (1 if i == B - 1 else 3)].insert(0, (i, ("proj",)))
    USES[STEPS - 1].append((B - 1, ("pc",)))


plan()
WORK = START + [use for uses in USES for use in uses]


def work_index(i, key):
    return WORK.index((i, key))


def work_bank(i, key):
    return 6 + work_index(i, key) % 2


def freed(n):
    return sum(key[0] != "den" for _, key in WORK[:n + 1])


def dens(n):
    return sum(key[0] == "den" for _, key in WORK[:n + 1])


def build(nc, pix0, pix1, pix2, index, ones, p128, p96, p65, out):
    n_cols = {p: offsets(p)[1] for p in PACKS}
    with ExitStack() as ctx:
        def sb(name, shape, dt=F32):
            return ctx.enter_context(nc.sbuf_tensor(name, shape, dt))

        packed = {p: sb(p + "_sb", [ROWS[p], n_cols[p]]) for p in PACKS}

        def w(pack, name, rows=None):
            a, n = offsets(pack)[0][name]
            return packed[pack][0:rows or ROWS[pack], a:a + n]

        ident = w("p128", "ident")
        ident96 = ident[0:HALF, 0:HALF]
        cls_rows = w("p128", "cls")
        interp1 = w("p128", "interp1").rearrange("p (a c t) -> p a c t", a=2, c=NC)
        causal = w("p128", "causal")
        eps = w("p128", "eps")
        b_gate = w("p128", "b_gate")
        tie = w("p128", "tie")
        b_proj = w("p128", "b_proj")
        B_qk = w("p128", "B_qk")
        B_v = w("p128", "B_v")
        den_rows = w("p128", "den_rows")
        W_proj = w("p128", "W_proj").rearrange("p (i n) -> p i n", i=BANKS)
        Wq = w("p96", "Wq").rearrange("p (i n) -> p i n", i=2)
        Wk = w("p96", "Wk").rearrange("p (i n) -> p i n", i=2)
        Wv = w("p96", "Wv").rearrange("p (i n) -> p i n", i=2)
        Wg = w("p96", "Wg").rearrange("p (i n) -> p i n", i=2)
        b_gk = w("p96", "b_gk")
        o_norm = w("p96", "o_norm")
        blockdiag = w("p96", "blockdiag")
        headcol = w("p96", "headcol")
        head_mean = w("p96", "head_mean")
        restart = w("p96", "restart")
        Wo = w("p96", "Wo").rearrange("p (i n) -> p i n", i=2)
        W_ga = w("p96", "W_ga").rearrange("p (i n) -> p i n", i=2)
        W_qk = w("p96", "W_qk").rearrange("p (i n) -> p i n", i=2)
        W_v = w("p96", "W_v").rearrange("p (i n) -> p i n", i=2)
        b_qk = w("p96", "b_qk")
        b_v = w("p128", "b_v")
        cls_heads = w("p96", "cls_heads").rearrange("p (i n) -> p i n", i=2)
        b_rep = [w("p65", f"b{i}", 65 if i == 2 else E) for i in range(3)]
        Wf = [w("p65", f"Wf{i}", 65 if i == 2 else E) for i in range(3)]
        W0 = w("p65", "W0", E).rearrange("p (i n) -> p i n", i=2)
        W1 = w("p65", "W1", E).rearrange("p (i n) -> p i n", i=2)
        W2 = w("p65", "W2", E).rearrange("p (i n) -> p i n", i=8)
        Wgk1 = w("p65", "Wgk1", 16).rearrange("p (i n) -> p i n", i=2)
        Wgk2 = w("p65", "Wgk2", 16)
        interp2 = w("p65", "interp2", E).rearrange("p (b c t) -> p b c t", b=B, c=NC)
        to_heads = w("p65", "to_heads", H)

        idx = sb("idx", [128, 2 + 8 + NC * GP], I32)
        G2 = sb("G2", [128, 2, B * 48])
        G1 = sb("G1", [128, 8, B * 12])
        G0 = sb("G0", [128, NC, GP, B * CH])
        Gp = sb("Gp", [128, 6 * D])
        G0p = Gp[:, 0:2 * D].rearrange("p (c b j d) -> p c b j d", c=NC, b=B, j=GP)
        G1p = Gp[:, 2 * D:4 * D].rearrange("p (b k d) -> p b k d", b=B, k=8)
        G2p = Gp[:, 4 * D:6 * D].rearrange("p (b k d) -> p b k d", b=B, k=2)
        wT = Gp[:, 0:B * T].rearrange("p (b t) -> p b t", b=B)
        M = sb("M", [HALF, 12, D])
        xT2 = M[:, :, :].rearrange("p a n -> p (a n)")[:, 0:2 * B * T].rearrange("p (a b t) -> p a b t", a=2, b=B)
        bias_h = sb("bias_h", [128, D])
        T2t = sb("T2t", [HALF, 8, B, NT2])
        T1t = sb("T1t", [HALF, 2, B, NT1])
        Z1 = sb("Z1", [128, 2, D])
        Z2 = sb("Z2", [E, D])
        T0t = sb("T0t", [HALF, NC, 2, TS])
        Wgk = sb("Wgk", [HALF, 2, HALF])
        h = sb("h", [128, NC, B, D])
        h1 = sb("h1", [128, NC, B, D])
        h1_cls = sb("h1_cls", [128, D])
        stats = sb("stats", [128, 6, B, 6])
        moments = sb("moments", [128, 6, B, 2])
        ln_var = sb("ln_var", [128, 6, B])
        rstd = sb("rstd", [128, 6, B])
        xh_tiles = sb("xh_tiles", [128, 2 + NC * B, D])
        xh = [xh_tiles[:, 0:1, :], xh_tiles[:, 1:2, :]] + [xh_tiles[:, 2 + B * c:2 + B * (c + 1), :] for c in (0, 1, 0, 1)]
        xT_cls = sb("xT_cls", [HALF, 2, 128])
        xT = [sb("xT", [HALF, 2, CW]), M[:, :, :].rearrange("p a n -> p (a n)")[:, 0:2 * CW].rearrange("p (a n) -> p a n", a=2)]
        q_cls = sb("q_cls", [HALF, 8])
        S0 = sb("S0", [HALF, D])
        shared = sb("shared", [128, 7 * CW + 4 * CW + 7 * (2 * CW + 8)])
        place = [0]

        def early(shape):
            n = int(np.prod(shape[1:]))
            t = shared[0:shape[0], place[0]:place[0] + n]
            place[0] += n
            return t

        late_place = [0]

        def late(shape, dt=F32):
            n = int(np.prod(shape[1:]))
            words = n if dt == F32 else n // 2
            t = shared[0:shape[0], late_place[0]:late_place[0] + words]
            late_place[0] += words
            return t if dt == F32 else t.bitcast(dt)

        zm = early([HALF, CW])
        za = early([HALF, CW])
        zl = early([HALF, CW])
        Gs = early([HALF, CW])
        Gc = early([HALF, CW])
        Eq = early([HALF, CW])
        Ek = early([HALF, CW])
        decay = sb("decay", [HALF, NC, 3, B])
        qt = early([HALF, NC * CW]).rearrange("p (c n) -> p c n", c=NC)
        kt = early([HALF, NC * CW]).rearrange("p (c n) -> p c n", c=NC)
        arena = sb("arena", [128, B * 2 * H * T // 2])
        qm = arena[0:HALF, 0:H * CW].rearrange("p (h c) -> p h c", h=H)
        Vp = arena[:, H * CW:H * CW + NC * B * H * 32].rearrange("p (c b h e) -> p c b h e", c=NC, b=B, h=H)
        A = arena[:, H * CW + NC * B * H * 32:H * CW + NC * B * H * 32 + 16 * TS].rearrange("p (n h t) -> p n h t", n=4, h=4)
        stack = arena[:, :].bitcast(F16).rearrange("p (b s h t) -> p b s h t", b=B, s=2, h=H)
        Sc = sb("Sc", [HALF, NC, B, D])
        S1 = sb("S1", [HALF, B, D])
        ktok = sb("ktok", [128, B, HALF])
        NORMW = 2 * CW + 2 * 4
        def norm_buf():
            t = early([HALF, NORMW])
            return [t[:, 0:2 * CW].rearrange("p (i n) -> p i n", i=2)] * NC + [t[:, 2 * CW:NORMW].rearrange("p (i n) -> p i n", i=2)]

        g_log, g_abs, g_raw, g_w, o_sq, o_ln, yT = (norm_buf() for _ in range(7))
        GW = NEXP + NR
        logits = sb("logits", [128, NC, B + 1, NEXP])
        pr = sb("pr", [128, NC, 6, B + 1, NEXP])
        sm = sb("sm", [128, NC, 8, B + 1])
        disp = sb("disp", [128, NC, B + 1, NEXP])
        aw = late([128, B + 1, NR]).rearrange("p (b n) -> p b n", b=B + 1)
        x2_cls = xT_cls
        qk_hi = late([HALF, 2, 4, T], F16).rearrange("p (a m t) -> p a m t", a=2, m=4)
        qk_lo = late([HALF, 2, 4, T], F16).rearrange("p (a m t) -> p a m t", a=2, m=4)
        cls_qk = sb("cls_qk", [HALF, 2, 2, 2, H], F16)
        w_rep = sb("w_rep", [NR, H])
        v2 = late([128, 2, 2, H, 32]).rearrange("p (a c h e) -> p a c h e", a=2, c=2, h=H)
        v_cls = late([HALF, H * 32]).rearrange("p (h e) -> p h e", h=H)
        mx = sb("mx", [128, 2, 2, H])
        mx_cls = sb("mx_cls", [H, 2])
        neg_m = T1t[0:H].rearrange("p a b n -> p (a b n)")[:, 0:T].bitcast(F16).rearrange("p (a t) -> p a t", a=2)
        pT = late([128, SLOTS, 2, T]).rearrange("p (n c t) -> p n c t", n=SLOTS, c=2)
        p_cls = late([HALF, 2, T]).rearrange("p (a t) -> p a t", a=2)
        s_clsk = late([H, T])
        s_clsq = late([128, 2 * H * NC]).rearrange("p (a h c) -> p a h c", a=2, h=H)
        p_clsq = late([128, 2 * H * NC]).rearrange("p (a h c) -> p a h c", a=2, h=H)
        raw = late([128, BANKS, T]).rearrange("p (a t) -> p a t", a=BANKS)
        den_r = late([128, 2, T]).rearrange("p (a t) -> p a t", a=2)
        oT = late([128, 2, BANKS, T]).rearrange("p (b a t) -> p b a t", b=2, a=BANKS)
        oT_cls = late([128, BANKS * B]).rearrange("p (a b) -> p a b", a=BANKS)
        res = h1
        res_cls = G2[0:B, 0, :]
        fin = h
        fin_cls = G2[0:B, 1, :]
        PS = ctx.enter_context(nc.psum_tensor("PS", [128, 8, BANK], F32))
        bounce = nc.dram_tensor("bounce", (B, 2, 4 * HALF, T), F16, kind="Internal").ap()

        NAMES = (
            "pool_chain v2_padded weights_a weights_b weights_c idx_loaded gathered_coarse gathered0 gathered1 dve_chain act_chain "
            "cls_cols pads_zero perm_done moments_done rstd_done xh_done cls_T xT_cls_evac bias_done bias_evac M_done "
            "M_evac Wgk_done Wgk_evac cls_proj cls_qk_evac S0_done o_cls g_read g_log g_logsig o_square "
            "ms_done o_log weight_log weight y_done wo_done h1_done coarse_T T2_evac T1_evac Z_done Z1_evac Z2_evac "
            "T0_done T0_evac h_mm h_evac xh_T xT_evac_a xT_evac_v z_done z_read z_log Gc_done decays "
            "q_done k_done qt_done kt_done qm_done v_done v_evac Sin_done sc_done A_done av_done kT_done kT_evac "
            "kv_done S1_done g_done xT2_evac ga_done logits_sub logits_exp disp_done aw_done aw_T wT_evac "
            "reps_done work_full work_free qk_hi_done bounced_out bounced stacked cls_qk_done sT_done p_done "
            "pv_done raw_done den_log den_rec p_cls_in p_cls_done s_clsq_in p_clsq_done p_col_done neg_m_done neg_m_stacked "
            "ones_stacked rows_zero oT_done res_done fin_done stored"
        ).split()
        s = {n: ctx.enter_context(nc.semaphore(n)) for n in NAMES}
        block = ctx.enter_context(nc.Block())

        SC_BANKS = (0, 3, 6, 7)
        H_BANKS = ((5, 6), (5, 4))
        XT_BANKS = ((7, 0), (4, 5))
        Z_BANK, Q_BANK, K_BANK = (3, 4), (1, 4), (2, 5)
        NG = B * (H // 4)
        o_ps = PS[0:HALF, 1:3, :]
        NORM = {
            2: (PS[0:HALF, 2, 0:8].rearrange("p (i n) -> p i n", i=2), PS[0:HALF, 4, 0:8].rearrange("p (i n) -> p i n", i=2),
                PS[0:HALF, 3, 0:8].rearrange("p (i n) -> p i n", i=2)),
            0: (o_ps, PS[0:HALF, 4:6, :], PS[0:HALF, 6:8, :]),
            1: (o_ps, PS[0:HALF, 4:6, :], PS[0:HALF, 6:8, :]),
        }
        TURN = {2: 1, 0: 2, 1: 3}

        def padded(t):
            return bass.AP(t.tensor, t.offset, [list(t.ap[0]), [64, H // 2], [48, 2], [1, HV]])

        def heads(t):
            return t.rearrange("p (a e v) -> p a e v", a=H // 2, e=2)

        def bc(t, shape):
            return t.to_broadcast(shape)

        @block.sync
        def _(sp):
            n128, n96, n65 = (offsets(p)[0] for p in ("p128", "p96", "p65"))
            sp.dma_start(idx[:, :], index).then_inc(s["idx_loaded"], 16)
            a = n128["interp1"][0]
            sp.dma_start(packed["p128"][:, 0:a], p128[:, 0:a]).then_inc(s["weights_a"], 16)
            b = n65["interp2"][0]
            sp.dma_start(packed["p65"][:, 0:b], p65[:, 0:b]).then_inc(s["weights_a"], 16)
            c = n96["W_ga"][0]
            sp.dma_start(packed["p96"][:, 0:c], p96[:, 0:c]).then_inc(s["weights_b"], 16)
            sp.dma_start(packed["p128"][:, a:], p128[:, a:]).then_inc(s["weights_b"], 16)
            sp.dma_start(packed["p65"][:, b:], p65[:, b:]).then_inc(s["weights_c"], 16)
            sp.dma_start(packed["p96"][:, c:], p96[:, c:]).then_inc(s["weights_c"], 16)
            def store(i):
                sp.wait_ge(s["fin_done"], i + 1)
                sp.dma_start(out[i, 1:T, :].rearrange("(c t) n -> t c n", c=NC), fin[:, :, i, :]).then_inc(s["stored"], 16)

            def negated_maxima(i):
                sp.wait_ge(s["neg_m_done"], i + 1)
                sp.dma_start(stack[64:65, i, 0], neg_m[:, i % 2, :]).then_inc(s["neg_m_stacked"], 16)

            for i in range(B):
                for part, t in ((0, qk_hi), (1, qk_lo)):
                    if part == 0:
                        sp.wait_ge(s["qk_hi_done"], 4 * (i + 1))
                    else:
                        sp.wait_ge(s["bounced_out"], i + 1)
                    sp.dma_start(bounce[i, part].rearrange("(m p) c -> p m c", m=4), t[:, i % 2]).then_inc(s["bounced"], 16)
                sp.wait_ge(s["bounced"], 32 * (i + 1))
                for side, parts in ((0, (0, 0, 1, 1)), (1, (0, 1, 0, 1))):
                    for slot, part in enumerate(parts):
                        src = bounce[i, part, side * D:(side + 1) * D, :].rearrange("(h d) c -> d h c", d=HD)
                        sp.dma_start(stack[HD * slot:HD * (slot + 1), i, side], src).then_inc(s["stacked"], 16)
                if i == 0:
                    sp.wait_ge(s["rows_zero"], 1)
                    sp.dma_start(stack[64:65, :, 1], ones).then_inc(s["ones_stacked"], 16)
                else:
                    negated_maxima(i - 1)
            negated_maxima(B - 1)
            for i in range(B - 1):
                store(i)
            store(B - 1)
            sp.wait_ge(s["fin_done"], B + 1)
            sp.dma_start(out[:, 0, :], fin_cls).then_inc(s["stored"], 16)
            sp.wait_ge(s["stored"], 16 * (B + 1))

        @block.gpsimd
        def _(pool):
            pool.wait_ge(s["idx_loaded"], 16)

            def gather(dst, table, col, sem):
                pool.indirect_dma_start(dst, None, table, bass.IndirectOffsetOnAxis(ap=idx[:, col:col + 1].bitcast(U32), axis=0)
                                        ).then_inc(s[sem], 16)

            for k in range(2):
                gather(G2[:, k, :], pix2, k, "gathered_coarse")
            for k in range(8):
                gather(G1[:, k, :], pix1, 2 + k, "gathered_coarse")
            for c in range(NC):
                for j in range(GP):
                    gather(G0[:, c, j, :], pix0, 10 + c * GP + j, f"gathered{c}")
            pool.wait_ge(s["sc_done"], 2 * NG)
            pool.memset(v2, 0.0).then_inc(s["pool_chain"], 1)
            pool.wait_ge(s["pool_chain"], 1)
            pool.memset(v2[:, :, :, :, 0], 1.0).then_inc(s["v2_padded"], 1)
            pool.wait_ge(s["v2_padded"], 1)
            pool.wait_ge(s["av_done"], 2 * NG)
            pool.wait_ge(s["S1_done"], B)
            pool.memset(arena[64:128, :], 0.0).then_inc(s["rows_zero"], 1)
            pool.wait_ge(s["rows_zero"], 1)
            pool.wait_ge(s["weights_b"], 32)
            pool.wait_ge(s["h1_done"], 1 + 2 * NC)
            pool.wait_ge(s["xh_done"], 4 + NC)
            pool.tensor_tensor(res_cls, h1_cls[0:B, :], b_proj[0:B, :], ALU.add).then_inc(s["res_done"], 1)
            for c in range(NC):
                for i in range(B):
                    pool.tensor_tensor(res[:, c, i, :], h1[:, c, i, :], b_proj, ALU.add).then_inc(s["res_done"], 1)
            for n in range(PAIRS):
                i, hd = n // H, n % H
                if hd == 0:
                    pool.wait_ge(s["p_clsq_done"], i + 1)
                if n >= SLOTS:
                    pool.wait_ge(s["pv_done"], n - SLOTS + 1)
                pool.tensor_copy(pT[:, n % SLOTS, :, 0], p_clsq[:, i % 2, hd, :]).then_inc(s["p_col_done"], 1)

        @block.scalar
        def _(act):
            chain = [0]

            def link(ins):
                chain[0] += 1
                ins.then_inc(s["act_chain"], 1)
                act.wait_ge(s["act_chain"], chain[0])

            def layer_norm(k, rows, n):
                act.wait_ge(s["moments_done"], k + 1)
                link(act.activation(ln_var[0:rows, k, 0:n], moments[0:rows, k, 0:n, 1], ACT.Ln,
                                    bias=eps[0:rows], scale=1.0))
                act.activation(rstd[0:rows, k, 0:n], ln_var[0:rows, k, 0:n], ACT.Exp, scale=-0.5
                               ).then_inc(s["rstd_done"], 1)

            def gate_parts(j):
                _, g_psum, _ = NORM[j]
                if j == 1:
                    act.wait_ge(s["y_done"], 2)
                act.activation(g_raw[j], g_psum, ACT.Copy).then_inc(s["g_read"], 1)
                act.wait_ge(s["g_read"], TURN[j])
                link(act.activation(g_abs[j], g_raw[j], ACT.Abs))
                link(act.activation(g_abs[j], g_abs[j], ACT.Exp, scale=-1.0))
                act.activation(g_abs[j], g_abs[j], ACT.Ln, bias=1.0).then_inc(s["g_log"], 1)

            def squares(j):
                act.activation(o_sq[j], NORM[j][0], ACT.Square).then_inc(s["o_square"], 1)

            def mean_logs(j):
                act.wait_ge(s["ms_done"], TURN[j])
                act.activation(o_ln[j], NORM[j][2], ACT.Ln, bias=eps[0:HALF], scale=1.0).then_inc(s["o_log"], 1)

            def weights(j):
                act.wait_ge(s["weight_log"], TURN[j])
                act.activation(o_sq[j], g_w[j], ACT.Exp).then_inc(s["weight"], 1)

            act.preload_act_table_set("natural_log_exp_and_others")
            act.wait_ge(s["weights_a"], 32)
            layer_norm(0, 128, 1)
            for i in range(1, 6, 2):
                act.wait_ge(s["M_done"], i + 1)
                act.activation(M[:, 2 * i:2 * i + 2, :], PS[0:HALF, 2 + i, 0:2 * D].rearrange("p (a n) -> p a n", a=2),
                               ACT.Copy).then_inc(s["M_evac"], 1)
            act.wait_ge(s["weights_b"], 32)
            act.wait_ge(s["cls_proj"], 1)
            gate_parts(2)
            act.wait_ge(s["o_cls"], 1)
            squares(2)
            act.wait_ge(s["coarse_T"], 1)
            act.activation(T2t[:, :, :, :], PS[0:HALF, 4, :].rearrange("p (b j n) -> p j b n", b=B, j=8), ACT.Copy).then_inc(s["T2_evac"], 1)
            mean_logs(2)
            weights(2)
            act.wait_ge(s["Z_done"], 1)
            act.activation(Z1[:, :, :], PS[:, 6, 0:2 * D].rearrange("p (a n) -> p a n", a=2), ACT.Copy).then_inc(s["Z1_evac"], 1)
            layer_norm(1, 128, 1)

            def patches(c):
                act.wait_ge(s["T0_done"], c + 1)
                act.activation(T0t[:, c], PS[0:HALF, 4, 0:2 * TS].rearrange("p (a n) -> p a n", a=2), ACT.Copy).then_inc(s["T0_evac"], 1)

            def tokens(c):
                patches(c)
                layer_norm(2 + c, 128, B)
                act.wait_ge(s["xh_T"], c + 1)
                act.activation(xT[c][:, 0, :], PS[0:HALF, XT_BANKS[c][0], :], ACT.Copy).then_inc(s["xT_evac_a"], 1)

            def decay_logs(c):
                act.wait_ge(s["z_done"], c + 1)
                act.activation(zm[:, :], PS[0:HALF, Z_BANK[c], :], ACT.Identity, bias=b_gk, scale=1.0).then_inc(s["z_read"], 1)
                act.wait_ge(s["z_read"], c + 1)
                link(act.activation(za[:, :], zm[:, :], ACT.Abs))
                link(act.activation(za[:, :], za[:, :], ACT.Exp, scale=-1.0))
                act.activation(zl[:, :], za[:, :], ACT.Ln, bias=1.0).then_inc(s["z_log"], 1)

            def decays(c):
                act.wait_ge(s["Gc_done"], c + 1)
                if c:
                    act.wait_ge(s["qt_done"], c)
                    act.wait_ge(s["kt_done"], c)
                act.activation(Eq[:, :], Gc[:, :], ACT.Exp, scale=1.0 / GATE_NORM).then_inc(s["decays"], 1)
                act.activation(Ek[:, :], Gc[:, :], ACT.Exp, scale=-1.0 / GATE_NORM).then_inc(s["decays"], 1)
                by_image = Gs[:, :].rearrange("p (b t) -> p b t", b=B)
                about = Gc[:, :].rearrange("p (b t) -> p b t", b=B)
                act.activation(decay[:, c, 0, :], by_image[:, :, TS // 2 - 1], ACT.Exp, scale=1.0 / GATE_NORM)
                act.activation(decay[:, c, 1, :], about[:, :, TS - 1], ACT.Exp, scale=1.0 / GATE_NORM)
                act.activation(decay[:, c, 2, :], by_image[:, :, TS - 1], ACT.Exp, scale=1.0 / GATE_NORM).then_inc(s["decays"], 1)

            def values(c):
                for i in range(B):
                    act.wait_ge(s["v_done"], 2 * c + i // 2 + 1)
                    if c == 0 and i == 0:
                        act.wait_ge(s["pads_zero"], 1)
                    v = PS[:, 6 + i // 2, (i % 2) * D:(i % 2 + 1) * D]
                    act.activation(padded(Vp[:, c, i]), heads(v), ACT.Copy).then_inc(s["v_evac"], 1)

            tokens(0)
            decay_logs(0)
            decays(0)
            act.wait_ge(s["g_done"], 1)
            gate_parts(0)
            values(0)
            tokens(1)
            decay_logs(1)
            act.wait_ge(s["kT_done"], 1)
            act.activation(ktok[:, :, :], PS[:, 0, 0:B * HALF].rearrange("p (b n) -> p b n", b=B), ACT.Copy).then_inc(s["kT_evac"], 1)
            act.wait_ge(s["av_done"], NG)
            squares(0)
            decays(1)
            mean_logs(0)
            weights(0)
            values(1)
            act.wait_ge(s["g_done"], 2)
            gate_parts(1)

            def inputs(c):
                layer_norm(4 + c, 128, B)
                act.wait_ge(s["xh_T"], 2 + c + 1)
                act.activation(xT2[:, 0, :, 1 + c * TS:1 + (c + 1) * TS], PS[0:HALF, 4, :].rearrange("p (b n) -> p b n", b=B),
                               ACT.Copy).then_inc(s["xT_evac_a"], 1)

            def experts(c):
                n = B + 1 if c == 0 else B
                act.wait_ge(s["logits_sub"], c + 1)
                act.activation(pr[:, c, 0, 0:n, :], pr[:, c, 0, 0:n, :], ACT.Exp).then_inc(s["logits_exp"], 1)

            def routed(c):
                act.wait_ge(s["aw_T"], c + 1)
                if c == 0:
                    for half in range(2):
                        act.activation(xT2[:, half, :, 0], x2_cls[:, half, 0:B], ACT.Copy)
                    act.activation(wT[:, :, 0], PS[:, 5, 0:B], ACT.Copy)
                    act.activation(w_rep[:, :], PS[:, 5, 0:H], ACT.Copy).then_inc(s["cls_cols"], 1)
                act.activation(wT[:, :, 1 + c * TS:1 + (c + 1) * TS], PS[:, 4, :].rearrange("p (b n) -> p b n", b=B),
                               ACT.Copy).then_inc(s["wT_evac"], 1)

            inputs(0)
            experts(0)
            act.wait_ge(s["av_done"], 2 * NG)
            squares(1)
            mean_logs(1)
            routed(0)
            weights(1)
            inputs(1)
            experts(1)
            routed(1)

            def high_part(i, m):
                    act.wait_ge(s["work_full"], work_index(i, ("qk", m)) + 1)
                    if i >= 2 and m == 0:
                        act.wait_ge(s["bounced"], 32 * (i - 1))
                    act.activation(qk_hi[:, i % 2, m, :], PS[0:HALF, work_bank(i, ("qk", m)), 0:T], ACT.Identity,
                                   bias=b_qk[:, m:m + 1], scale=1.0).then_inc(s["qk_hi_done"], 1)

            def cls_probs(i):
                act.wait_ge(s["p_cls_in"], i + 1)
                act.wait_ge(s["pads_zero"], 2)
                if i >= 2:
                    act.wait_ge(s["pv_done"], H * (i - 1))
                act.activation(p_cls[0:H, i % 2, :], s_clsk[:, :], ACT.Exp, scale=ATT_SCALE).then_inc(s["p_cls_done"], 1)

            def cls_query_probs(i):
                act.wait_ge(s["s_clsq_in"], i + 1)
                if i >= 2:
                    act.wait_ge(s["p_col_done"], H * (i - 1))
                act.activation(p_clsq[:, i % 2], s_clsq[:, i % 2], ACT.Exp, scale=ATT_SCALE).then_inc(s["p_clsq_done"], 1)

            def probs(n):
                act.wait_ge(s["sT_done"], n + 1)
                if n >= SLOTS:
                    act.wait_ge(s["pv_done"], n - SLOTS + 1)
                act.activation(pT[:, n % SLOTS, :, 1:T], PS[:, n % 3, :].rearrange("p (c t) -> p c t", c=NC), ACT.Exp, scale=ATT_SCALE
                               ).then_inc(s["p_done"], 1)

            def denominators(i, b):
                r = BANKS * i + b
                act.wait_ge(s["work_full"], work_index(i, ("den", b)) + 1)
                if r >= 2:
                    act.wait_ge(s["oT_done"], r - 1)
                act.activation(den_r[:, r % 2, :], PS[:, work_bank(i, ("den", b)), 0:T], ACT.Ln).then_inc(s["den_log"], 1)
                act.wait_ge(s["den_log"], r + 1)
                act.activation(den_r[:, r % 2, :], den_r[:, r % 2, :], ACT.Exp, scale=-1.0).then_inc(s["den_rec"], 1)

            def reads(uses):
                for i, key in uses:
                    if key[0] == "qk":
                        high_part(i, key[1])
                    elif key == ("ck",):
                        cls_probs(i)
                    elif key == ("cs",):
                        cls_query_probs(i)
                    elif key[0] == "den":
                        denominators(i, key[1])

            reads(START)
            for g in range(STEPS):
                if g < PAIRS:
                    probs(g)
                reads(USES[g])

        @block.vector
        def _(dve):
            chain = [0]

            def link(ins):
                chain[0] += 1
                ins.then_inc(s["dve_chain"], 1)
                dve.wait_ge(s["dve_chain"], chain[0])

            def copy_then(out_, in_, sem):
                dve.tensor_copy(out_, in_).then_inc(s[sem], 1)

            def moments_of(k, tiles):
                for i, t in enumerate(tiles):
                    last = dve.bn_stats(stats[:, k, i, :], t)
                link(last)
                for i in range(len(tiles)):
                    last = dve.bn_aggr(moments[:, k, i, :], stats[:, k, i, :])
                last.then_inc(s["moments_done"], 1)

            def normalise(k, tiles):
                dve.wait_ge(s["moments_done"], k + 1)
                dve.wait_ge(s["rstd_done"], k + 1)
                for i, t in enumerate(tiles):
                    last = dve.tensor_scalar(xh[k][:, i, :], t, moments[:, k, i, 0:1], rstd[:, k, i:i + 1],
                                             ALU.subtract, ALU.mult)
                last.then_inc(s["xh_done"], 1)

            def gate_logsig(j):
                dve.wait_ge(s["g_log"], TURN[j])
                if j == 1:
                    dve.wait_ge(s["weight_log"], 2)
                dve.scalar_tensor_tensor(g_log[j], g_raw[j], 0.0, g_abs[j], ALU.min, ALU.subtract).then_inc(s["g_logsig"], 1)

            def weight_logs(j):
                dve.wait_ge(s["o_log"], TURN[j])
                dve.wait_ge(s["g_logsig"], TURN[j])
                dve.scalar_tensor_tensor(g_w[j], o_ln[j], -0.5, g_log[j], ALU.mult, ALU.add).then_inc(s["weight_log"], 1)

            def outputs(j):
                dve.wait_ge(s["weight"], TURN[j])
                link(dve.scalar_tensor_tensor(g_w[j], g_raw[j], o_norm, o_sq[j], ALU.mult, ALU.mult))
                dve.tensor_tensor(yT[j], NORM[j][0], g_w[j], ALU.mult).then_inc(s["y_done"], 1)

            dve.memset(Vp[:, :, :, :, :], 0.0).then_inc(s["pads_zero"], 1)

            dve.wait_ge(s["weights_a"], 32)
            moments_of(0, [cls_rows])
            normalise(0, [cls_rows])
            dve.wait_ge(s["bias_done"], 1)
            copy_then(bias_h[:, :], PS[:, 1, 0:D], "bias_evac")
            dve.wait_ge(s["cls_T"], 1)
            copy_then(xT_cls[:, :, :], PS[0:HALF, 0, 0:256].rearrange("p (i n) -> p i n", i=2), "xT_cls_evac")
            for i in range(0, 6, 2):
                dve.wait_ge(s["M_done"], i + 1)
                dve.tensor_copy(M[:, 2 * i:2 * i + 2, :], PS[0:HALF, 2 + i, 0:2 * D].rearrange("p (a n) -> p a n", a=2)
                                ).then_inc(s["M_evac"], 1)
            dve.wait_ge(s["Wgk_done"], 1)
            copy_then(Wgk[:, :, :], PS[0:HALF, 0, 0:D].rearrange("p (i n) -> p i n", i=2), "Wgk_evac")
            dve.wait_ge(s["weights_b"], 32)
            dve.wait_ge(s["cls_proj"], 1)
            dve.tensor_scalar(q_cls[:, 0:4], PS[0:HALF, 1, 0:4], Q_SCALE, None, ALU.mult)
            link(dve.tensor_copy(q_cls[:, 4:8], PS[0:HALF, 1, 4:8]))
            dve.scalar_tensor_tensor(S0[:, :], PS[0:HALF, 1, 16:16 + D], q_cls[:, 4:5], blockdiag, ALU.mult, ALU.mult
                                     ).then_inc(s["S0_done"], 1)
            dve.wait_ge(s["gathered_coarse"], 16 * 10)
            dve.tensor_copy(G2p[:, :, :, :], G2[:, :, :].rearrange("p k (b d) -> p b k d", b=B))
            dve.tensor_copy(G1p[:, :, :, :], G1[:, :, :].rearrange("p k (b d) -> p b k d", b=B)).then_inc(s["perm_done"], 1)
            gate_logsig(2)
            dve.wait_ge(s["coarse_T"], 1)
            copy_then(T1t[:, :, :, :], PS[0:HALF, 5, :].rearrange("p (b k n) -> p k b n", b=B, k=2), "T1_evac")
            weight_logs(2)
            outputs(2)
            dve.wait_ge(s["Z_done"], 1)
            copy_then(Z2[:, :], PS[0:E, 7, 0:D], "Z2_evac")
            dve.wait_ge(s["wo_done"], 1)
            dve.tensor_tensor(h1_cls[:, :], PS[:, 0, 0:D], cls_rows, ALU.add).then_inc(s["h1_done"], 1)
            dve.wait_ge(s["h1_done"], 1)
            moments_of(1, [h1_cls[:, :]])
            normalise(1, [h1_cls[:, :]])

            def permute(c):
                dve.wait_ge(s[f"gathered{c}"], 16 * GP)
                for i in range(B):
                    last = dve.tensor_copy(G0p[:, c, i, :, :], G0[:, c, :, CH * i:CH * (i + 1)])
                last.then_inc(s["perm_done"], 1)

            def add_bias(c):
                for a in range(2):
                    dve.wait_ge(s["h_mm"], 2 * c + a + 1)
                    last = dve.tensor_tensor(h[:, c, 2 * a:2 * a + 2, :], PS[:, H_BANKS[c][a], 0:2 * D].rearrange("p (a n) -> p a n", a=2),
                                             bias_h[:, :].unsqueeze(1).to_broadcast([128, 2, D]), ALU.add)
                    last.then_inc(s["h_evac"], 1)
                dve.wait_ge(s["h_evac"], 2 * (c + 1))

            def tiles_of(x, c):
                return [x[:, c, i, :] for i in range(B)]

            def features(c):
                dve.wait_ge(s["xh_T"], c + 1)
                copy_then(xT[c][:, 1, :], PS[0:HALF, XT_BANKS[c][1], :], "xT_evac_v")

            def running_sums(c):
                dve.wait_ge(s["z_log"], c + 1)
                link(dve.scalar_tensor_tensor(zm[:, :], zm[:, :], 0.0, zl[:, :], ALU.min, ALU.subtract))
                if c:
                    dve.wait_ge(s["decays"], 3 * c)
                link(dve.tensor_tensor_scan(Gs[:, :], restart, zm[:, :], 0.0, ALU.mult, ALU.add))
                by_image = Gs[:, :].rearrange("p (b t) -> p b t", b=B)
                middle = by_image[:, :, TS // 2 - 1:TS // 2].to_broadcast([HALF, B, TS])
                dve.tensor_tensor(Gc[:, :].rearrange("p (b t) -> p b t", b=B), by_image, middle, ALU.subtract
                                  ).then_inc(s["Gc_done"], 1)

            def decayed(c):
                dve.wait_ge(s["decays"], 3 * c + 1)
                dve.wait_ge(s["q_done"], c + 1)
                dve.scalar_tensor_tensor(qt[:, c, :], PS[0:HALF, Q_BANK[c], :], Q_SCALE, Eq[:, :], ALU.mult, ALU.mult
                                         ).then_inc(s["qt_done"], 1)
                dve.wait_ge(s["decays"], 3 * c + 2)
                dve.wait_ge(s["k_done"], c + 1)
                dve.tensor_tensor(kt[:, c, :], PS[0:HALF, K_BANK[c], :], Ek[:, :], ALU.mult).then_inc(s["kt_done"], 1)

            def masked_queries(c):
                dve.wait_ge(s["qt_done"], c + 1)
                if c:
                    dve.wait_ge(s["sc_done"], NG * c)
                for hd in range(H):
                    dve.tensor_scalar(qm[:, hd, :], qt[:, c, :], headcol[:, hd:hd + 1], None, ALU.mult).then_inc(s["qm_done"], 1)

            def states_in(c):
                dve.wait_ge(s["decays"], 3 * c + 3)
                for i in range(B):
                    state = S0[:, :] if c == 0 else S1[:, i, :]
                    last = dve.tensor_scalar(Sc[:, c, i, :], state, decay[:, c, 0, i:i + 1], None, ALU.mult)
                last.then_inc(s["Sin_done"], 1)

            def causal_scores(c, g):
                n = NG * c + g
                dve.wait_ge(s["sc_done"], n + 1)
                if n >= 4:
                    dve.wait_ge(s["av_done"], n - 3)
                sc = PS[:, SC_BANKS[n % 4], :].rearrange("p (h t) -> p h t", h=4)
                dve.tensor_tensor(A[:, n % 4], sc, causal.unsqueeze(1).to_broadcast([128, 4, TS]), ALU.mult
                                  ).then_inc(s["A_done"], 1)

            def h1_sum(c):
                for a, bank in ((0, 0), (1, 3)):
                    dve.wait_ge(s["wo_done"], 1 + 2 * c + a + 1)
                    dve.tensor_tensor(h1[:, c, 2 * a:2 * a + 2, :], PS[:, bank, 0:2 * D].rearrange("p (a n) -> p a n", a=2),
                                      h[:, c, 2 * a:2 * a + 2, :], ALU.add).then_inc(s["h1_done"], 1)

            def state_after():
                for i in range(B):
                    dve.wait_ge(s["kv_done"], i // 2 + 1)
                    bank = (3, 0)[i // 2]
                    link(dve.scalar_tensor_tensor(S1[:, i, :], PS[0:HALF, bank, (i % 2) * D:(i % 2 + 1) * D], decay[:, 0, 1, i:i + 1],
                                                  blockdiag, ALU.mult, ALU.mult))
                    dve.scalar_tensor_tensor(S1[:, i, :], S0[:, :], decay[:, 0, 2, i:i + 1], S1[:, i, :], ALU.mult, ALU.add
                                             ).then_inc(s["S1_done"], 1)
                dve.wait_ge(s["S1_done"], B)

            def inputs(c):
                dve.wait_ge(s["xh_T"], 2 + c + 1)
                dve.tensor_copy(xT2[:, 1, :, 1 + c * TS:1 + (c + 1) * TS], PS[0:HALF, 5, :].rearrange("p (b n) -> p b n", b=B)
                                ).then_inc(s["xT2_evac"], 1)

            def route(c):
                units = [PS[:, 4 + i // 2, (i % 2) * GW:(i % 2 + 1) * GW] for i in range(B)]
                if c == 0:
                    units.append(PS[:, 5, 2 * GW:3 * GW])
                n = len(units)
                lg, P = logits[:, c, 0:n, :], [pr[:, c, a, 0:n, :] for a in range(6)]
                r = [sm[:, c, a, 0:n] for a in range(8)]

                def wide(x):
                    return x.unsqueeze(2).to_broadcast([128, n, NEXP])

                dve.wait_ge(s["ga_done"], c + 1)
                for a, u in enumerate(units):
                    last = dve.tensor_tensor(logits[:, c, a, :], u[:, 0:NEXP], b_gate, ALU.add)
                link(last)
                link(dve.tensor_reduce(r[0], lg, AX.X, ALU.max))
                dve.tensor_tensor(P[0], lg, wide(r[0]), ALU.subtract).then_inc(s["logits_sub"], 1)
                dve.wait_ge(s["logits_exp"], c + 1)
                link(dve.tensor_reduce(r[1], P[0], AX.X, ALU.add))
                link(dve.reciprocal(r[2], r[1]))
                link(dve.tensor_tensor(P[1], P[0], wide(r[2]), ALU.mult))
                chosen = []
                left = P[1]
                for turn in range(2):
                    link(dve.tensor_reduce(r[3 + 2 * turn], left, AX.X, ALU.max))
                    link(dve.tensor_tensor(P[2 + turn], left, wide(r[3 + 2 * turn]), ALU.is_ge))
                    link(dve.tensor_tensor(P[2 + turn], P[2 + turn], tie.unsqueeze(1).to_broadcast([128, n, NEXP]), ALU.mult))
                    link(dve.tensor_reduce(r[4 + 2 * turn], P[2 + turn], AX.X, ALU.max))
                    link(dve.tensor_tensor(P[2 + turn], P[2 + turn], wide(r[4 + 2 * turn]), ALU.is_equal))
                    chosen.append(P[2 + turn])
                    if turn == 0:
                        link(dve.scalar_tensor_tensor(P[4], P[2], -2.0, P[1], ALU.mult, ALU.add))
                        left = P[4]
                link(dve.tensor_tensor(P[5], chosen[0], chosen[1], ALU.add))
                link(dve.scalar_tensor_tensor(disp[:, c, 0:n, :], P[5], LORA_SCALE, P[1], ALU.mult, ALU.mult))
                if c:
                    dve.wait_ge(s["aw_T"], c)
                for a, u in enumerate(units):
                    down = u[:, NEXP:NEXP + NR].rearrange("p (e r) -> p e r", e=NEXP)
                    last = dve.tensor_tensor(aw[:, a, :].rearrange("p (e r) -> p e r", e=NEXP), down,
                                             disp[:, c, a, :].unsqueeze(2).to_broadcast([128, NEXP, RANK]), ALU.mult)
                last.then_inc(s["aw_done"], 1)

            permute(0)
            add_bias(0)
            moments_of(2, tiles_of(h, 0))
            normalise(2, tiles_of(h, 0))
            dve.wait_ge(s["cls_T"], 2)
            dve.tensor_copy(x2_cls[:, :, :], PS[0:HALF, 2, 0:256].rearrange("p (i n) -> p i n", i=2)).then_inc(s["xT2_evac"], 1)
            features(0)
            running_sums(0)
            decayed(0)
            masked_queries(0)
            states_in(0)
            permute(1)
            between = {3: lambda: (add_bias(1), moments_of(3, tiles_of(h, 1))), 5: lambda: normalise(3, tiles_of(h, 1)),
                       6: lambda: gate_logsig(0), 8: lambda: features(1)}
            for g in range(NG):
                causal_scores(0, g)
                if g in between:
                    between[g]()
            running_sums(1)
            state_after()
            decayed(1)
            weight_logs(0)
            outputs(0)
            masked_queries(1)
            states_in(1)
            h1_sum(0)
            between = {1: lambda: moments_of(4, tiles_of(h1, 0)), 3: lambda: normalise(4, tiles_of(h1, 0)),
                       4: lambda: gate_logsig(1), 6: lambda: inputs(0)}
            for g in range(NG):
                causal_scores(1, g)
                if g in between:
                    between[g]()
            route(0)
            weight_logs(1)
            outputs(1)
            h1_sum(1)
            dve.wait_ge(s["h1_done"], 5)
            moments_of(5, tiles_of(h1, 1))
            normalise(5, tiles_of(h1, 1))
            inputs(1)
            route(1)
            dve.memset(p_cls, 0.0)
            dve.memset(v_cls, 0.0).then_inc(s["pads_zero"], 1)
            dve.wait_ge(s["pads_zero"], 2)
            dve.tensor_copy(v_cls[0:H, :, 0], ident[0:H, 0:H]).then_inc(s["pads_zero"], 1)
            dve.wait_ge(s["pads_zero"], 3)
            dve.wait_ge(s["v2_padded"], 1)

            def read(n):
                i, key = WORK[n]
                kind = key[0]
                if kind == "den":
                    return
                dve.wait_ge(s["work_full"], n + 1)
                ps = PS[:, 6 + n % 2, :]
                if kind == "qk":
                    m = key[1]
                    dve.wait_ge(s["qk_hi_done"], 4 * i + m + 1)
                    if i >= 2 and m == 0:
                        dve.wait_ge(s["bounced"], 32 * (i - 1))
                    last = dve.scalar_tensor_tensor(qk_lo[:, i % 2, m, :], ps[0:HALF, 0:T], b_qk[:, m:m + 1],
                                                    qk_hi[:, i % 2, m, :], ALU.add, ALU.subtract)
                    last.then_inc(s["work_free"], 1)
                    if m == 3:
                        dve.wait_ge(s["work_free"], freed(n))
                        dve.nop().then_inc(s["bounced_out"], 1)
                        if i == 0:
                            for side in range(2):
                                for part, t in ((0, qk_hi), (1, qk_lo)):
                                    for half in range(2):
                                        last = dve.tensor_tensor(cls_qk[:, side, part, half, :], cls_heads[:, half, :],
                                                                 t[:, 0, 2 * side + half, 0:1].to_broadcast([HALF, H]), ALU.mult)
                            last.then_inc(s["cls_qk_done"], 1)
                elif kind == "vc":
                    v = v_cls[0:H, :, 1:1 + HD]

                    def by_head(t):
                        return t.rearrange("p (h v) -> p h v", h=H)

                    link(dve.tensor_tensor(v, by_head(ps[0:H, 0:D]), by_head(b_v[0:H, :]), ALU.add))
                    dve.tensor_tensor(v, v, by_head(to_heads), ALU.mult).then_inc(s["work_free"], 1)
                elif kind == "v":
                    if i >= 2:
                        dve.wait_ge(s["pv_done"], H * (i - 1))
                    for c in range(NC):
                        last = dve.tensor_tensor(v2[:, i % 2, c, :, 1:1 + HD], ps[:, c * D:(c + 1) * D].rearrange("p (h v) -> p h v", h=H),
                                                 b_v.rearrange("p (h v) -> p h v", h=H), ALU.add)
                    last.then_inc(s["work_free"], 1)
                elif kind == "cq":
                    dve.tensor_reduce(mx_cls[:, i % 2:i % 2 + 1], ps[0:H, 0:T], AX.X, ALU.max).then_inc(s["work_free"], 1)
                elif kind == "max":
                    c, hd = key[1:]
                    dve.tensor_reduce(mx[:, i % 2, c, hd:hd + 1], ps[:, 0:T], AX.X, ALU.max).then_inc(s["work_free"], 1)
                elif kind == "mT":
                    if i >= 2:
                        dve.wait_ge(s["neg_m_stacked"], 16 * (i - 1))
                    dve.tensor_scalar(neg_m[:, i % 2, 0:1], mx_cls[:, i % 2:i % 2 + 1], -1.0, None, ALU.mult)
                    dve.tensor_scalar(neg_m[:, i % 2, 1:T], ps[0:H, 0:NTOK], -1.0, None, ALU.mult).then_inc(s["work_free"], 1)
                    dve.wait_ge(s["work_free"], freed(n))
                    dve.nop().then_inc(s["neg_m_done"], 1)
                elif kind == "ck":
                    if i >= 1:
                        dve.wait_ge(s["p_cls_done"], i)
                    dve.tensor_tensor(s_clsk[:, :], ps[0:H, 0:T], neg_m[:, i % 2, :], ALU.add).then_inc(s["work_free"], 1)
                    dve.wait_ge(s["work_free"], freed(n))
                    dve.nop().then_inc(s["p_cls_in"], 1)
                elif kind == "cs":
                    if i >= 2:
                        dve.wait_ge(s["p_clsq_done"], i - 1)
                    dve.tensor_copy(s_clsq[:, i % 2], ps[:, 0:H * NC].rearrange("p (h c) -> p h c", h=H)).then_inc(s["work_free"], 1)
                    dve.wait_ge(s["work_free"], freed(n))
                    dve.nop().then_inc(s["s_clsq_in"], 1)
                elif kind == "proj":
                    dve.wait_ge(s["res_done"], 1 + 2 * B)
                    dve.tensor_tensor(fin[:, :, i, :], ps[:, 0:2 * D].rearrange("p (c n) -> p c n", c=NC), res[:, :, i, :], ALU.add
                                      ).then_inc(s["work_free"], 1)
                    dve.wait_ge(s["work_free"], freed(n))
                    dve.nop().then_inc(s["fin_done"], 1)
                elif kind == "pc":
                    dve.tensor_tensor(fin_cls, ps[0:B, 0:D], res_cls, ALU.add).then_inc(s["fin_done"], 1)

            def take_raw(i, b):
                dve.wait_ge(s["pv_done"], H * i + 4 * b + 4)
                if i:
                    dve.wait_ge(s["oT_done"], BANKS * (i - 1) + b + 1)
                    dve.wait_ge(s["work_full"], work_index(i - 1, ("den", b)) + 1)
                dve.tensor_copy(raw[:, b, :], PS[:, 3 + b, 0:T]).then_inc(s["raw_done"], 1)

            def divide(i, b):
                r = BANKS * i + b
                dve.wait_ge(s["raw_done"], r + 1)
                dve.wait_ge(s["den_rec"], r + 1)
                if i >= 2 and b == 0:
                    dve.wait_ge(s["work_full"], work_index(i - 2, ("proj",)) + 1)
                dve.tensor_tensor(oT_cls[:, b, i:i + 1], raw[:, b, 0:1], den_r[:, r % 2, 0:1], ALU.mult)
                dve.tensor_tensor(oT[:, i % 2, b, :], raw[:, b, :], den_r[:, r % 2, :], ALU.mult).then_inc(s["oT_done"], 1)

            n_use = 0
            for _ in START:
                read(n_use)
                n_use += 1
            for g in range(STEPS):
                for i, b in RAWS[g]:
                    take_raw(i, b)
                for i, b in DIVIDES[g]:
                    divide(i, b)
                for _ in USES[g]:
                    read(n_use)
                    n_use += 1

        @block.tensor
        def _(pe):
            def halves(out_, lhs, rhs):
                for half in range(2):
                    last = pe.matmul(out_, lhs[half], rhs[half], start=(half == 0), stop=(half == 1), skip_group_check=True)
                return last

            pe.wait_ge(s["weights_a"], 32)
            for i in range(3):
                last = pe.matmul(PS[:, 1, 0:D], b_rep[i], Wf[i], start=(i == 0), stop=(i == 2))
            last.then_inc(s["bias_done"], 1)
            factors = [(W0[:, i, :], 0) for i in range(2)] + [(W1[:, i, :], 1) for i in range(2)] + [(W2[:, i, :], 2) for i in range(8)]
            for i, (f, level) in enumerate(factors):
                last = pe.matmul(PS[0:HALF, 2 + i // 2, (i % 2) * D:(i % 2 + 1) * D], f, Wf[level][0:E], start=True, stop=True)
                if i % 2:
                    last.then_inc(s["M_done"], 1)
            pe.wait_ge(s["xh_done"], 1)
            for half in range(2):
                last = pe.transpose(PS[0:HALF, 0, half * 128:(half + 1) * 128], xh[0][:, 0, half * HALF:(half + 1) * HALF], ident)
            last.then_inc(s["cls_T"], 1)
            pe.wait_ge(s["xT_cls_evac"], 1)
            for half in range(2):
                last = pe.matmul(PS[0:HALF, 0, half * HALF:(half + 1) * HALF], Wgk1[:, half, :], Wgk2, start=True, stop=True)
            last.then_inc(s["Wgk_done"], 1)
            pe.wait_ge(s["weights_b"], 32)
            pe.wait_ge(s["bias_evac"], 1)
            pe.wait_ge(s["M_evac"], 6)
            x4 = [xT_cls[:, i, 0:B] for i in range(2)]
            halves(PS[0:HALF, 1, 0:4], [Wq[:, i, :] for i in range(2)], x4)
            halves(PS[0:HALF, 1, 4:8], [Wk[:, i, :] for i in range(2)], x4)
            for m in range(2):
                halves(PS[0:HALF, 4, 4 * m:4 * m + 4], [Wg[:, i, m * HALF:(m + 1) * HALF] for i in range(2)], x4)
            halves(PS[0:HALF, 1, 16:16 + D], [xT_cls[:, i, 0:HALF] for i in range(2)], [Wv[:, i, :] for i in range(2)]
                   ).then_inc(s["cls_proj"], 1)
            pe.wait_ge(s["S0_done"], 1)
            for m in range(2):
                last = pe.matmul(PS[0:HALF, 2, 4 * m:4 * m + 4], S0[:, m * HALF:(m + 1) * HALF], q_cls[:, 0:4], start=True, stop=True)
            last.then_inc(s["o_cls"], 1)

            def mean_squares(j):
                _, _, ms_psum = NORM[j]
                pe.wait_ge(s["o_square"], TURN[j])
                for m in range(2):
                    last = pe.matmul(ms_psum[:, m, :], head_mean, o_sq[j][:, m, :], start=True, stop=True)
                last.then_inc(s["ms_done"], 1)

            pe.wait_ge(s["perm_done"], 1)
            pe.wait_ge(s["g_read"], 1)
            for i in range(B):
                pe.transpose(PS[0:HALF, 4, i * 128:(i + 1) * 128], G2p[:, i, :, :], ident)
            for i in range(B):
                last = pe.transpose(PS[0:HALF, 5, i * 128:(i + 1) * 128], G1p[:, i, :, :], ident)
            last.then_inc(s["coarse_T"], 1)
            mean_squares(2)
            pe.wait_ge(s["T1_evac"], 1)
            for a in range(2):
                for half in range(2):
                    pe.matmul(PS[:, 6, a * D:(a + 1) * D], T1t[:, half, 2 * a:2 * a + 2, :], M[:, 2 + half, :],
                              start=(half == 0), stop=(half == 1))
            pe.wait_ge(s["T2_evac"], 1)
            for j in range(8):
                last = pe.matmul(PS[0:E, 7, 0:D], T2t[:, j, :, :], M[:, 4 + j, :], start=(j == 0), stop=(j == 7))
            last.then_inc(s["Z_done"], 1)
            pe.wait_ge(s["y_done"], 1)
            pe.wait_ge(s["Wgk_evac"], 1)
            halves(PS[:, 0, 0:D], [yT[2][:, i, 0:1].to_broadcast([HALF, 128]) for i in range(2)], [Wo[:, i, :] for i in range(2)]
                   ).then_inc(s["wo_done"], 1)

            def patches(c):
                pe.wait_ge(s["perm_done"], c + 2)
                if c == 0:
                    pe.wait_ge(s["T2_evac"], 1)
                else:
                    pe.wait_ge(s["g_read"], 2)
                for a in range(2):
                    last = pe.transpose(PS[0:HALF, 4, a * TS:(a + 1) * TS], G0p[:, c, 2 * a:2 * a + 2, :, :], ident)
                last.then_inc(s["T0_done"], 1)

            def tokens(c):
                pe.wait_ge(s["T0_evac"], c + 1)
                if c == 0:
                    pe.wait_ge(s["weights_c"], 32)
                    pe.wait_ge(s["Z1_evac"], 1)
                    pe.wait_ge(s["Z2_evac"], 1)
                for i in range(B):
                    out_ = PS[:, H_BANKS[c][i // 2], (i % 2) * D:(i % 2 + 1) * D]
                    pe.matmul(out_, T0t[:, c, i // 2, :], M[:, i % 2, :], start=True, stop=False, skip_group_check=True)
                    pe.matmul(out_, interp1[:, i % 2, c, :], Z1[:, i // 2, :], start=False, stop=False, skip_group_check=True)
                    last = pe.matmul(out_, interp2[:, i, c, :], Z2[:, :], start=False, stop=True, skip_group_check=True)
                    if i % 2:
                        last.then_inc(s["h_mm"], 1)

            def features(c):
                pe.wait_ge(s["xh_done"], 2 + c + 1)
                pe.wait_ge(s["h_evac"], 2 * (c + 1))
                for half in range(2):
                    for i in range(B):
                        last = pe.transpose(PS[0:HALF, XT_BANKS[c][half], i * TS:(i + 1) * TS],
                                            xh[2 + c][:, i, half * HALF:(half + 1) * HALF], ident)
                last.then_inc(s["xh_T"], 1)

            def columns(c):
                return [xT[c][:, i, :] for i in range(2)]

            def decay_inputs(c):
                pe.wait_ge(s["xT_evac_a"], c + 1)
                pe.wait_ge(s["xT_evac_v"], c + 1)
                halves(PS[0:HALF, Z_BANK[c], :], [Wgk[:, i, :] for i in range(2)], columns(c)).then_inc(s["z_done"], 1)

            def queries(c):
                if c:
                    pe.wait_ge(s["z_read"], c + 1)
                halves(PS[0:HALF, Q_BANK[c], :], [Wq[:, i, :] for i in range(2)], columns(c)).then_inc(s["q_done"], 1)

            def keys(c):
                halves(PS[0:HALF, K_BANK[c], :], [Wk[:, i, :] for i in range(2)], columns(c)).then_inc(s["k_done"], 1)

            def gates(c):
                if c:
                    pe.wait_ge(s["qt_done"], c + 1)
                    pe.wait_ge(s["kt_done"], c + 1)
                for m in range(2):
                    last = halves(PS[0:HALF, 4 + m, :], [Wg[:, i, m * HALF:(m + 1) * HALF] for i in range(2)], columns(c))
                last.then_inc(s["g_done"], 1)

            def values_in(c):
                if c:
                    pe.wait_ge(s["o_log"], 2)
                for i in range(B):
                    last = halves(PS[:, 6 + i // 2, (i % 2) * D:(i % 2 + 1) * D],
                                  [xT[c][:, a, i * TS:(i + 1) * TS] for a in range(2)], [Wv[:, a, :] for a in range(2)])
                    if i % 2:
                        last.then_inc(s["v_done"], 1)

            def linear_attention(c, between):
                pe.wait_ge(s["qt_done"], c + 1)
                pe.wait_ge(s["kt_done"], c + 1)
                pe.wait_ge(s["Sin_done"], c + 1)
                first = [True, True]
                for i in range(B):
                    for m in range(2):
                        pe.matmul(PS[0:HALF, 1 + m, i * TS:(i + 1) * TS], Sc[:, c, i, m * HALF:(m + 1) * HALF],
                                  qt[:, c, i * TS:(i + 1) * TS], start=first[m], stop=False, skip_group_check=True)
                        first[m] = False
                pe.wait_ge(s["z_read"], c + 1)
                pe.wait_ge(s["v_evac"], B * (c + 1))
                if c:
                    pe.wait_ge(s["h1_done"], 3)

                def scores(n):
                    g = n - NG * c
                    i, hg = g // 3, g % 3
                    pe.wait_ge(s["qm_done"], H * c + 4 * hg + 4)
                    if g >= 4:
                        pe.wait_ge(s["A_done"], n - 3)
                    pe.matmul(PS[:, SC_BANKS[n % 4], :], kt[:, c, i * TS:(i + 1) * TS],
                              qm[:, 4 * hg:4 * hg + 4, i * TS:(i + 1) * TS], start=True, stop=True).then_inc(s["sc_done"], 1)

                def values(n):
                    g = n - NG * c
                    i, hg = g // 3, g % 3
                    pe.wait_ge(s["A_done"], n + 1)
                    for a in (0, 2, 1, 3):
                        hd = 4 * hg + a
                        pair = hd // 2
                        row = 32 * (pair % 3)
                        last = pe.matmul(PS[row:row + 32, 1 + pair // 3, i * TS:(i + 1) * TS], Vp[:, c, i, hd, :], A[:, n % 4, a, :],
                                         start=False, stop=False, skip_group_check=True)
                    last.then_inc(s["av_done"], 1)

                for g in range(NG + 2):
                    if g < NG:
                        scores(NG * c + g)
                    if g >= 2:
                        values(NG * c + g - 2)
                    if g in between:
                        between[g]()

            def out_projection(c):
                pe.wait_ge(s["y_done"], 1 + c + 1)
                if c == 0:
                    pe.wait_ge(s["S1_done"], B)
                for i in range(B):
                    last = halves(PS[:, (0, 3)[i // 2], (i % 2) * D:(i % 2 + 1) * D],
                                  [yT[c][:, a, i * TS:(i + 1) * TS] for a in range(2)], [Wo[:, a, :] for a in range(2)])
                    if i % 2:
                        last.then_inc(s["wo_done"], 1)

            def input_features(c):
                pe.wait_ge(s["xh_done"], 4 + c + 1)
                if c == 0:
                    pe.wait_ge(s["g_read"], 3)
                else:
                    pe.wait_ge(s["wT_evac"], 1)
                    pe.wait_ge(s["cls_cols"], 1)
                for half in range(2):
                    for i in range(B):
                        last = pe.transpose(PS[0:HALF, 4 + half, i * TS:(i + 1) * TS],
                                            xh[4 + c][:, i, half * HALF:(half + 1) * HALF], ident)
                last.then_inc(s["xh_T"], 1)

            def gates_and_downs(c):
                pe.wait_ge(s["xT_evac_a"], 2 + c + 1)
                pe.wait_ge(s["xT2_evac"], 1 + c + 1)
                pe.wait_ge(s["weights_c"], 32)
                for i in range(B):
                    last = halves(PS[:, 4 + i // 2, (i % 2) * GW:(i % 2 + 1) * GW],
                                  [xT2[:, a, i, 1 + c * TS:1 + (c + 1) * TS] for a in range(2)], [W_ga[:, a, :] for a in range(2)])
                if c == 0:
                    last = halves(PS[:, 5, 2 * GW:3 * GW], [x2_cls[:, a, :] for a in range(2)], [W_ga[:, a, :] for a in range(2)])
                last.then_inc(s["ga_done"], 1)

            def weighted_downs(c):
                pe.wait_ge(s["aw_done"], c + 1)
                for i in range(B):
                    last = pe.transpose(PS[:, 4, i * TS:(i + 1) * TS], aw[:, i, :], ident)
                if c == 0:
                    last = pe.transpose(PS[:, 5, 0:TS], aw[:, B, :], ident)
                last.then_inc(s["aw_T"], 1)

            patches(0)
            tokens(0)
            pe.wait_ge(s["xh_done"], 2)
            for half in range(2):
                last = pe.transpose(PS[0:HALF, 2, half * 128:(half + 1) * 128], xh[1][:, 0, half * HALF:(half + 1) * HALF], ident)
            last.then_inc(s["cls_T"], 1)
            features(0)
            decay_inputs(0)
            queries(0)
            pe.wait_ge(s["xT2_evac"], 1)
            keys(0)
            gates(0)
            values_in(0)
            linear_attention(0, {1: lambda: patches(1), 3: lambda: tokens(1), 7: lambda: features(1),
                                 9: lambda: (decay_inputs(1), keys(1)), 11: lambda: queries(1)})
            pe.wait_ge(s["A_done"], NG)
            for i in range(B):
                last = pe.transpose(PS[:, 0, i * HALF:(i + 1) * HALF], kt[:, 0, i * TS:(i + 1) * TS], ident96)
            last.then_inc(s["kT_done"], 1)
            pe.wait_ge(s["kT_evac"], 1)
            for i in range(B):
                last = pe.matmul(PS[0:HALF, (3, 0)[i // 2], (i % 2) * D:(i % 2 + 1) * D], ktok[:, i, :], padded(Vp[:, 0, i]),
                                 start=True, stop=True)
                if i % 2:
                    last.then_inc(s["kv_done"], 1)
            mean_squares(0)
            gates(1)
            values_in(1)
            out_projection(0)
            linear_attention(1, {5: lambda: input_features(0), 8: lambda: gates_and_downs(0)})
            pe.wait_ge(s["A_done"], 2 * NG)
            mean_squares(1)
            weighted_downs(0)
            out_projection(1)
            input_features(1)
            gates_and_downs(1)
            weighted_downs(1)
            pe.wait_ge(s["wT_evac"], 2)
            pe.wait_ge(s["pads_zero"], 3)
            pe.wait_ge(s["o_log"], 3)

            at = [0]

            def work(i, key):
                n = at[0]
                at[0] += 1
                assert WORK[n] == (i, key)
                if n >= 2:
                    if WORK[n - 2][1][0] == "den":
                        pe.wait_ge(s["den_log"], dens(n - 2))
                    else:
                        pe.wait_ge(s["work_free"], freed(n - 2))
                ps = PS[:, 6 + n % 2, :]
                kind = key[0]
                if kind == "qk":
                    m = key[1]
                    for half in range(2):
                        pe.matmul(ps[0:HALF, 0:T], W_qk[:, half, m * HALF:(m + 1) * HALF], xT2[:, half, i, :],
                                  start=(half == 0), stop=False)
                    last = pe.matmul(ps[0:HALF, 0:T], B_qk[:, m * HALF:(m + 1) * HALF], wT[:, i, :], start=False, stop=True)
                elif kind == "vc":
                    for half in range(2):
                        pe.matmul(ps[0:H, 0:D], x2_cls[:, half, 0:H], W_v[:, half, :], start=(half == 0), stop=False)
                    last = pe.matmul(ps[0:H, 0:D], w_rep[:, :], B_v, start=False, stop=True)
                elif kind == "v":
                    for c in range(NC):
                        cols = slice(1 + c * TS, 1 + (c + 1) * TS)
                        for half in range(2):
                            pe.matmul(ps[:, c * D:(c + 1) * D], xT2[:, half, i, cols], W_v[:, half, :], start=(half == 0), stop=False)
                        last = pe.matmul(ps[:, c * D:(c + 1) * D], wT[:, i, cols], B_v, start=False, stop=True)
                elif kind in ("cq", "ck"):
                    if kind == "cq" and i == 0:
                        pe.wait_ge(s["cls_qk_done"], 1)
                    if kind == "cq":
                        pe.wait_ge(s["bounced_out"], i + 1)
                    side = 0 if kind == "cq" else 1
                    steps = [(a, b, half) for a, b in ((0, 0), (0, 1), (1, 0)) for half in range(2)]
                    for n_, (a, b, half) in enumerate(steps):
                        t = (qk_hi, qk_lo)[b]
                        last = pe.matmul(ps[0:H, 0:T], cls_qk[:, side, a, half, :], t[:, i % 2, 2 * (1 - side) + half, :],
                                         start=(n_ == 0), stop=(n_ == len(steps) - 1))
                elif kind == "max":
                    c, hd = key[1:]
                    if c == 0 and hd == 0:
                        pe.wait_ge(s["stacked"], 128 * (i + 1))
                        pe.wait_ge(s["rows_zero"], 1)
                        pe.wait_ge(s["ones_stacked"], 16)
                    last = pe.matmul(ps[:, 0:T], stack[:, i, 0, hd, 1 + c * TS:1 + (c + 1) * TS], stack[:, i, 1, hd, :],
                                     start=True, stop=True)
                elif kind == "mT":
                    pe.wait_ge(s["work_free"], freed(work_index(i, ("max", NC - 1, H - 1))))
                    for c in range(NC):
                        last = pe.transpose(ps[0:H, c * TS:(c + 1) * TS], mx[:, i % 2, c, :], ident)
                elif kind == "cs":
                    pe.wait_ge(s["neg_m_stacked"], 16 * (i + 1))
                    pe.wait_ge(s["ones_stacked"], 16)
                    for hd in range(H):
                        for c in range(NC):
                            last = pe.matmul(ps[:, NC * hd + c:NC * hd + c + 1], stack[:, i, 1, hd, 1 + c * TS:1 + (c + 1) * TS],
                                             stack[:, i, 0, hd, 0:1], start=True, stop=True)
                elif kind == "den":
                    pe.wait_ge(s["raw_done"], BANKS * i + key[1] + 1)
                    last = pe.matmul(ps[:, 0:T], den_rows, raw[:, key[1], :], start=True, stop=True)
                elif kind == "proj":
                    for b in range(BANKS):
                        pe.wait_ge(s["oT_done"], BANKS * i + b + 1)
                        for c in range(NC):
                            last = pe.matmul(ps[:, c * D:(c + 1) * D], oT[:, i % 2, b, 1 + c * TS:1 + (c + 1) * TS], W_proj[:, b, :],
                                             start=(b == 0 and c == 0), stop=(b == BANKS - 1), skip_group_check=True)
                elif kind == "pc":
                    for b in range(BANKS):
                        last = pe.matmul(ps[0:B, 0:D], oT_cls[:, b, :], W_proj[:, b, :], start=(b == 0), stop=(b == BANKS - 1))
                last.then_inc(s["work_full"], 1)

            def key_scores(n):
                i, hd = n // H, n % H
                if n >= 3:
                    pe.wait_ge(s["p_done"], n - 2)
                for c in range(NC):
                    last = pe.matmul(PS[:, n % 3, c * NTOK:(c + 1) * NTOK], stack[:, i, 1, hd, 1 + c * TS:1 + (c + 1) * TS],
                                     stack[:, i, 0, hd, 1:T], start=True, stop=True)
                last.then_inc(s["sT_done"], 1)

            def weighted_values(i, b):
                first = H * i + 4 * b
                if i:
                    pe.wait_ge(s["raw_done"], BANKS * (i - 1) + b + 1)
                pe.wait_ge(s["p_cls_done"], i + 1)
                pe.matmul(PS[:, 3 + b, 0:T], v_cls[:, 4 * b:4 * b + 4, :], p_cls[:, i % 2, :], start=True, stop=False,
                          skip_group_check=True)
                for c in range(NC):
                    for a in range(4):
                        n = first + a
                        if c == 0:
                            pe.wait_ge(s["p_done"], n + 1)
                            pe.wait_ge(s["p_col_done"], n + 1)
                        last = pe.matmul(PS[32 * a:32 * a + 32, 3 + b, 0:T], v2[:, i % 2, c, 4 * b + a, :], pT[:, n % SLOTS, c, :],
                                         start=False, stop=False, skip_group_check=True)
                        if c == NC - 1:
                            last.then_inc(s["pv_done"], 1)

            for j, key in START:
                work(j, key)
            for g in range(STEPS):
                if g < PAIRS:
                    key_scores(g)
                for j, key in USES[g]:
                    work(j, key)
                if 0 <= g - LAG < PAIRS and (g - LAG) % 4 == 3:
                    weighted_values((g - LAG) // H, (g - LAG) % H // 4)


def interpolation(length, n_out):
    pos = (np.arange(n_out, dtype=np.float32) + np.float32(0.5)) * np.float32(length / n_out) - np.float32(0.5)
    pos = np.clip(pos, np.float32(0), np.float32(length - 1))
    lo = np.floor(pos).astype(np.int32)
    up = np.minimum(lo + 1, length - 1)
    frac = (pos - lo).astype(np.float32)
    m = np.zeros((length, n_out), np.float32)
    np.add.at(m, (lo, np.arange(n_out)), np.float32(1) - frac)
    np.add.at(m, (up, np.arange(n_out)), frac)
    return m

def kernel(**inputs):
    import concourse.bacc as bacc
    from concourse.bass_utils import run_bass_kernel_spmd

    a = {k.replace("L0_", ""): np.asarray(v) for k, v in inputs.items()}
    x = a["x"]
    f32 = np.float32

    def patches(p):
        n = IMG // p
        return np.ascontiguousarray(x.reshape(B, CH, n, p, n, p).transpose(2, 4, 0, 3, 5, 1).reshape(n * n, B * p * p * CH))

    index = np.concatenate([
        a["tok_idx2"].reshape(NT2, 2, 8).transpose(2, 0, 1).reshape(128, 2),
        a["tok_idx1"].reshape(NT1, 2, 8).transpose(1, 0, 2).reshape(128, 8),
        a["tok_idx0"].reshape(NC, TS, GP).transpose(1, 0, 2).reshape(128, NC * GP)], axis=1)

    def split(m):
        return m.reshape(2, HALF, -1).transpose(1, 0, 2).reshape(HALF, -1)

    def rows(v, n):
        return np.broadcast_to(v.reshape(1, -1), (n, v.size))

    i1, i2 = interpolation(NT1, NTOK), interpolation(NT2, NTOK)
    interp1 = np.zeros((2, NT1, 2, NC, TS), f32)
    for p in range(2):
        interp1[p, :, p] = i1.reshape(NT1, NC, TS)
    interp2 = np.zeros((B, NT2, B, NC, TS), f32)
    for p in range(B):
        interp2[p, :, p] = i2.reshape(NT2, NC, TS)
    W0 = np.zeros((E, 2, 2, 48), f32)
    for p in range(2):
        W0[:, p, p] = a["tok_W0"]
    WfT = a["tok_Wf"].T
    heads96 = np.arange(HALF) // HD
    den_rows = np.zeros((4, 32, 4, 32), f32)
    den_rows[np.arange(4), 0, np.arange(4), :] = 1
    W_proj = np.zeros((4, 32, BANKS, D), f32)
    W_proj[:, 1:1 + HD] = a["ffn_W_proj"].T.reshape(BANKS, 4, HD, D).transpose(1, 2, 0, 3)
    cls_heads = np.zeros((HALF, 2, H), f32)
    to_heads = np.zeros((H, 2, HALF), f32)
    for half in range(2):
        cls_heads[np.arange(HALF), half, half * HH + heads96] = 1
        to_heads[half * HH + heads96, half, np.arange(HALF)] = 1
    restart = np.ones((HALF, B, TS), f32)
    restart[:, :, 0] = 0
    lora_up = a["ffn_B_lora"].transpose(0, 2, 1).reshape(NR, 3 * D)
    W_qkvT = a["ffn_W_qkv"].T
    parts = {
        "ident": np.eye(128, dtype=f32), "cls": rows(a["cls_tok"], 128), "interp1": interp1.reshape(128, -1),
        "causal": np.triu(np.ones((TS, TS), f32)), "eps": np.full((128, 1), EPS, f32), "b_gate": rows(a["ffn_b_gate"], 128),
        "tie": rows(np.arange(NEXP, 0, -1).astype(f32), 128), "b_proj": rows(a["ffn_b_proj"], 128),
        "b_v": rows(a["ffn_b_qkv"][2 * D:], 128), "B_qk": lora_up[:, 0:2 * D], "B_v": lora_up[:, 2 * D:],
        "den_rows": den_rows.reshape(128, -1), "W_proj": W_proj.reshape(128, -1),
        "Wq": split(a["attn_Wq"]), "Wk": split(a["attn_Wk"]), "Wv": split(a["attn_Wv"]), "Wg": split(a["attn_Wg"]),
        "b_gk": a["attn_bgk2"].reshape(HALF, 1), "o_norm": np.tile(a["attn_o_norm_w"], HH).reshape(HALF, 1),
        "blockdiag": (np.arange(HALF)[:, None] // HK == np.arange(D)[None] // HV).astype(f32),
        "headcol": (np.arange(HALF)[:, None] // HK == np.arange(H)[None]).astype(f32),
        "head_mean": (heads96[:, None] == heads96[None]).astype(f32) / f32(HV), "restart": restart.reshape(HALF, -1),
        "Wo": split(a["attn_Wo"]),
        "W_ga": split(np.concatenate([a["ffn_W_gate"].T, a["ffn_A"].reshape(NR, D).T], axis=1)),
        "W_qk": split(W_qkvT[:, 0:2 * D]), "W_v": split(W_qkvT[:, 2 * D:]), "b_qk": a["ffn_b_qkv"][0:2 * D].reshape(4, HALF).T,
        "cls_heads": cls_heads.reshape(HALF, -1),
        "b0": np.broadcast_to(a["tok_b0"][:, None], (E, 128)), "b1": np.broadcast_to(a["tok_b1"][:, None], (E, 128)),
        "b2": np.concatenate([np.broadcast_to(a["tok_b2"][:, None], (E, 128)), np.ones((1, 128), f32)]),
        "Wf0": WfT[0:E], "Wf1": WfT[E:2 * E], "Wf2": np.concatenate([WfT[2 * E:], a["tok_bf"].reshape(1, D)]),
        "W0": W0.reshape(E, -1), "W1": a["tok_W1"],
        "W2": a["tok_W2"].reshape(E, 2, 8, 48).transpose(0, 2, 1, 3).reshape(E, -1),
        "Wgk1": a["attn_Wgk1"].T, "Wgk2": a["attn_Wgk2"], "interp2": interp2.reshape(E, -1), "to_heads": to_heads.reshape(H, -1),
    }
    arrays = {"pix0": patches(1), "pix1": patches(2), "pix2": patches(4), "index": np.ascontiguousarray(index),
              "ones": np.ones((1, B, H, T), np.float16)}
    for p, blocks in PACKS.items():
        at, n = offsets(p)
        packed = np.zeros((ROWS[p], n), f32)
        for name, cols in blocks:
            m = parts[name]
            packed[0:m.shape[0], at[name][0]:at[name][0] + cols] = m
        arrays[p] = packed

    nc = bacc.Bacc("TRN2", target_bir_lowering=False, num_devices=1)
    args = [nc.dram_tensor("in_" + n, v.shape, mybir.dt.from_np(v.dtype), kind="ExternalInput").ap() for n, v in arrays.items()]
    out = nc.dram_tensor("out_0", (B, T, D), F32, kind="ExternalOutput").ap()
    build(nc, *args, out)
    r = run_bass_kernel_spmd(nc, [{"in_" + n: v for n, v in arrays.items()}], core_ids=[0])
    return r.results[0]["out_0"]
```

```python
from contextlib import ExitStack

import numpy as np

import concourse.bass as bass
from concourse import mybir

F32 = mybir.dt.float32
F16 = mybir.dt.float16
I32 = mybir.dt.int32
U32 = mybir.dt.uint32
ALU = mybir.AluOpType
ACT = mybir.ActivationFunctionType
AX = mybir.AxisListType

B, IMG, CH = 4, 64, 3
D, H = 192, 12
HALF = D // 2
HK, HV = D // 2 // H, D // H
HD = D // H
E = 64
GP = 16
NTOK = IMG * IMG // GP
TS = 128
NC = NTOK // TS
T = NTOK + 1
NT1, NT2 = NTOK // 4, NTOK // 16
NEXP, RANK = 8, 16
NR = NEXP * RANK
CW = B * TS
PW = 2 * TS
BANK = 512
EPS = 1e-5
GATE_NORM = 16.0
Q_SCALE = float(HK) ** -0.5
ATT_SCALE = float(HD) ** -0.5
LORA_SCALE = 32.0 / RANK
HH = H // 2

PACKS = {
    "p128": [("ident", 128), ("cls", D), ("eps", 1), ("interp1", 2 * NC * TS), ("causal", TS),
             ("b_gate", NEXP), ("tie", NEXP), ("b_proj", D), ("b_v", D), ("B_qk", 2 * D), ("B_v", D), ("den_rows", TS), ("W_proj", H // 4 * D)],
    "p96": [("Wq", 2 * HALF), ("Wk", 2 * HALF), ("Wv", 2 * D), ("Wg", 2 * D), ("b_gk", 1), ("o_norm", 1),
            ("blockdiag", D), ("in_group", 4), ("group", 3), ("head_mean", HALF), ("restart", CW), ("Wo", 2 * D),
            ("W_ga", 2 * (NEXP + NR)), ("W_qk", 2 * 2 * D), ("W_v", 2 * D), ("b_qk", 4),
            ("cls_heads", 2 * H)],
    "p65": [("b0", 128), ("b1", 128), ("b2", 128), ("Wf0", D), ("Wf1", D), ("Wf2", D), ("W0", 4 * 48),
            ("W1", 2 * HALF), ("W2", 8 * HALF), ("Wgk1", D), ("Wgk2", HALF), ("interp2", B * NC * TS),
            ("to_heads", D)],
}
ROWS = {"p128": 128, "p96": 96, "p65": 65}


def offsets(pack):
    at, n = {}, 0
    for name, cols in PACKS[pack]:
        at[name] = (n, cols)
        n += cols
    return at, n

PAIRS = B * H
LAG = 2
SLOTS = 8
BANKS = H // 4
STEPS = PAIRS + 5
START = []
FIRST = 7
ROUTE, TURNED = 5, 9
USES = [[] for _ in range(STEPS)]
RAWS = [[] for _ in range(STEPS)]
DIVIDES = [[] for _ in range(STEPS)]


def plan():
    for i in range(B):
        qk = [(i, ("qk", m)) for m in range(4)]
        maxima = [(i, ("max", c, hd)) for hd in range(H) for c in range(NC)]
        last = [(i, ("mT",)), (i, ("ck",)), (i, ("cs",))]
        first = H * (i - 1)
        if i == 0:
            START.extend(qk + [(0, ("vc",)), (0, ("v",)), (0, ("cq",)), (1, ("qk", 0)), (1, ("qk", 1))] + maxima[0:8]
                         + [(1, ("qk", 2))] + maxima[8:12] + [(1, ("qk", 3))] + maxima[12:16] + [(1, ("cq",))] + maxima[16:] + last)
        else:
            if i > 1:
                for k, use in enumerate(qk + [(i, ("cq",))]):
                    USES[first - 10 + k // 2].append(use)
            begin, steps = (first, 9) if i == 1 else (first - 2, 10)
            for k, use in enumerate(maxima):
                USES[begin + k * steps // len(maxima)].append(use)
            USES[first + 4].append((i, ("v",)))
            for k, use in enumerate(last):
                USES[begin + steps + (0, 1, 2 if i == 1 else 3)[k]].append(use)
        for b in range(BANKS):
            done = H * i + 4 * b + 3 + LAG + 1
            late = i == B - 1 and b == BANKS - 1
            RAWS[done].append((i, b))
            USES[done + (0 if late else 1)].insert(0, (i, ("den", b)))
            DIVIDES[done + (1 if late else 2)].append((i, b))
        USES[H * i + H + LAG + (1 if i == B - 1 else 3)].insert(0, (i, ("proj",)))
    USES[STEPS - 1].append((B - 1, ("pc",)))


plan()
WORK = START + [use for uses in USES for use in uses]


def work_index(i, key):
    return WORK.index((i, key))


def bank_of(n):
    if n < FIRST:
        return 6 + n % 2
    if n < len(START) - 3:
        return 2 + (n - FIRST) % 6
    return (2, 6, 7)[n % 3]


def former(n):
    return max((m for m in range(n) if bank_of(m) == bank_of(n)), default=None)


def work_bank(i, key):
    return bank_of(work_index(i, key))


def freed(n):
    return sum(key[0] != "den" for _, key in WORK[:n + 1])


def dens(n):
    return sum(key[0] == "den" for _, key in WORK[:n + 1])


def build(nc, pix0, pix1, pix2, index, ones, p128, p96, p65, out):
    n_cols = {p: offsets(p)[1] for p in PACKS}
    with ExitStack() as ctx:
        def sb(name, shape, dt=F32):
            return ctx.enter_context(nc.sbuf_tensor(name, shape, dt))

        packed = {p: sb(p + "_sb", [ROWS[p], n_cols[p]]) for p in PACKS}

        def w(pack, name, rows=None):
            a, n = offsets(pack)[0][name]
            return packed[pack][0:rows or ROWS[pack], a:a + n]

        def halved(t):
            return t.bitcast(F16).rearrange("p (a n) -> p a n", a=2)

        ident = w("p128", "ident")
        ident96 = ident[0:HALF, 0:HALF]
        cls_rows = w("p128", "cls")
        interp1 = w("p128", "interp1").rearrange("p (a c t) -> p a c t", a=2, c=NC)
        causal = w("p128", "causal")
        eps = w("p128", "eps")
        b_gate = w("p128", "b_gate")
        tie = w("p128", "tie")
        b_proj = w("p128", "b_proj")
        B_qk = w("p128", "B_qk")
        B_v = w("p128", "B_v")
        den_rows = w("p128", "den_rows")
        W_proj = w("p128", "W_proj").rearrange("p (i n) -> p i n", i=BANKS)
        Wq = w("p96", "Wq").rearrange("p (i n) -> p i n", i=2)
        Wk = w("p96", "Wk").rearrange("p (i n) -> p i n", i=2)
        Wv = w("p96", "Wv").rearrange("p (i n) -> p i n", i=2)
        Wg = w("p96", "Wg").rearrange("p (i n) -> p i n", i=2)
        qkvg = packed["p96"][:, 0:6 * D]
        b_gk = w("p96", "b_gk")
        o_norm = w("p96", "o_norm")
        blockdiag = w("p96", "blockdiag")
        in_group = w("p96", "in_group")
        group = w("p96", "group")
        head_mean = w("p96", "head_mean")
        restart = w("p96", "restart")
        Wo = w("p96", "Wo").rearrange("p (i n) -> p i n", i=2)
        W_ga = w("p96", "W_ga")
        at_qk = offsets("p96")[0]["W_qk"][0]
        W_qkv = packed["p96"][:, at_qk:at_qk + 6 * D]
        b_qk = w("p96", "b_qk")
        b_v = w("p128", "b_v")
        cls_heads = w("p96", "cls_heads").rearrange("p (i n) -> p i n", i=2)
        b_rep = [w("p65", f"b{i}", 65 if i == 2 else E) for i in range(3)]
        Wf = [w("p65", f"Wf{i}", 65 if i == 2 else E) for i in range(3)]
        W0 = w("p65", "W0", E).rearrange("p (i n) -> p i n", i=2)
        W1 = w("p65", "W1", E).rearrange("p (i n) -> p i n", i=2)
        W2 = w("p65", "W2", E).rearrange("p (i n) -> p i n", i=8)
        Wgk1 = w("p65", "Wgk1", 16).rearrange("p (i n) -> p i n", i=2)
        Wgk2 = w("p65", "Wgk2", 16)
        interp2 = w("p65", "interp2", E).rearrange("p (b c t) -> p b c t", b=B, c=NC)
        to_heads = w("p65", "to_heads", H)

        idx = sb("idx", [128, 2 + 8 + NC * GP], I32)
        G2 = sb("G2", [128, 2, B * 48])
        G1 = sb("G1", [128, 8, B * 12])
        G0 = sb("G0", [128, NC, GP, B * CH])
        Gp = sb("Gp", [128, 6 * D])
        G0p = Gp[:, 0:2 * D].rearrange("p (c b j d) -> p c b j d", c=NC, b=B, j=GP)
        G1p = Gp[:, 2 * D:4 * D].rearrange("p (b k d) -> p b k d", b=B, k=8)
        G2p = Gp[:, 4 * D:6 * D].rearrange("p (b k d) -> p b k d", b=B, k=2)
        wT = halved(Gp[:, 0:B * T]).rearrange("p a (b t) -> p a b t", b=B)
        M = sb("M", [HALF, 12, D])
        xT2 = halved(M[:, :, :].rearrange("p a n -> p (a n)")[:, 0:2 * B * T]).rearrange("p a (i b t) -> p a i b t", i=2, b=B)
        bias_h = sb("bias_h", [128, D])
        T2t = sb("T2t", [HALF, 8, B, NT2])
        T1t = sb("T1t", [HALF, 2, B, NT1])
        Z1 = sb("Z1", [128, 2, D])
        Z2 = sb("Z2", [E, D])
        T0t = sb("T0t", [HALF, NC, 2, TS])
        h = sb("h", [128, NC, B, D])
        h1 = sb("h1", [128, NC, B, D])
        h1_cls = sb("h1_cls", [128, D])
        LN = (0, 1, 2, 6, 10, 14, 16, 18)
        stats = sb("stats", [128, LN[-1], 6])
        moments = sb("moments", [128, LN[-1], 2])
        ln_var = sb("ln_var", [128, LN[-1]])
        rstd = sb("rstd", [128, LN[-1]])
        xh_tiles = sb("xh_tiles", [128, 2 + NC * B, D])
        xh = [xh_tiles[:, 0:1, :], xh_tiles[:, 1:2, :]] + [
            xh_tiles[:, a:b, :] for a, b in ((2, 6), (6, 10), (2, 6), (6, 8), (8, 10))]
        xT_cls = sb("xT_cls", [HALF, 2, 128])
        xT = [halved(sb("xT", [HALF, 2 * CW])[:, :]), halved(M[:, :, :].rearrange("p a n -> p (a n)")[:, 0:2 * CW])]
        xT = [t.rearrange("p a (i n) -> p a i n", i=2) for t in xT]
        q_cls = sb("q_cls", [HALF, 8])
        S0 = sb("S0", [HALF, D])
        shared = sb("shared", [128, 7 * CW + 4 * CW + 7 * (2 * CW + 8)])
        place = [0]

        def early(shape):
            n = int(np.prod(shape[1:]))
            t = shared[0:shape[0], place[0]:place[0] + n]
            place[0] += n
            return t

        late_place = [0]

        def late(shape, dt=F32):
            n = int(np.prod(shape[1:]))
            words = n if dt == F32 else n // 2
            t = shared[0:shape[0], late_place[0]:late_place[0] + words]
            late_place[0] += words
            return t if dt == F32 else t.bitcast(dt)

        zm = early([HALF, CW])
        za = early([HALF, CW])
        zl = early([HALF, CW])
        Gs = early([HALF, CW])
        Gc = early([HALF, CW])
        Eq = early([HALF, CW])
        Ek = early([HALF, CW])
        decay = sb("decay", [HALF, NC, 3, B])
        qt = early([HALF, NC * CW]).rearrange("p (c n) -> p c n", c=NC)
        kt = early([HALF, NC * CW]).rearrange("p (c n) -> p c n", c=NC)
        arena = sb("arena", [128, B * 2 * H * T // 2])
        qm = arena[0:HALF, 0:4 * CW].rearrange("p (a c) -> p a c", a=4)
        km = arena[0:HALF, 4 * CW:7 * CW].rearrange("p (a c) -> p a c", a=3)
        Vp = arena[:, H * CW:H * CW + NC * B * H * 32].rearrange("p (c b h e) -> p c b h e", c=NC, b=B, h=H)
        A = arena[:, H * CW + NC * B * H * 32:H * CW + NC * B * H * 32 + 16 * TS].rearrange("p (n h t) -> p n h t", n=4, h=4)
        free = (4 + 3) * CW
        Wgk_parts = halved(arena[0:HALF, free:free + D]).rearrange("p a (i n) -> p a i n", i=2)
        qkvg_parts = halved(arena[0:HALF, free + D:free + 7 * D])

        def gla_weights(name):
            at, n = offsets("p96")[0][name]
            return qkvg_parts[:, :, at:at + n].rearrange("p a (i n) -> p a i n", i=2)

        stack = arena[:, :].bitcast(F16).rearrange("p (b s h t) -> p b s h t", b=B, s=2, h=H)
        Sc = sb("Sc", [HALF, NC, B, D])
        S1 = sb("S1", [HALF, B, D])
        ktok = sb("ktok", [128, B, HALF])
        ga_parts = halved(T0t[:, :, :, :].rearrange("p c a t -> p (c a t)")[:, 0:2 * (NEXP + NR)])
        W_ga_parts = ga_parts.rearrange("p a (i n) -> p a i n", i=2)
        qkv_parts = halved(Sc[:, :, :, :].rearrange("p c b n -> p (c b n)")[:, 0:6 * D])
        W_qk_parts = qkv_parts[:, :, 0:4 * D].rearrange("p a (i n) -> p a i n", i=2)
        W_v_parts = qkv_parts[:, :, 4 * D:6 * D].rearrange("p a (i n) -> p a i n", i=2)
        B_qk_parts = halved(ktok[:, :, :].rearrange("p b n -> p (b n)"))
        B_v_parts = halved(Z1[:, :, :].rearrange("p a n -> p (a n)")[:, 0:D])
        NORMW = 2 * CW + 2 * 4
        def norm_buf():
            t = early([HALF, NORMW])
            return [t[:, 0:2 * CW].rearrange("p (i n) -> p i n", i=2)] * NC + [t[:, 2 * CW:NORMW].rearrange("p (i n) -> p i n", i=2)]

        g_log, g_abs, g_raw, g_w, o_sq, o_ln, yT = (norm_buf() for _ in range(7))
        GW = NEXP + NR
        UNITS = ((0, (0, 1, 2, 3), 0, (4, 5)), (1, (0, 1), B + 1, (4, 5)), (1, (2, 3), B + 3, (0, 1)))
        NU = B + 5
        logits = sb("logits", [128, NU, NEXP])
        pr = sb("pr", [128, 6, NU, NEXP])
        sm = sb("sm", [128, 8, NU])
        disp = sb("disp", [128, NU, NEXP])
        aw = late([128, B + 1, NR]).rearrange("p (b n) -> p b n", b=B + 1)
        x2_cls = halved(xT_cls[:, :, :].rearrange("p i n -> p (i n)")).rearrange("p a (i n) -> p a i n", i=2)
        qk_hi = late([HALF, 2, 4, T], F16).rearrange("p (a m t) -> p a m t", a=2, m=4)
        qk_lo = late([HALF, 2, 4, T], F16).rearrange("p (a m t) -> p a m t", a=2, m=4)
        cls_qk = sb("cls_qk", [HALF, 2, 2, 2, H], F16)
        w_rep = sb("w_rep", [NR, 2, H], F16)
        v2 = late([128, 2, 2, H, 32]).rearrange("p (a c h e) -> p a c h e", a=2, c=2, h=H)
        v_cls = late([H, H * 32]).rearrange("p (h e) -> p h e", h=H)
        v_cls_parts = late([HALF, H * 32], F16).rearrange("p (h e) -> p h e", h=H)
        mx = sb("mx", [128, 2, 2, H])
        mx_cls = sb("mx_cls", [H, 2])
        neg_m = T1t[0:H].rearrange("p a b n -> p (a b n)")[:, 0:T].bitcast(F16).rearrange("p (a t) -> p a t", a=2)
        pT = late([128, SLOTS, 2, T]).rearrange("p (n c t) -> p n c t", n=SLOTS, c=2)
        p_cls = late([HALF, 2, T], F16).rearrange("p (a t) -> p a t", a=2)
        s_clsk = late([H, T])
        s_clsq = late([128, 2 * H * NC]).rearrange("p (a h c) -> p a h c", a=2, h=H)
        p_clsq = late([128, 2 * H * NC]).rearrange("p (a h c) -> p a h c", a=2, h=H)
        raw = late([128, BANKS, T]).rearrange("p (a t) -> p a t", a=BANKS)
        den_r = late([128, 2, T]).rearrange("p (a t) -> p a t", a=2)
        oT = late([128, 2, BANKS, T]).rearrange("p (b a t) -> p b a t", b=2, a=BANKS)
        oT_cls = late([128, BANKS * B]).rearrange("p (a b) -> p a b", a=BANKS)
        res = h1
        res_cls = G2[0:B, 0, :]
        fin = h
        fin_cls = G2[0:B, 1, :]
        PS = ctx.enter_context(nc.psum_tensor("PS", [128, 8, BANK], F32))
        bounce = nc.dram_tensor("bounce", (B, 2, 4 * HALF, T), F16, kind="Internal").ap()

        NAMES = (
            "pool_chain first_zeros v2_padded cls_padded weights_a weights_b weights_c idx_loaded gathered_coarse gathered0 gathered1 dve_chain act_chain "
            "cls_cols pads_zero perm_done moments_done rstd_done xh_done cls_T xT_cls_evac bias_done bias_evac M_done "
            "M_evac Wgk_done Wgk_evac cls_proj S0_done o_cls g_read g_log g_logsig o_square "
            "ms_done o_log weight_log weight y_done wo_done h1_done coarse_T T2_evac T1_evac Z_done Z1_evac Z2_evac "
            "T0_done T0_evac h_mm h_evac xh_T xT_hi xT_lo x2_cls_done x2_hi x2_lo wT_hi wT_lo qkvg_hi qkvg_lo weight_parts z_done z_abs z_read z_log Gc_done decays "
            "q_done k_done qt_done kt_done qm_done km_done v_done v_evac Sin_done sc_done A_done av_done kT_done kT_evac "
            "kv_done S1_done g_done ga_done logits_sub logits_exp aw_done aw_T "
            "work_full work_free qk_hi_done bounced_out bounced_hi bounced_lo stacked cls_qk_done sT_done p_done "
            "pv_done raw_done den_log den_rec p_cls_in p_cls_hi p_cls_done v_cls_done s_clsq_in p_clsq_done p_col_done neg_m_done neg_m_stacked "
            "ones_stacked rows_zero oT_done res_done fin_done stored"
        ).split()
        s = {n: ctx.enter_context(nc.semaphore(n)) for n in NAMES}
        block = ctx.enter_context(nc.Block())

        SC_BANKS = ((0, 3, 6, 7), (0, 3, 6))
        H_BANKS = ((5, 6), (5, 4))
        XT_BANKS = ((7, 0), (4, 5))
        Z_BANK, Q_BANK, K_BANK = (3, 4), (1, 4), (2, 5)
        MS_BANK, WO_BANK = ((6, 7), (7, 6)), ((0, 3), (7, 3))
        NG = B * (H // 4)

        def in_halves(t):
            return t.rearrange("p (i n) -> p i n", i=2)

        CLS = (2, 0)

        def norm_of(c, pair):
            if (c, pair) == CLS:
                return 1, in_halves(PS[0:HALF, 2, 0:8]), in_halves(PS[0:HALF, 3, 0:8]), slice(0, 4)
            return (2 + 2 * c + pair, in_halves(PS[0:HALF, 1 + pair, :]), in_halves(PS[0:HALF, MS_BANK[c][pair], :]),
                    slice(pair * PW, (pair + 1) * PW))

        GATES = {2: in_halves(PS[0:HALF, 4, 0:8]), 0: PS[0:HALF, 4:6, :], 1: PS[0:HALF, 4:6, :]}
        GTURN = {2: 1, 0: 2, 1: 3}

        def padded(t):
            return bass.AP(t.tensor, t.offset, [list(t.ap[0]), [64, H // 2], [48, 2], [1, HV]])

        def heads(t):
            return t.rearrange("p (a e v) -> p a e v", a=H // 2, e=2)

        @block.sync
        def _(sp):
            n128, n96, n65 = (offsets(p)[0] for p in ("p128", "p96", "p65"))
            sp.dma_start(idx[:, :], index).then_inc(s["idx_loaded"], 16)
            a = n128["interp1"][0]
            sp.dma_start(packed["p128"][:, 0:a], p128[:, 0:a]).then_inc(s["weights_a"], 16)
            b = n65["interp2"][0]
            sp.dma_start(packed["p65"][:, 0:b], p65[:, 0:b]).then_inc(s["weights_a"], 16)
            c = n96["W_ga"][0]
            sp.dma_start(packed["p96"][:, 0:c], p96[:, 0:c]).then_inc(s["weights_b"], 16)
            sp.dma_start(packed["p128"][:, a:], p128[:, a:]).then_inc(s["weights_b"], 16)
            sp.dma_start(packed["p65"][:, b:], p65[:, b:]).then_inc(s["weights_c"], 16)
            sp.dma_start(packed["p96"][:, c:], p96[:, c:]).then_inc(s["weights_c"], 16)
            def store(i):
                sp.wait_ge(s["fin_done"], i + 1)
                sp.dma_start(out[i, 1:T, :].rearrange("(c t) n -> t c n", c=NC), fin[:, :, i, :]).then_inc(s["stored"], 16)

            def negated_maxima(i):
                sp.wait_ge(s["neg_m_done"], i + 1)
                sp.dma_start(stack[64:65, i, 0], neg_m[:, i % 2, :]).then_inc(s["neg_m_stacked"], 16)

            sp.wait_ge(s["rows_zero"], 1)
            sp.dma_start(stack[64:65, :, 1], ones).then_inc(s["ones_stacked"], 16)

            for i in range(B):
                for part, t in ((0, qk_hi), (1, qk_lo)):
                    if part == 0:
                        sp.wait_ge(s["qk_hi_done"], 4 * (i + 1))
                    else:
                        sp.wait_ge(s["bounced_out"], i + 1)
                    sp.dma_start(bounce[i, part].rearrange("(m p) c -> p m c", m=4), t[:, i % 2]).then_inc(s[("bounced_hi", "bounced_lo")[part]], 16)
                for part in range(2):
                    sp.wait_ge(s[("bounced_hi", "bounced_lo")[part]], 16 * (i + 1))
                    for side, slots in ((0, ((0, 1), (2, 3))[part]), (1, ((0, 2), (1, 3))[part])):
                        for slot in slots:
                            src = bounce[i, part, side * D:(side + 1) * D, :].rearrange("(h d) c -> d h c", d=HD)
                            sp.dma_start(stack[HD * slot:HD * (slot + 1), i, side], src).then_inc(s["stacked"], 16)
                if i:
                    negated_maxima(i - 1)
            negated_maxima(B - 1)
            for i in range(B - 1):
                store(i)
            store(B - 1)
            sp.wait_ge(s["fin_done"], B + 1)
            sp.dma_start(out[:, 0, :], fin_cls).then_inc(s["stored"], 16)
            sp.wait_ge(s["stored"], 16 * (B + 1))

        @block.gpsimd
        def _(pool):
            pool.wait_ge(s["idx_loaded"], 16)

            def gather(dst, table, col, sem):
                pool.indirect_dma_start(dst, None, table, bass.IndirectOffsetOnAxis(ap=idx[:, col:col + 1].bitcast(U32), axis=0)
                                        ).then_inc(s[sem], 16)

            for k in range(2):
                gather(G2[:, k, :], pix2, k, "gathered_coarse")
            for k in range(8):
                gather(G1[:, k, :], pix1, 2 + k, "gathered_coarse")
            for c in range(NC):
                for j in range(GP):
                    gather(G0[:, c, j, :], pix0, 10 + c * GP + j, f"gathered{c}")
            def masked_keys(c):
                pool.wait_ge(s["kt_done"], c + 1)
                if c:
                    pool.wait_ge(s["sc_done"], NG * c)
                for a in range(3):
                    pool.tensor_scalar(km[:, a, :], kt[:, c, :], group[:, a:a + 1], None, ALU.mult).then_inc(s["km_done"], 1)
                    pool.wait_ge(s["km_done"], 3 * c + a + 1)

            pool.wait_ge(s["weights_b"], 32)
            masked_keys(0)
            parts = [0]

            def split(dst, weights):
                parts[0] += 2
                pool.tensor_copy(dst[:, 0], weights).then_inc(s["weight_parts"], 1)
                pool.wait_ge(s["weight_parts"], parts[0] - 1)
                pool.tensor_tensor(dst[:, 1], weights, dst[:, 0], ALU.subtract).then_inc(s["weight_parts"], 1)
                pool.wait_ge(s["weight_parts"], parts[0])

            pool.wait_ge(s["weights_b"], 32)
            pool.wait_ge(s["weights_c"], 32)
            pool.wait_ge(s["h_mm"], 2 * NC)
            split(ga_parts, W_ga)
            split(B_v_parts, B_v)
            pool.wait_ge(s["kv_done"], 2)
            split(B_qk_parts, B_qk)
            masked_keys(1)
            pool.wait_ge(s["sc_done"], NG + 1)
            split(qkv_parts, W_qkv)
            pool.wait_ge(s["sc_done"], 2 * NG)
            pool.memset(v2, 0.0).then_inc(s["pool_chain"], 1)
            pool.wait_ge(s["pool_chain"], 1)
            pool.memset(v2[:, :, :, :, 0], 1.0).then_inc(s["v2_padded"], 1)
            pool.wait_ge(s["v2_padded"], 1)
            pool.wait_ge(s["av_done"], 2 * NG)
            pool.wait_ge(s["S1_done"], B)
            pool.memset(arena[64:128, :], 0.0).then_inc(s["rows_zero"], 1)
            pool.wait_ge(s["rows_zero"], 1)
            pool.wait_ge(s["wo_done"], 5)
            pool.memset(p_cls, 0.0).then_inc(s["pool_chain"], 1)
            pool.wait_ge(s["pool_chain"], 2)
            pool.memset(v_cls_parts, 0.0).then_inc(s["pool_chain"], 1)
            pool.wait_ge(s["pool_chain"], 3)
            pool.memset(v_cls, 0.0).then_inc(s["cls_padded"], 1)
            pool.wait_ge(s["cls_padded"], 1)
            pool.wait_ge(s["weights_b"], 32)
            pool.wait_ge(s["h1_done"], 1 + 2 * NC)
            pool.wait_ge(s["xh_done"], 7)
            pool.tensor_tensor(res_cls, h1_cls[0:B, :], b_proj[0:B, :], ALU.add).then_inc(s["res_done"], 1)
            for c in range(NC):
                for i in range(B):
                    pool.tensor_tensor(res[:, c, i, :], h1[:, c, i, :], b_proj, ALU.add).then_inc(s["res_done"], 1)
            for n in range(PAIRS):
                i, hd = n // H, n % H
                if hd == 0:
                    pool.wait_ge(s["p_clsq_done"], i + 1)
                if n >= SLOTS:
                    pool.wait_ge(s["pv_done"], n - SLOTS + 1)
                pool.tensor_copy(pT[:, n % SLOTS, :, 0], p_clsq[:, i % 2, hd, :]).then_inc(s["p_col_done"], 1)

        @block.scalar
        def _(act):
            chain = [0]

            def link(ins):
                chain[0] += 1
                ins.then_inc(s["act_chain"], 1)
                act.wait_ge(s["act_chain"], chain[0])

            def layer_norm(k):
                act.wait_ge(s["moments_done"], k + 1)
                t = slice(LN[k], LN[k + 1])
                link(act.activation(ln_var[:, t], moments[:, t, 1], ACT.Ln, bias=eps, scale=1.0))
                act.activation(rstd[:, t], ln_var[:, t], ACT.Exp, scale=-0.5).then_inc(s["rstd_done"], 1)

            def gate_parts(j):
                if j == 1:
                    act.wait_ge(s["y_done"], 3)
                act.activation(g_raw[j], GATES[j], ACT.Copy).then_inc(s["g_read"], 1)
                act.wait_ge(s["g_read"], GTURN[j])
                link(act.activation(g_abs[j], g_raw[j], ACT.Abs))
                link(act.activation(g_abs[j], g_abs[j], ACT.Exp, scale=-1.0))
                act.activation(g_abs[j], g_abs[j], ACT.Ln, bias=1.0).then_inc(s["g_log"], 1)

            def squares(c, pair):
                _, o, _, cols = norm_of(c, pair)
                act.activation(o_sq[c][:, :, cols], o, ACT.Square).then_inc(s["o_square"], 1)

            def mean_logs(c, pair):
                turn, _, ms, cols = norm_of(c, pair)
                act.wait_ge(s["ms_done"], turn)
                act.activation(o_ln[c][:, :, cols], ms, ACT.Ln, bias=eps[0:HALF], scale=1.0).then_inc(s["o_log"], 1)

            def weights(c, pair):
                turn, _, _, cols = norm_of(c, pair)
                act.wait_ge(s["weight_log"], turn)
                act.activation(o_sq[c][:, :, cols], g_w[c][:, :, cols], ACT.Exp).then_inc(s["weight"], 1)

            act.preload_act_table_set("natural_log_exp_and_others")
            act.wait_ge(s["weights_a"], 32)
            layer_norm(0)
            for i in range(1, 6, 2):
                act.wait_ge(s["M_done"], i + 1)
                act.activation(M[:, 2 * i:2 * i + 2, :], PS[0:HALF, 2 + i, 0:2 * D].rearrange("p (a n) -> p a n", a=2),
                               ACT.Copy).then_inc(s["M_evac"], 1)
            act.wait_ge(s["weights_b"], 32)
            act.wait_ge(s["cls_proj"], 1)
            gate_parts(2)
            act.activation(qkvg_parts[:, 0], qkvg, ACT.Copy).then_inc(s["qkvg_hi"], 1)
            act.wait_ge(s["o_cls"], 1)
            squares(*CLS)
            act.wait_ge(s["coarse_T"], 1)
            act.activation(T2t[:, :, :, :], PS[0:HALF, 4, :].rearrange("p (b j n) -> p j b n", b=B, j=8), ACT.Copy).then_inc(s["T2_evac"], 1)
            mean_logs(*CLS)
            weights(*CLS)
            act.wait_ge(s["Z_done"], 1)
            act.activation(Z1[:, :, :], PS[:, 6, 0:2 * D].rearrange("p (a n) -> p a n", a=2), ACT.Copy).then_inc(s["Z1_evac"], 1)
            layer_norm(1)

            def patches(c):
                act.wait_ge(s["T0_done"], c + 1)
                act.activation(T0t[:, c], PS[0:HALF, 4, 0:2 * TS].rearrange("p (a n) -> p a n", a=2), ACT.Copy).then_inc(s["T0_evac"], 1)

            def tokens(c):
                patches(c)
                layer_norm(2 + c)
                act.wait_ge(s["xh_T"], c + 1)
                for half in range(2):
                    act.activation(xT[c][:, 0, half, :], PS[0:HALF, XT_BANKS[c][half], :], ACT.Copy).then_inc(s["xT_hi"], 1)

            def decay_logs(c):
                act.wait_ge(s["z_done"], c + 1)
                act.activation(za[:, :], PS[0:HALF, Z_BANK[c], :], ACT.Abs, bias=b_gk, scale=1.0).then_inc(s["z_abs"], 1)
                act.wait_ge(s["z_abs"], c + 1)
                link(act.activation(za[:, :], za[:, :], ACT.Exp, scale=-1.0))
                act.activation(zl[:, :], za[:, :], ACT.Ln, bias=1.0).then_inc(s["z_log"], 1)

            def decays(c):
                act.wait_ge(s["Gc_done"], c + 1)
                if c:
                    act.wait_ge(s["qt_done"], c)
                    act.wait_ge(s["kt_done"], c)
                act.activation(Eq[:, :], Gc[:, :], ACT.Exp, scale=1.0 / GATE_NORM).then_inc(s["decays"], 1)
                act.activation(Ek[:, :], Gc[:, :], ACT.Exp, scale=-1.0 / GATE_NORM).then_inc(s["decays"], 1)
                by_image = Gs[:, :].rearrange("p (b t) -> p b t", b=B)
                about = Gc[:, :].rearrange("p (b t) -> p b t", b=B)
                act.activation(decay[:, c, 0, :], by_image[:, :, TS // 2 - 1], ACT.Exp, scale=1.0 / GATE_NORM)
                act.activation(decay[:, c, 1, :], about[:, :, TS - 1], ACT.Exp, scale=1.0 / GATE_NORM)
                act.activation(decay[:, c, 2, :], by_image[:, :, TS - 1], ACT.Exp, scale=1.0 / GATE_NORM).then_inc(s["decays"], 1)

            def values(c):
                for i in range(B):
                    act.wait_ge(s["v_done"], 2 * c + i // 2 + 1)
                    if c == 0 and i == 0:
                        act.wait_ge(s["pads_zero"], 1)
                    v = PS[:, 6 + i // 2, (i % 2) * D:(i % 2 + 1) * D]
                    act.activation(padded(Vp[:, c, i]), heads(v), ACT.Copy).then_inc(s["v_evac"], 1)

            tokens(0)
            decay_logs(0)
            decays(0)
            act.wait_ge(s["g_done"], 1)
            gate_parts(0)
            values(0)
            tokens(1)
            decay_logs(1)
            act.wait_ge(s["kT_done"], 1)
            act.activation(ktok[:, :, :], PS[:, 0, 0:B * HALF].rearrange("p (b n) -> p b n", b=B), ACT.Copy).then_inc(s["kT_evac"], 1)
            act.wait_ge(s["av_done"], NG)
            squares(0, 0)
            squares(0, 1)
            decays(1)
            for pair in range(2):
                mean_logs(0, pair)
            for pair in range(2):
                weights(0, pair)
            values(1)
            act.wait_ge(s["g_done"], 2)
            gate_parts(1)

            def inputs(u):
                c, images, _, banks = UNITS[u]
                layer_norm(4 + u)
                act.wait_ge(s["xh_T"], 2 + u + 1)
                for half in range(2):
                    act.activation(xT2[:, 0, half, images[0]:images[-1] + 1, 1 + c * TS:1 + (c + 1) * TS],
                                   PS[0:HALF, banks[half], 0:len(images) * TS].rearrange("p (b n) -> p b n", n=TS), ACT.Copy
                                   ).then_inc(s["x2_hi"], 1)

            def experts(u):
                _, images, at, _ = UNITS[u]
                t = slice(at, at + len(images) + (u == 0))
                act.wait_ge(s["logits_sub"], u + 1)
                act.activation(pr[:, 0, t, :], pr[:, 0, t, :], ACT.Exp).then_inc(s["logits_exp"], 1)

            def routed(u):
                c, images, _, banks = UNITS[u]
                act.wait_ge(s["aw_T"], u + 1)
                if u == 0:
                    for part in range(2):
                        act.activation(xT2[:, part, :, :, 0], x2_cls[:, part, :, 0:B], ACT.Copy)
                    act.activation(wT[:, 0, :, 0], PS[:, 4, 0:B], ACT.Copy)
                    act.activation(w_rep[:, 0, :], PS[:, 4, 0:H], ACT.Copy).then_inc(s["cls_cols"], 1)
                act.activation(wT[:, 0, images[0]:images[-1] + 1, 1 + c * TS:1 + (c + 1) * TS],
                               PS[:, banks[1], 0:len(images) * TS].rearrange("p (b n) -> p b n", n=TS), ACT.Copy
                               ).then_inc(s["wT_hi"], 1)

            inputs(0)
            experts(0)
            act.wait_ge(s["av_done"], NG + NG // 2)
            squares(1, 0)
            mean_logs(1, 0)
            routed(0)
            weights(1, 0)
            act.wait_ge(s["av_done"], 2 * NG)
            squares(1, 1)
            mean_logs(1, 1)
            weights(1, 1)
            inputs(1)
            experts(1)
            inputs(2)
            routed(1)

            def high_part(i, m):
                    act.wait_ge(s["work_full"], work_index(i, ("qk", m)) + 1)
                    if i >= 2 and m == 0:
                        act.wait_ge(s["bounced_hi"], 16 * (i - 1))
                    act.activation(qk_hi[:, i % 2, m, :], PS[0:HALF, work_bank(i, ("qk", m)), 0:T], ACT.Identity,
                                   bias=b_qk[:, m:m + 1], scale=1.0).then_inc(s["qk_hi_done"], 1)

            def cls_probs(i):
                act.wait_ge(s["p_cls_in"], i + 1)
                act.wait_ge(s["pads_zero"], 2)
                if i >= 2:
                    act.wait_ge(s["pv_done"], H * (i - 1))
                link(act.activation(s_clsk[:, :], s_clsk[:, :], ACT.Exp, scale=ATT_SCALE))
                act.activation(p_cls[0:H, i % 2, :], s_clsk[:, :], ACT.Copy)
                act.activation(p_cls[32:32 + H, i % 2, :], s_clsk[:, :], ACT.Copy).then_inc(s["p_cls_hi"], 1)

            def cls_query_probs(i):
                act.wait_ge(s["s_clsq_in"], i + 1)
                if i >= 2:
                    act.wait_ge(s["p_col_done"], H * (i - 1))
                act.activation(p_clsq[:, i % 2], s_clsq[:, i % 2], ACT.Exp, scale=ATT_SCALE).then_inc(s["p_clsq_done"], 1)

            def probs(n):
                act.wait_ge(s["sT_done"], n + 1)
                if n >= SLOTS:
                    act.wait_ge(s["pv_done"], n - SLOTS + 1)
                act.activation(pT[:, n % SLOTS, :, 1:T], PS[:, n % 2, :].rearrange("p (c t) -> p c t", c=NC), ACT.Exp, scale=ATT_SCALE
                               ).then_inc(s["p_done"], 1)

            def denominators(i, b):
                r = BANKS * i + b
                act.wait_ge(s["work_full"], work_index(i, ("den", b)) + 1)
                if r >= 2:
                    act.wait_ge(s["oT_done"], r - 1)
                act.activation(den_r[:, r % 2, :], PS[:, work_bank(i, ("den", b)), 0:T], ACT.Ln).then_inc(s["den_log"], 1)
                act.wait_ge(s["den_log"], r + 1)
                act.activation(den_r[:, r % 2, :], den_r[:, r % 2, :], ACT.Exp, scale=-1.0).then_inc(s["den_rec"], 1)

            def reads(uses):
                for i, key in uses:
                    if key[0] == "qk":
                        high_part(i, key[1])
                    elif key == ("ck",):
                        cls_probs(i)
                    elif key == ("cs",):
                        cls_query_probs(i)
                    elif key[0] == "den":
                        denominators(i, key[1])

            reads(START[0:ROUTE])
            experts(2)
            reads(START[ROUTE:TURNED])
            routed(2)
            reads(START[TURNED:])
            for g in range(STEPS):
                if g < PAIRS:
                    probs(g)
                reads(USES[g])

        @block.vector
        def _(dve):
            chain = [0]

            def link(ins):
                chain[0] += 1
                ins.then_inc(s["dve_chain"], 1)
                dve.wait_ge(s["dve_chain"], chain[0])

            def copy_then(out_, in_, sem):
                dve.tensor_copy(out_, in_).then_inc(s[sem], 1)

            def moments_of(k, tiles):
                for i, t in enumerate(tiles):
                    last = dve.bn_stats(stats[:, LN[k] + i, :], t)
                link(last)
                for i in range(LN[k], LN[k + 1]):
                    last = dve.bn_aggr(moments[:, i, :], stats[:, i, :])
                last.then_inc(s["moments_done"], 1)

            def normalise(k, tiles):
                dve.wait_ge(s["moments_done"], k + 1)
                dve.wait_ge(s["rstd_done"], k + 1)
                for i, t in enumerate(tiles):
                    last = dve.tensor_scalar(xh[k][:, i, :], t, moments[:, LN[k] + i, 0:1], rstd[:, LN[k] + i:LN[k] + i + 1],
                                             ALU.subtract, ALU.mult)
                last.then_inc(s["xh_done"], 1)

            def gate_logsig(j):
                dve.wait_ge(s["g_log"], GTURN[j])
                if j == 1:
                    dve.wait_ge(s["weight_log"], 3)
                dve.scalar_tensor_tensor(g_log[j], g_raw[j], 0.0, g_abs[j], ALU.min, ALU.subtract).then_inc(s["g_logsig"], 1)

            def weight_logs(c, pair):
                turn, _, _, cols = norm_of(c, pair)
                dve.wait_ge(s["o_log"], turn)
                dve.wait_ge(s["g_logsig"], GTURN[c])
                dve.scalar_tensor_tensor(g_w[c][:, :, cols], o_ln[c][:, :, cols], -0.5, g_log[c][:, :, cols], ALU.mult, ALU.add
                                         ).then_inc(s["weight_log"], 1)

            def outputs(c, pair):
                turn, o, _, cols = norm_of(c, pair)
                dve.wait_ge(s["weight"], turn)
                link(dve.scalar_tensor_tensor(g_w[c][:, :, cols], g_raw[c][:, :, cols], o_norm, o_sq[c][:, :, cols], ALU.mult, ALU.mult))
                dve.tensor_tensor(yT[c][:, :, cols], o, g_w[c][:, :, cols], ALU.mult).then_inc(s["y_done"], 1)

            dve.memset(Vp[:, 0, 0, 0:4, :], 0.0).then_inc(s["first_zeros"], 1)
            dve.wait_ge(s["first_zeros"], 1)
            dve.memset(arena[:, H * CW + 128:H * CW + NC * B * H * 32], 0.0).then_inc(s["pads_zero"], 1)

            dve.wait_ge(s["weights_a"], 32)
            moments_of(0, [cls_rows])
            normalise(0, [cls_rows])
            dve.wait_ge(s["bias_done"], 1)
            copy_then(bias_h[:, :], PS[:, 1, 0:D], "bias_evac")
            dve.wait_ge(s["cls_T"], 1)
            copy_then(xT_cls[:, :, :], PS[0:HALF, 0, 0:256].rearrange("p (i n) -> p i n", i=2), "xT_cls_evac")
            for i in range(0, 6, 2):
                dve.wait_ge(s["M_done"], i + 1)
                dve.tensor_copy(M[:, 2 * i:2 * i + 2, :], PS[0:HALF, 2 + i, 0:2 * D].rearrange("p (a n) -> p a n", a=2)
                                ).then_inc(s["M_evac"], 1)
            dve.wait_ge(s["Wgk_done"], 1)
            gk = PS[0:HALF, 0, 0:D].rearrange("p (i n) -> p i n", i=2)
            link(dve.tensor_copy(Wgk_parts[:, 0], gk))
            dve.tensor_tensor(Wgk_parts[:, 1], gk, Wgk_parts[:, 0], ALU.subtract).then_inc(s["Wgk_evac"], 1)
            dve.wait_ge(s["weights_b"], 32)
            dve.wait_ge(s["cls_proj"], 1)
            dve.tensor_scalar(q_cls[:, 0:4], PS[0:HALF, 1, 0:4], Q_SCALE, None, ALU.mult)
            link(dve.tensor_copy(q_cls[:, 4:8], PS[0:HALF, 1, 4:8]))
            dve.scalar_tensor_tensor(S0[:, :], PS[0:HALF, 1, 16:16 + D], q_cls[:, 4:5], blockdiag, ALU.mult, ALU.mult
                                     ).then_inc(s["S0_done"], 1)
            def permute(c):
                dve.wait_ge(s[f"gathered{c}"], 16 * GP)
                for i in range(B):
                    last = dve.tensor_copy(G0p[:, c, i, :, :], G0[:, c, :, CH * i:CH * (i + 1)])
                last.then_inc(s["perm_done"], 1)

            dve.wait_ge(s["gathered_coarse"], 16 * 10)
            dve.tensor_copy(G2p[:, :, :, :], G2[:, :, :].rearrange("p k (b d) -> p b k d", b=B))
            dve.tensor_copy(G1p[:, :, :, :], G1[:, :, :].rearrange("p k (b d) -> p b k d", b=B)).then_inc(s["perm_done"], 1)
            gate_logsig(2)
            dve.wait_ge(s["coarse_T"], 1)
            copy_then(T1t[:, :, :, :], PS[0:HALF, 5, :].rearrange("p (b k n) -> p k b n", b=B, k=2), "T1_evac")
            weight_logs(*CLS)
            outputs(*CLS)
            dve.wait_ge(s["qkvg_hi"], 1)
            dve.tensor_tensor(qkvg_parts[:, 1], qkvg, qkvg_parts[:, 0], ALU.subtract).then_inc(s["qkvg_lo"], 1)
            dve.wait_ge(s["Z_done"], 1)
            copy_then(Z2[:, :], PS[0:E, 7, 0:D], "Z2_evac")
            permute(0)
            dve.wait_ge(s["wo_done"], 1)
            dve.tensor_tensor(h1_cls[:, :], PS[:, 0, 0:D], cls_rows, ALU.add).then_inc(s["h1_done"], 1)
            dve.wait_ge(s["h1_done"], 1)
            moments_of(1, [h1_cls[:, :]])
            normalise(1, [h1_cls[:, :]])

            def add_bias(c):
                for a in range(2):
                    dve.wait_ge(s["h_mm"], 2 * c + a + 1)
                    last = dve.tensor_tensor(h[:, c, 2 * a:2 * a + 2, :], PS[:, H_BANKS[c][a], 0:2 * D].rearrange("p (a n) -> p a n", a=2),
                                             bias_h[:, :].unsqueeze(1).to_broadcast([128, 2, D]), ALU.add)
                    last.then_inc(s["h_evac"], 1)
                dve.wait_ge(s["h_evac"], 2 * (c + 1))

            def tiles_of(x, c):
                return [x[:, c, i, :] for i in range(B)]

            def features(c):
                for half in range(2):
                    dve.wait_ge(s["xT_hi"], 2 * c + half + 1)
                    dve.tensor_tensor(xT[c][:, 1, half, :], PS[0:HALF, XT_BANKS[c][half], :], xT[c][:, 0, half, :], ALU.subtract
                                      ).then_inc(s["xT_lo"], 1)

            def clipped(c):
                dve.wait_ge(s["z_abs"], c + 1)
                dve.tensor_scalar(zm[:, :], PS[0:HALF, Z_BANK[c], :], b_gk, 0.0, ALU.add, ALU.min).then_inc(s["z_read"], 1)

            def running_sums(c):
                dve.wait_ge(s["z_read"], c + 1)
                dve.wait_ge(s["z_log"], c + 1)
                link(dve.tensor_tensor(zm[:, :], zm[:, :], zl[:, :], ALU.subtract))
                if c:
                    dve.wait_ge(s["decays"], 3 * c)
                link(dve.tensor_tensor_scan(Gs[:, :], restart, zm[:, :], 0.0, ALU.mult, ALU.add))
                by_image = Gs[:, :].rearrange("p (b t) -> p b t", b=B)
                middle = by_image[:, :, TS // 2 - 1:TS // 2].to_broadcast([HALF, B, TS])
                dve.tensor_tensor(Gc[:, :].rearrange("p (b t) -> p b t", b=B), by_image, middle, ALU.subtract
                                  ).then_inc(s["Gc_done"], 1)

            def decayed(c):
                dve.wait_ge(s["decays"], 3 * c + 1)
                dve.wait_ge(s["q_done"], c + 1)
                dve.scalar_tensor_tensor(qt[:, c, :], PS[0:HALF, Q_BANK[c], :], Q_SCALE, Eq[:, :], ALU.mult, ALU.mult
                                         ).then_inc(s["qt_done"], 1)
                dve.wait_ge(s["decays"], 3 * c + 2)
                dve.wait_ge(s["k_done"], c + 1)
                dve.tensor_tensor(kt[:, c, :], PS[0:HALF, K_BANK[c], :], Ek[:, :], ALU.mult).then_inc(s["kt_done"], 1)

            def masked_queries(c):
                dve.wait_ge(s["qt_done"], c + 1)
                if c:
                    dve.wait_ge(s["sc_done"], NG * c)
                for a in range(4):
                    dve.tensor_scalar(qm[:, a, :], qt[:, c, :], in_group[:, a:a + 1], None, ALU.mult).then_inc(s["qm_done"], 1)

            def states_in(c):
                dve.wait_ge(s["decays"], 3 * c + 3)
                for i in range(B):
                    state = S0[:, :] if c == 0 else S1[:, i, :]
                    last = dve.tensor_scalar(Sc[:, c, i, :], state, decay[:, c, 0, i:i + 1], None, ALU.mult)
                last.then_inc(s["Sin_done"], 1)

            def causal_scores(c, g):
                n = NG * c + g
                dve.wait_ge(s["sc_done"], n + 1)
                if n >= 4:
                    dve.wait_ge(s["av_done"], n - 3)
                sc = PS[:, SC_BANKS[c][g % len(SC_BANKS[c])], :].rearrange("p (h t) -> p h t", h=4)
                dve.tensor_tensor(A[:, n % 4], sc, causal.unsqueeze(1).to_broadcast([128, 4, TS]), ALU.mult
                                  ).then_inc(s["A_done"], 1)

            def h1_sum(c, pair):
                dve.wait_ge(s["wo_done"], 1 + 2 * c + pair + 1)
                dve.tensor_tensor(h1[:, c, 2 * pair:2 * pair + 2, :],
                                  PS[:, WO_BANK[c][pair], 0:2 * D].rearrange("p (a n) -> p a n", a=2),
                                  h[:, c, 2 * pair:2 * pair + 2, :], ALU.add).then_inc(s["h1_done"], 1)

            def state_after():
                for i in range(B):
                    dve.wait_ge(s["kv_done"], i // 2 + 1)
                    bank = (3, 0)[i // 2]
                    link(dve.scalar_tensor_tensor(S1[:, i, :], PS[0:HALF, bank, (i % 2) * D:(i % 2 + 1) * D], decay[:, 0, 1, i:i + 1],
                                                  blockdiag, ALU.mult, ALU.mult))
                    dve.scalar_tensor_tensor(S1[:, i, :], S0[:, :], decay[:, 0, 2, i:i + 1], S1[:, i, :], ALU.mult, ALU.add
                                             ).then_inc(s["S1_done"], 1)
                dve.wait_ge(s["S1_done"], B)

            def unit_tiles(u):
                c, images, _, _ = UNITS[u]
                return [h1[:, c, i, :] for i in images]

            def inputs(u):
                c, images, _, banks = UNITS[u]
                for half in range(2):
                    dve.wait_ge(s["x2_hi"], 2 * u + half + 1)
                    x = [xT2[:, part, half, images[0]:images[-1] + 1, 1 + c * TS:1 + (c + 1) * TS] for part in range(2)]
                    dve.tensor_tensor(x[1], PS[0:HALF, banks[half], 0:len(images) * TS].rearrange("p (b n) -> p b n", n=TS), x[0],
                                      ALU.subtract).then_inc(s["x2_lo"], 1)

            def routed(u):
                c, images, _, banks = UNITS[u]
                dve.wait_ge(s["wT_hi"], u + 1)
                if u == 0:
                    dve.wait_ge(s["cls_cols"], 1)
                    dve.tensor_tensor(wT[:, 1, :, 0], PS[:, 4, 0:B], wT[:, 0, :, 0], ALU.subtract)
                    dve.tensor_tensor(w_rep[:, 1, :], PS[:, 4, 0:H], w_rep[:, 0, :], ALU.subtract)
                x = [wT[:, part, images[0]:images[-1] + 1, 1 + c * TS:1 + (c + 1) * TS] for part in range(2)]
                dve.tensor_tensor(x[1], PS[:, banks[1], 0:len(images) * TS].rearrange("p (b n) -> p b n", n=TS), x[0], ALU.subtract
                                  ).then_inc(s["wT_lo"], 1)

            def unit(u):
                _, images, at, banks = UNITS[u]
                blocks = [PS[:, banks[i // 2], (i % 2) * GW:(i % 2 + 1) * GW] for i in range(len(images))]
                if u == 0:
                    blocks.append(PS[:, 5, 2 * GW:3 * GW])
                t = slice(at, at + len(blocks))
                return blocks, [pr[:, a, t, :] for a in range(6)], [sm[:, a, t] for a in range(8)]

            def wide(x):
                return x.unsqueeze(2).to_broadcast([128, x.shape[1], NEXP])

            def gate_probs(u):
                blocks, P, r = unit(u)
                at = UNITS[u][2]
                dve.wait_ge(s["ga_done"], u + 1)
                for a, x in enumerate(blocks):
                    last = dve.tensor_tensor(logits[:, at + a, :], x[:, 0:NEXP], b_gate, ALU.add)
                link(last)
                lg = logits[:, at:at + len(blocks), :]
                link(dve.tensor_reduce(r[0], lg, AX.X, ALU.max))
                dve.tensor_tensor(P[0], lg, wide(r[0]), ALU.subtract).then_inc(s["logits_sub"], 1)
                dve.wait_ge(s["logits_exp"], u + 1)
                link(dve.tensor_reduce(r[1], P[0], AX.X, ALU.add))
                link(dve.reciprocal(r[2], r[1]))
                link(dve.tensor_tensor(P[1], P[0], wide(r[2]), ALU.mult))

            def choose(u, turn):
                _, P, r = unit(u)
                if turn == 1:
                    link(dve.scalar_tensor_tensor(P[4], P[2], -2.0, P[1], ALU.mult, ALU.add))
                left, n = P[1 if turn == 0 else 4], P[1].shape[1]
                link(dve.tensor_reduce(r[3 + 2 * turn], left, AX.X, ALU.max))
                link(dve.tensor_tensor(P[2 + turn], left, wide(r[3 + 2 * turn]), ALU.is_ge))
                link(dve.tensor_tensor(P[2 + turn], P[2 + turn], tie.unsqueeze(1).to_broadcast([128, n, NEXP]), ALU.mult))
                link(dve.tensor_reduce(r[4 + 2 * turn], P[2 + turn], AX.X, ALU.max))
                link(dve.tensor_tensor(P[2 + turn], P[2 + turn], wide(r[4 + 2 * turn]), ALU.is_equal))

            def weigh(u):
                blocks, P, _ = unit(u)
                at = UNITS[u][2]
                link(dve.tensor_tensor(P[5], P[2], P[3], ALU.add))
                link(dve.scalar_tensor_tensor(disp[:, at:at + len(blocks), :], P[5], LORA_SCALE, P[1], ALU.mult, ALU.mult))
                if u:
                    dve.wait_ge(s["aw_T"], u)
                for a, x in enumerate(blocks):
                    down = x[:, NEXP:NEXP + NR].rearrange("p (e r) -> p e r", e=NEXP)
                    last = dve.tensor_tensor(aw[:, a, :].rearrange("p (e r) -> p e r", e=NEXP), down,
                                             disp[:, at + a, :].unsqueeze(2).to_broadcast([128, NEXP, RANK]), ALU.mult)
                last.then_inc(s["aw_done"], 1)

            add_bias(0)
            moments_of(2, tiles_of(h, 0))
            normalise(2, tiles_of(h, 0))
            dve.wait_ge(s["cls_T"], 2)
            turned = PS[0:HALF, 2, 0:256].rearrange("p (i n) -> p i n", i=2)
            link(dve.tensor_copy(x2_cls[:, 0], turned))
            dve.tensor_tensor(x2_cls[:, 1], turned, x2_cls[:, 0], ALU.subtract).then_inc(s["x2_cls_done"], 1)
            features(0)
            clipped(0)
            running_sums(0)
            decayed(0)
            states_in(0)
            masked_queries(0)
            permute(1)
            for g in range(NG):
                causal_scores(0, g)
                if g == 3:
                    add_bias(1)
                    moments_of(3, tiles_of(h, 1))
                elif g == 5:
                    normalise(3, tiles_of(h, 1))
                elif g == 6:
                    gate_logsig(0)
                elif g == 8:
                    features(1)
                elif g == 10:
                    clipped(1)
            running_sums(1)
            state_after()
            decayed(1)
            states_in(1)
            for pair in range(2):
                weight_logs(0, pair)
            for pair in range(2):
                outputs(0, pair)
            masked_queries(1)
            for pair in range(2):
                h1_sum(0, pair)
            for g in range(NG):
                causal_scores(1, g)
                if g == 0:
                    dve.wait_ge(s["h1_done"], 3)
                    moments_of(4, unit_tiles(0))
                elif g == 1:
                    normalise(4, unit_tiles(0))
                elif g == 3:
                    inputs(0)
                elif g == 5:
                    gate_probs(0)
                elif g == 7:
                    choose(0, 0)
                elif g == 8:
                    choose(0, 1)
                elif g == 9:
                    weigh(0)
                elif g == 10:
                    gate_logsig(1)
            weight_logs(1, 0)
            outputs(1, 0)
            routed(0)
            h1_sum(1, 0)
            dve.wait_ge(s["h1_done"], 4)
            moments_of(5, unit_tiles(1))
            weight_logs(1, 1)
            normalise(5, unit_tiles(1))
            outputs(1, 1)
            inputs(1)
            h1_sum(1, 1)
            dve.wait_ge(s["h1_done"], 5)
            moments_of(6, unit_tiles(2))
            gate_probs(1)
            normalise(6, unit_tiles(2))
            choose(1, 0)
            choose(1, 1)
            weigh(1)
            inputs(2)
            routed(1)
            dve.wait_ge(s["cls_padded"], 1)
            dve.tensor_copy(v_cls[0:H, :, 0], ident[0:H, 0:H]).then_inc(s["pads_zero"], 1)
            dve.wait_ge(s["pads_zero"], 2)
            dve.wait_ge(s["v2_padded"], 1)

            def read(n):
                i, key = WORK[n]
                kind = key[0]
                if kind == "den":
                    return
                dve.wait_ge(s["work_full"], n + 1)
                ps = PS[:, bank_of(n), :]
                if kind == "qk":
                    m = key[1]
                    dve.wait_ge(s["qk_hi_done"], 4 * i + m + 1)
                    if i >= 2 and m == 0:
                        dve.wait_ge(s["bounced_lo"], 16 * (i - 1))
                    last = dve.scalar_tensor_tensor(qk_lo[:, i % 2, m, :], ps[0:HALF, 0:T], b_qk[:, m:m + 1],
                                                    qk_hi[:, i % 2, m, :], ALU.add, ALU.subtract)
                    last.then_inc(s["work_free"], 1)
                    if m == 3:
                        dve.wait_ge(s["work_free"], freed(n))
                        dve.nop().then_inc(s["bounced_out"], 1)
                        if i == 0:
                            for side in range(2):
                                for part, t in ((0, qk_hi), (1, qk_lo)):
                                    for half in range(2):
                                        last = dve.tensor_tensor(cls_qk[:, side, part, half, :], cls_heads[:, half, :],
                                                                 t[:, 0, 2 * side + half, 0:1].to_broadcast([HALF, H]), ALU.mult)
                            last.then_inc(s["cls_qk_done"], 1)
                elif kind == "vc":
                    v = v_cls[0:H, :, 1:1 + HD]

                    def by_head(t):
                        return t.rearrange("p (h v) -> p h v", h=H)

                    link(dve.tensor_tensor(v, by_head(ps[0:H, 0:D]), by_head(b_v[0:H, :]), ALU.add))
                    dve.tensor_tensor(v, v, by_head(to_heads), ALU.mult).then_inc(s["work_free"], 1)
                    dve.wait_ge(s["work_free"], freed(n))
                    link(dve.tensor_copy(v_cls_parts[0:H], v_cls[0:H]))
                    dve.tensor_copy(v_cls_parts[64:64 + H], v_cls_parts[0:H])
                    dve.tensor_tensor(v_cls_parts[32:32 + H], v_cls[0:H], v_cls_parts[0:H], ALU.subtract).then_inc(s["v_cls_done"], 1)
                elif kind == "v":
                    if i >= 2:
                        dve.wait_ge(s["pv_done"], H * (i - 1))
                    for c in range(NC):
                        last = dve.tensor_tensor(v2[:, i % 2, c, :, 1:1 + HD], ps[:, c * D:(c + 1) * D].rearrange("p (h v) -> p h v", h=H),
                                                 b_v.rearrange("p (h v) -> p h v", h=H), ALU.add)
                    last.then_inc(s["work_free"], 1)
                elif kind == "cq":
                    dve.tensor_reduce(mx_cls[:, i % 2:i % 2 + 1], ps[0:H, 0:T], AX.X, ALU.max).then_inc(s["work_free"], 1)
                elif kind == "max":
                    c, hd = key[1:]
                    dve.tensor_reduce(mx[:, i % 2, c, hd:hd + 1], ps[:, 0:T], AX.X, ALU.max).then_inc(s["work_free"], 1)
                elif kind == "mT":
                    if i >= 2:
                        dve.wait_ge(s["neg_m_stacked"], 16 * (i - 1))
                    dve.tensor_scalar(neg_m[:, i % 2, 0:1], mx_cls[:, i % 2:i % 2 + 1], -1.0, None, ALU.mult)
                    dve.tensor_scalar(neg_m[:, i % 2, 1:T], ps[0:H, 0:NTOK], -1.0, None, ALU.mult).then_inc(s["work_free"], 1)
                    dve.wait_ge(s["work_free"], freed(n))
                    dve.nop().then_inc(s["neg_m_done"], 1)
                elif kind == "ck":
                    if i >= 1:
                        dve.wait_ge(s["p_cls_done"], i)
                    dve.tensor_tensor(s_clsk[:, :], ps[0:H, 0:T], neg_m[:, i % 2, :], ALU.add).then_inc(s["work_free"], 1)
                    dve.wait_ge(s["work_free"], freed(n))
                    dve.nop().then_inc(s["p_cls_in"], 1)
                elif kind == "cs":
                    dve.wait_ge(s["p_cls_hi"], i + 1)
                    dve.tensor_tensor(p_cls[64:64 + H, i % 2, :], s_clsk[:, :], p_cls[0:H, i % 2, :], ALU.subtract
                                      ).then_inc(s["p_cls_done"], 1)
                    if i >= 2:
                        dve.wait_ge(s["p_clsq_done"], i - 1)
                    dve.tensor_copy(s_clsq[:, i % 2], ps[:, 0:H * NC].rearrange("p (h c) -> p h c", h=H)).then_inc(s["work_free"], 1)
                    dve.wait_ge(s["work_free"], freed(n))
                    dve.nop().then_inc(s["s_clsq_in"], 1)
                elif kind == "proj":
                    dve.wait_ge(s["res_done"], 1 + 2 * B)
                    dve.tensor_tensor(fin[:, :, i, :], ps[:, 0:2 * D].rearrange("p (c n) -> p c n", c=NC), res[:, :, i, :], ALU.add
                                      ).then_inc(s["work_free"], 1)
                    dve.wait_ge(s["work_free"], freed(n))
                    dve.nop().then_inc(s["fin_done"], 1)
                elif kind == "pc":
                    dve.tensor_tensor(fin_cls, ps[0:B, 0:D], res_cls, ALU.add).then_inc(s["fin_done"], 1)

            def take_raw(i, b):
                dve.wait_ge(s["pv_done"], H * i + 4 * b + 4)
                if i:
                    dve.wait_ge(s["oT_done"], BANKS * (i - 1) + b + 1)
                    dve.wait_ge(s["work_full"], work_index(i - 1, ("den", b)) + 1)
                dve.tensor_copy(raw[:, b, :], PS[:, 3 + b, 0:T]).then_inc(s["raw_done"], 1)

            def divide(i, b):
                r = BANKS * i + b
                dve.wait_ge(s["raw_done"], r + 1)
                dve.wait_ge(s["den_rec"], r + 1)
                if i >= 2 and b == 0:
                    dve.wait_ge(s["work_full"], work_index(i - 2, ("proj",)) + 1)
                dve.tensor_tensor(oT_cls[:, b, i:i + 1], raw[:, b, 0:1], den_r[:, r % 2, 0:1], ALU.mult)
                dve.tensor_tensor(oT[:, i % 2, b, :], raw[:, b, :], den_r[:, r % 2, :], ALU.mult).then_inc(s["oT_done"], 1)

            n_use = 0
            for k in range(len(START)):
                if k == ROUTE:
                    gate_probs(2)
                    choose(2, 0)
                    choose(2, 1)
                    weigh(2)
                if k == TURNED:
                    routed(2)
                read(n_use)
                n_use += 1
            for g in range(STEPS):
                for i, b in RAWS[g]:
                    take_raw(i, b)
                for i, b in DIVIDES[g]:
                    divide(i, b)
                for _ in USES[g]:
                    read(n_use)
                    n_use += 1

        @block.tensor
        def _(pe):
            def halves(out_, lhs, rhs):
                for half in range(2):
                    last = pe.matmul(out_, lhs[half], rhs[half], start=(half == 0), stop=(half == 1), skip_group_check=True)
                return last

            def products(out_, pairs):
                steps = [(lhs(a), rhs(b)) for a, b in ((0, 0), (0, 1), (1, 0)) for lhs, rhs in pairs]
                for n_, (lhs, rhs) in enumerate(steps):
                    last = pe.matmul(out_, lhs, rhs, start=(n_ == 0), stop=(n_ == len(steps) - 1), skip_group_check=True)
                return last

            def weights_by(parts, cols, x):
                return [(lambda a, half=half: parts[:, a, half, cols], lambda b, half=half: x(b, half)) for half in range(2)]

            def by_weights(x, parts):
                return [(lambda a, half=half: x(a, half), lambda b, half=half: parts[:, b, half, :]) for half in range(2)]

            def keep_clock(n, bank, operand):
                for _ in range(n):
                    pe.matmul(PS[:, bank, 0:128], operand, operand, start=True, stop=True)

            pe.wait_ge(s["first_zeros"], 1)
            keep_clock(11, 0, arena[:, H * CW:H * CW + 128])
            pe.wait_ge(s["weights_a"], 32)
            for i in range(3):
                last = pe.matmul(PS[:, 1, 0:D], b_rep[i], Wf[i], start=(i == 0), stop=(i == 2))
            last.then_inc(s["bias_done"], 1)
            factors = [(W0[:, i, :], 0) for i in range(2)] + [(W1[:, i, :], 1) for i in range(2)] + [(W2[:, i, :], 2) for i in range(8)]
            for i, (f, level) in enumerate(factors):
                last = pe.matmul(PS[0:HALF, 2 + i // 2, (i % 2) * D:(i % 2 + 1) * D], f, Wf[level][0:E], start=True, stop=True)
                if i % 2:
                    last.then_inc(s["M_done"], 1)
            pe.wait_ge(s["xh_done"], 1)
            for half in range(2):
                last = pe.transpose(PS[0:HALF, 0, half * 128:(half + 1) * 128], xh[0][:, 0, half * HALF:(half + 1) * HALF], ident)
            last.then_inc(s["cls_T"], 1)
            pe.wait_ge(s["xT_cls_evac"], 1)
            for half in range(2):
                last = pe.matmul(PS[0:HALF, 0, half * HALF:(half + 1) * HALF], Wgk1[:, half, :], Wgk2, start=True, stop=True)
            last.then_inc(s["Wgk_done"], 1)
            pe.wait_ge(s["weights_b"], 32)
            pe.wait_ge(s["bias_evac"], 1)
            pe.wait_ge(s["M_evac"], 6)
            x4 = [xT_cls[:, i, 0:B] for i in range(2)]
            halves(PS[0:HALF, 1, 0:4], [Wq[:, i, :] for i in range(2)], x4)
            halves(PS[0:HALF, 1, 4:8], [Wk[:, i, :] for i in range(2)], x4)
            for m in range(2):
                halves(PS[0:HALF, 4, 4 * m:4 * m + 4], [Wg[:, i, m * HALF:(m + 1) * HALF] for i in range(2)], x4)
            halves(PS[0:HALF, 1, 16:16 + D], [xT_cls[:, i, 0:HALF] for i in range(2)], [Wv[:, i, :] for i in range(2)]
                   ).then_inc(s["cls_proj"], 1)
            pe.wait_ge(s["S0_done"], 1)
            for m in range(2):
                last = pe.matmul(PS[0:HALF, 2, 4 * m:4 * m + 4], S0[:, m * HALF:(m + 1) * HALF], q_cls[:, 0:4], start=True, stop=True)
            last.then_inc(s["o_cls"], 1)

            def mean_squares(c, pair):
                turn, _, ms, cols = norm_of(c, pair)
                pe.wait_ge(s["o_square"], turn)
                pe.matmul(ms, head_mean, o_sq[c][:, :, cols], start=True, stop=True).then_inc(s["ms_done"], 1)

            pe.wait_ge(s["perm_done"], 1)
            pe.wait_ge(s["g_read"], 1)
            for i in range(B):
                pe.transpose(PS[0:HALF, 4, i * 128:(i + 1) * 128], G2p[:, i, :, :], ident)
            for i in range(B):
                last = pe.transpose(PS[0:HALF, 5, i * 128:(i + 1) * 128], G1p[:, i, :, :], ident)
            last.then_inc(s["coarse_T"], 1)
            mean_squares(*CLS)
            pe.wait_ge(s["T1_evac"], 1)
            for a in range(2):
                for half in range(2):
                    pe.matmul(PS[:, 6, a * D:(a + 1) * D], T1t[:, half, 2 * a:2 * a + 2, :], M[:, 2 + half, :],
                              start=(half == 0), stop=(half == 1))
            pe.wait_ge(s["T2_evac"], 1)
            for j in range(8):
                last = pe.matmul(PS[0:E, 7, 0:D], T2t[:, j, :, :], M[:, 4 + j, :], start=(j == 0), stop=(j == 7))
            last.then_inc(s["Z_done"], 1)
            pe.wait_ge(s["y_done"], 1)
            pe.wait_ge(s["Wgk_evac"], 1)
            halves(PS[:, 0, 0:D], [yT[2][:, i, 0:1].to_broadcast([HALF, 128]) for i in range(2)], [Wo[:, i, :] for i in range(2)]
                   ).then_inc(s["wo_done"], 1)

            def patches(c):
                pe.wait_ge(s["perm_done"], c + 2)
                if c == 0:
                    pe.wait_ge(s["T2_evac"], 1)
                else:
                    pe.wait_ge(s["g_read"], 2)
                for a in range(2):
                    last = pe.transpose(PS[0:HALF, 4, a * TS:(a + 1) * TS], G0p[:, c, 2 * a:2 * a + 2, :, :], ident)
                last.then_inc(s["T0_done"], 1)

            def tokens_of(c, i):
                return PS[:, H_BANKS[c][i // 2], (i % 2) * D:(i % 2 + 1) * D]

            def coarse_tokens(c):
                if c == 0:
                    pe.wait_ge(s["weights_c"], 32)
                    pe.wait_ge(s["Z1_evac"], 1)
                    pe.wait_ge(s["Z2_evac"], 1)
                for i in range(B):
                    pe.matmul(tokens_of(c, i), interp1[:, i % 2, c, :], Z1[:, i // 2, :], start=(i % 2 == 0), stop=False, skip_group_check=True)
                    pe.matmul(tokens_of(c, i), interp2[:, i, c, :], Z2[:, :], start=False, stop=False, skip_group_check=True)

            def tokens(c):
                pe.wait_ge(s["T0_evac"], c + 1)
                if c:
                    coarse_tokens(c)
                for i in range(B):
                    last = pe.matmul(tokens_of(c, i), T0t[:, c, i // 2, :], M[:, i % 2, :], start=False, stop=True, skip_group_check=True)
                    if i % 2:
                        last.then_inc(s["h_mm"], 1)

            def features(c):
                pe.wait_ge(s["xh_done"], 2 + c + 1)
                pe.wait_ge(s["h_evac"], 2 * (c + 1))
                for half in range(2):
                    for i in range(B):
                        last = pe.transpose(PS[0:HALF, XT_BANKS[c][half], i * TS:(i + 1) * TS],
                                            xh[2 + c][:, i, half * HALF:(half + 1) * HALF], ident)
                last.then_inc(s["xh_T"], 1)

            def columns(c):
                return lambda part, half: xT[c][:, part, half, :]

            ALL = slice(0, HALF)

            def decay_inputs(c):
                pe.wait_ge(s["xT_lo"], 2 * (c + 1))
                products(PS[0:HALF, Z_BANK[c], :], weights_by(Wgk_parts, ALL, columns(c))).then_inc(s["z_done"], 1)

            def queries(c):
                pe.wait_ge(s["qkvg_lo"], 1)
                if c:
                    pe.wait_ge(s["z_read"], c + 1)
                products(PS[0:HALF, Q_BANK[c], :], weights_by(gla_weights("Wq"), ALL, columns(c))).then_inc(s["q_done"], 1)

            def keys(c):
                products(PS[0:HALF, K_BANK[c], :], weights_by(gla_weights("Wk"), ALL, columns(c))).then_inc(s["k_done"], 1)

            def gates(c):
                if c:
                    pe.wait_ge(s["qt_done"], c + 1)
                    pe.wait_ge(s["kt_done"], c + 1)
                for m in range(2):
                    cols = slice(m * HALF, (m + 1) * HALF)
                    last = products(PS[0:HALF, 4 + m, :], weights_by(gla_weights("Wg"), cols, columns(c)))
                last.then_inc(s["g_done"], 1)

            def values_in(c):
                if c:
                    pe.wait_ge(s["o_log"], 3)
                for i in range(B):
                    x = lambda part, half: xT[c][:, part, half, i * TS:(i + 1) * TS]
                    last = products(PS[:, 6 + i // 2, (i % 2) * D:(i % 2 + 1) * D], by_weights(x, gla_weights("Wv")))
                    if i % 2:
                        last.then_inc(s["v_done"], 1)

            def linear_attention(c):
                pe.wait_ge(s["qt_done"], c + 1)
                pe.wait_ge(s["kt_done"], c + 1)
                pe.wait_ge(s["Sin_done"], c + 1)
                for i in range(B):
                    if c and i % 2 == 0:
                        pe.wait_ge(s["y_done"], 2 + i // 2)
                    for m in range(2):
                        pe.matmul(PS[0:HALF, 1 + i // 2, m * PW + (i % 2) * TS:m * PW + (i % 2 + 1) * TS], Sc[:, c, i, m * HALF:(m + 1) * HALF],
                                  qt[:, c, i * TS:(i + 1) * TS], start=(i % 2 == 0 and m == 0), stop=False, skip_group_check=True)
                pe.wait_ge(s["z_read"], c + 1)
                pe.wait_ge(s["v_evac"], B * (c + 1))
                if c:
                    pe.wait_ge(s["h1_done"], 3)
                ring = len(SC_BANKS[c])

                def scores(n):
                    g = n - NG * c
                    i, hg = g // 3, g % 3
                    pe.wait_ge(s["qm_done"], 4 * (c + 1))
                    pe.wait_ge(s["km_done"], 3 * c + hg + 1)
                    if g >= ring:
                        pe.wait_ge(s["A_done"], n - ring + 1)
                    pe.matmul(PS[:, SC_BANKS[c][g % ring], :], km[:, hg, i * TS:(i + 1) * TS],
                              qm[:, :, i * TS:(i + 1) * TS], start=True, stop=True).then_inc(s["sc_done"], 1)

                def values(n):
                    g = n - NG * c
                    i, hg = g // 3, g % 3
                    pe.wait_ge(s["A_done"], n + 1)
                    for a in (0, 2, 1, 3):
                        hd = 4 * hg + a
                        pair = hd // 2
                        row = 32 * (pair % 3)
                        at = pair // 3 * PW + (i % 2) * TS
                        last = pe.matmul(PS[row:row + 32, 1 + i // 2, at:at + TS], Vp[:, c, i, hd, :], A[:, n % 4, a, :],
                                         start=False, stop=False, skip_group_check=True)
                    last.then_inc(s["av_done"], 1)

                for g in range(NG + 2):
                    if g < NG:
                        scores(NG * c + g)
                    if g >= 2:
                        values(NG * c + g - 2)
                    if c == 0:
                        if g == 1:
                            patches(1)
                        elif g == 3:
                            tokens(1)
                        elif g == 7:
                            features(1)
                        elif g == 9:
                            decay_inputs(1)
                            keys(1)
                        elif g == 11:
                            queries(1)
                    else:
                        if g == 3:
                            input_features(0)
                        elif g == 5:
                            gates_and_downs(0)
                        elif g == 10:
                            mean_squares(1, 0)
                        elif g == 12:
                            weighted_downs(0)

            def out_projection(c, pair):
                pe.wait_ge(s["y_done"], 1 + 2 * c + pair + 1)
                if c == 0:
                    pe.wait_ge(s["S1_done"], B)
                for i in (2 * pair, 2 * pair + 1):
                    last = halves(PS[:, WO_BANK[c][pair], (i % 2) * D:(i % 2 + 1) * D],
                                  [yT[c][:, a, i * TS:(i + 1) * TS] for a in range(2)], [Wo[:, a, :] for a in range(2)])
                last.then_inc(s["wo_done"], 1)

            def input_features(u):
                _, images, _, banks = UNITS[u]
                pe.wait_ge(s["xh_done"], 4 + u + 1)
                if u == 0:
                    pe.wait_ge(s["g_read"], 3)
                elif u == 1:
                    pe.wait_ge(s["wT_lo"], 1)
                else:
                    pe.wait_ge(s["A_done"], 2 * NG)
                    pe.wait_ge(s["y_done"], 5)
                for half in range(2):
                    for i in range(len(images)):
                        last = pe.transpose(PS[0:HALF, banks[half], i * TS:(i + 1) * TS],
                                            xh[4 + u][:, i, half * HALF:(half + 1) * HALF], ident)
                last.then_inc(s["xh_T"], 1)

            def gates_and_downs(u):
                c, images, _, banks = UNITS[u]
                pe.wait_ge(s["x2_lo"], 2 * (u + 1))
                pe.wait_ge(s["weight_parts"], 2)
                for n, i in enumerate(images):
                    x = lambda part, half: xT2[:, part, half, i, 1 + c * TS:1 + (c + 1) * TS]
                    last = products(PS[:, banks[n // 2], (n % 2) * GW:(n % 2 + 1) * GW], by_weights(x, W_ga_parts))
                if u == 0:
                    last = products(PS[:, 5, 2 * GW:3 * GW], by_weights(lambda part, half: x2_cls[:, part, half, :], W_ga_parts))
                last.then_inc(s["ga_done"], 1)

            def weighted_downs(u):
                _, images, _, banks = UNITS[u]
                pe.wait_ge(s["aw_done"], u + 1)
                for i in range(len(images)):
                    last = pe.transpose(PS[:, banks[1], i * TS:(i + 1) * TS], aw[:, i, :], ident)
                if u == 0:
                    last = pe.transpose(PS[:, 4, 0:TS], aw[:, B, :], ident)
                last.then_inc(s["aw_T"], 1)

            coarse_tokens(0)
            keep_clock(4, 3, ident)
            patches(0)
            tokens(0)
            pe.wait_ge(s["xh_done"], 2)
            for half in range(2):
                last = pe.transpose(PS[0:HALF, 2, half * 128:(half + 1) * 128], xh[1][:, 0, half * HALF:(half + 1) * HALF], ident)
            last.then_inc(s["cls_T"], 1)
            keep_clock(12, 3, ident)
            features(0)
            keep_clock(6, 3, ident)
            decay_inputs(0)
            queries(0)
            pe.wait_ge(s["x2_cls_done"], 1)
            keys(0)
            gates(0)
            values_in(0)
            keep_clock(8, 0, ident)
            linear_attention(0)
            pe.wait_ge(s["A_done"], NG)
            for i in range(B):
                last = pe.transpose(PS[:, 0, i * HALF:(i + 1) * HALF], kt[:, 0, i * TS:(i + 1) * TS], ident96)
            last.then_inc(s["kT_done"], 1)
            pe.wait_ge(s["kT_evac"], 1)
            for i in range(B):
                last = pe.matmul(PS[0:HALF, (3, 0)[i // 2], (i % 2) * D:(i % 2 + 1) * D], ktok[:, i, :], padded(Vp[:, 0, i]),
                                 start=True, stop=True)
                if i % 2:
                    last.then_inc(s["kv_done"], 1)
            mean_squares(0, 0)
            mean_squares(0, 1)
            gates(1)
            values_in(1)
            out_projection(0, 0)
            out_projection(0, 1)
            linear_attention(1)
            pe.wait_ge(s["A_done"], 2 * NG)
            keep_clock(4, 0, ident)
            mean_squares(1, 1)
            out_projection(1, 0)
            keep_clock(12, 0, ident)
            input_features(1)
            out_projection(1, 1)
            gates_and_downs(1)
            keep_clock(8, 0, ident)
            input_features(2)
            keep_clock(8, 3, ident)
            weighted_downs(1)
            gates_and_downs(2)
            pe.wait_ge(s["wT_lo"], 2)
            pe.wait_ge(s["weight_parts"], 8)
            pe.wait_ge(s["pads_zero"], 2)
            pe.wait_ge(s["o_log"], 5)

            at = [0]

            def work(i, key):
                n = at[0]
                at[0] += 1
                assert WORK[n] == (i, key)
                before = former(n)
                if before is not None:
                    if WORK[before][1][0] == "den":
                        pe.wait_ge(s["den_log"], dens(before))
                    else:
                        pe.wait_ge(s["work_free"], freed(before))
                ps = PS[:, bank_of(n), :]
                kind = key[0]
                if kind == "qk":
                    m = key[1]
                    if i >= 2:
                        pe.wait_ge(s["wT_lo"], 3)
                    cols = slice(m * HALF, (m + 1) * HALF)
                    last = products(ps[0:HALF, 0:T], weights_by(W_qk_parts, cols, lambda part, half: xT2[:, part, half, i, :])
                                    + [(lambda a: B_qk_parts[:, a, cols], lambda b: wT[:, b, i, :])])
                elif kind == "vc":
                    last = products(ps[0:H, 0:D], by_weights(lambda part, half: x2_cls[:, part, half, 0:H], W_v_parts)
                                    + [(lambda a: w_rep[:, a, :], lambda b: B_v_parts[:, b, :])])
                elif kind == "v":
                    for c in range(NC):
                        cols = slice(1 + c * TS, 1 + (c + 1) * TS)
                        last = products(ps[:, c * D:(c + 1) * D], by_weights(lambda part, half: xT2[:, part, half, i, cols], W_v_parts)
                                        + [(lambda a: wT[:, a, i, cols], lambda b: B_v_parts[:, b, :])])
                elif kind in ("cq", "ck"):
                    if kind == "cq" and i == 0:
                        pe.wait_ge(s["cls_qk_done"], 1)
                    if kind == "cq":
                        pe.wait_ge(s["bounced_out"], i + 1)
                    side = 0 if kind == "cq" else 1
                    steps = [(a, b, half) for a, b in ((0, 0), (0, 1), (1, 0)) for half in range(2)]
                    for n_, (a, b, half) in enumerate(steps):
                        t = (qk_hi, qk_lo)[b]
                        last = pe.matmul(ps[0:H, 0:T], cls_qk[:, side, a, half, :], t[:, i % 2, 2 * (1 - side) + half, :],
                                         start=(n_ == 0), stop=(n_ == len(steps) - 1))
                elif kind == "max":
                    c, hd = key[1:]
                    if c == 0 and hd == 0:
                        pe.wait_ge(s["stacked"], 128 * (i + 1))
                        pe.wait_ge(s["rows_zero"], 1)
                        pe.wait_ge(s["ones_stacked"], 16)
                    last = pe.matmul(ps[:, 0:T], stack[:, i, 0, hd, 1 + c * TS:1 + (c + 1) * TS], stack[:, i, 1, hd, :],
                                     start=True, stop=True)
                elif kind == "mT":
                    pe.wait_ge(s["work_free"], freed(work_index(i, ("max", NC - 1, H - 1))))
                    for c in range(NC):
                        last = pe.transpose(ps[0:H, c * TS:(c + 1) * TS], mx[:, i % 2, c, :], ident)
                elif kind == "cs":
                    pe.wait_ge(s["neg_m_stacked"], 16 * (i + 1))
                    pe.wait_ge(s["ones_stacked"], 16)
                    for hd in range(H):
                        for c in range(NC):
                            last = pe.matmul(ps[:, NC * hd + c:NC * hd + c + 1], stack[:, i, 1, hd, 1 + c * TS:1 + (c + 1) * TS],
                                             stack[:, i, 0, hd, 0:1], start=True, stop=True)
                elif kind == "den":
                    pe.wait_ge(s["raw_done"], BANKS * i + key[1] + 1)
                    last = pe.matmul(ps[:, 0:T], den_rows, raw[:, key[1], :], start=True, stop=True)
                elif kind == "proj":
                    for b in range(BANKS):
                        pe.wait_ge(s["oT_done"], BANKS * i + b + 1)
                        for c in range(NC):
                            last = pe.matmul(ps[:, c * D:(c + 1) * D], oT[:, i % 2, b, 1 + c * TS:1 + (c + 1) * TS], W_proj[:, b, :],
                                             start=(b == 0 and c == 0), stop=(b == BANKS - 1), skip_group_check=True)
                elif kind == "pc":
                    for b in range(BANKS):
                        last = pe.matmul(ps[0:B, 0:D], oT_cls[:, b, :], W_proj[:, b, :], start=(b == 0), stop=(b == BANKS - 1))
                last.then_inc(s["work_full"], 1)

            def key_scores(n):
                i, hd = n // H, n % H
                if n >= 2:
                    pe.wait_ge(s["p_done"], n - 1)
                for c in range(NC):
                    last = pe.matmul(PS[:, n % 2, c * NTOK:(c + 1) * NTOK], stack[:, i, 1, hd, 1 + c * TS:1 + (c + 1) * TS],
                                     stack[:, i, 0, hd, 1:T], start=True, stop=True)
                last.then_inc(s["sT_done"], 1)

            def weighted_values(i, b):
                first = H * i + 4 * b
                if i:
                    pe.wait_ge(s["raw_done"], BANKS * (i - 1) + b + 1)
                pe.wait_ge(s["p_cls_done"], i + 1)
                pe.wait_ge(s["v_cls_done"], 1)
                pe.matmul(PS[:, 3 + b, 0:T], v_cls_parts[:, 4 * b:4 * b + 4, :], p_cls[:, i % 2, :], start=True, stop=False,
                          skip_group_check=True)
                for c in range(NC):
                    for a in range(4):
                        n = first + a
                        if c == 0:
                            pe.wait_ge(s["p_done"], n + 1)
                            pe.wait_ge(s["p_col_done"], n + 1)
                        last = pe.matmul(PS[32 * a:32 * a + 32, 3 + b, 0:T], v2[:, i % 2, c, 4 * b + a, :], pT[:, n % SLOTS, c, :],
                                         start=False, stop=False, skip_group_check=True)
                        if c == NC - 1:
                            last.then_inc(s["pv_done"], 1)

            for j, key in START[0:TURNED]:
                work(j, key)
            weighted_downs(2)
            for j, key in START[TURNED:]:
                work(j, key)
            pe.wait_ge(s["wT_lo"], 3)
            for g in range(STEPS):
                if g < PAIRS:
                    key_scores(g)
                for j, key in USES[g]:
                    work(j, key)
                if 0 <= g - LAG < PAIRS and (g - LAG) % 4 == 3:
                    weighted_values((g - LAG) // H, (g - LAG) % H // 4)


def interpolation(length, n_out):
    pos = (np.arange(n_out, dtype=np.float32) + np.float32(0.5)) * np.float32(length / n_out) - np.float32(0.5)
    pos = np.clip(pos, np.float32(0), np.float32(length - 1))
    lo = np.floor(pos).astype(np.int32)
    up = np.minimum(lo + 1, length - 1)
    frac = (pos - lo).astype(np.float32)
    m = np.zeros((length, n_out), np.float32)
    np.add.at(m, (lo, np.arange(n_out)), np.float32(1) - frac)
    np.add.at(m, (up, np.arange(n_out)), frac)
    return m

def kernel(**inputs):
    import concourse.bacc as bacc
    from concourse.bass_utils import run_bass_kernel_spmd

    a = {k.replace("L0_", ""): np.asarray(v) for k, v in inputs.items()}
    x = a["x"]
    f32 = np.float32

    def patches(p):
        n = IMG // p
        return np.ascontiguousarray(x.reshape(B, CH, n, p, n, p).transpose(2, 4, 0, 3, 5, 1).reshape(n * n, B * p * p * CH))

    index = np.concatenate([
        a["tok_idx2"].reshape(NT2, 2, 8).transpose(2, 0, 1).reshape(128, 2),
        a["tok_idx1"].reshape(NT1, 2, 8).transpose(1, 0, 2).reshape(128, 8),
        a["tok_idx0"].reshape(NC, TS, GP).transpose(1, 0, 2).reshape(128, NC * GP)], axis=1)

    def split(m):
        return m.reshape(2, HALF, -1).transpose(1, 0, 2).reshape(HALF, -1)

    def rows(v, n):
        return np.broadcast_to(v.reshape(1, -1), (n, v.size))

    i1, i2 = interpolation(NT1, NTOK), interpolation(NT2, NTOK)
    interp1 = np.zeros((2, NT1, 2, NC, TS), f32)
    for p in range(2):
        interp1[p, :, p] = i1.reshape(NT1, NC, TS)
    interp2 = np.zeros((B, NT2, B, NC, TS), f32)
    for p in range(B):
        interp2[p, :, p] = i2.reshape(NT2, NC, TS)
    W0 = np.zeros((E, 2, 2, 48), f32)
    for p in range(2):
        W0[:, p, p] = a["tok_W0"]
    WfT = a["tok_Wf"].T
    heads96 = np.arange(HALF) // HD
    den_rows = np.zeros((4, 32, 4, 32), f32)
    den_rows[np.arange(4), 0, np.arange(4), :] = 1
    W_proj = np.zeros((4, 32, BANKS, D), f32)
    W_proj[:, 1:1 + HD] = a["ffn_W_proj"].T.reshape(BANKS, 4, HD, D).transpose(1, 2, 0, 3)
    cls_heads = np.zeros((HALF, 2, H), f32)
    to_heads = np.zeros((H, 2, HALF), f32)
    for half in range(2):
        cls_heads[np.arange(HALF), half, half * HH + heads96] = 1
        to_heads[half * HH + heads96, half, np.arange(HALF)] = 1
    restart = np.ones((HALF, B, TS), f32)
    restart[:, :, 0] = 0
    lora_up = a["ffn_B_lora"].transpose(0, 2, 1).reshape(NR, 3 * D)
    W_qkvT = a["ffn_W_qkv"].T
    parts = {
        "ident": np.eye(128, dtype=f32), "cls": rows(a["cls_tok"], 128), "interp1": interp1.reshape(128, -1),
        "causal": np.triu(np.ones((TS, TS), f32)), "eps": np.full((128, 1), EPS, f32), "b_gate": rows(a["ffn_b_gate"], 128),
        "tie": rows(np.arange(NEXP, 0, -1).astype(f32), 128), "b_proj": rows(a["ffn_b_proj"], 128),
        "b_v": rows(a["ffn_b_qkv"][2 * D:], 128), "B_qk": lora_up[:, 0:2 * D], "B_v": lora_up[:, 2 * D:],
        "den_rows": den_rows.reshape(128, -1), "W_proj": W_proj.reshape(128, -1),
        "Wq": split(a["attn_Wq"]), "Wk": split(a["attn_Wk"]), "Wv": split(a["attn_Wv"]), "Wg": split(a["attn_Wg"]),
        "b_gk": a["attn_bgk2"].reshape(HALF, 1), "o_norm": np.tile(a["attn_o_norm_w"], HH).reshape(HALF, 1),
        "blockdiag": (np.arange(HALF)[:, None] // HK == np.arange(D)[None] // HV).astype(f32),
        "in_group": (np.arange(HALF)[:, None] // HK % 4 == np.arange(4)[None]).astype(f32),
        "group": (np.arange(HALF)[:, None] // (4 * HK) == np.arange(3)[None]).astype(f32),
        "head_mean": (heads96[:, None] == heads96[None]).astype(f32) / f32(HV), "restart": restart.reshape(HALF, -1),
        "Wo": split(a["attn_Wo"]),
        "W_ga": split(np.concatenate([a["ffn_W_gate"].T, a["ffn_A"].reshape(NR, D).T], axis=1)),
        "W_qk": split(W_qkvT[:, 0:2 * D]), "W_v": split(W_qkvT[:, 2 * D:]), "b_qk": a["ffn_b_qkv"][0:2 * D].reshape(4, HALF).T,
        "cls_heads": cls_heads.reshape(HALF, -1),
        "b0": np.broadcast_to(a["tok_b0"][:, None], (E, 128)), "b1": np.broadcast_to(a["tok_b1"][:, None], (E, 128)),
        "b2": np.concatenate([np.broadcast_to(a["tok_b2"][:, None], (E, 128)), np.ones((1, 128), f32)]),
        "Wf0": WfT[0:E], "Wf1": WfT[E:2 * E], "Wf2": np.concatenate([WfT[2 * E:], a["tok_bf"].reshape(1, D)]),
        "W0": W0.reshape(E, -1), "W1": a["tok_W1"],
        "W2": a["tok_W2"].reshape(E, 2, 8, 48).transpose(0, 2, 1, 3).reshape(E, -1),
        "Wgk1": a["attn_Wgk1"].T, "Wgk2": a["attn_Wgk2"], "interp2": interp2.reshape(E, -1), "to_heads": to_heads.reshape(H, -1),
    }
    arrays = {"pix0": patches(1), "pix1": patches(2), "pix2": patches(4), "index": np.ascontiguousarray(index),
              "ones": np.ones((1, B, H, T), np.float16)}
    for p, blocks in PACKS.items():
        at, n = offsets(p)
        packed = np.zeros((ROWS[p], n), f32)
        for name, cols in blocks:
            m = parts[name]
            packed[0:m.shape[0], at[name][0]:at[name][0] + cols] = m
        arrays[p] = packed

    nc = bacc.Bacc("TRN2", target_bir_lowering=False, num_devices=1)
    args = [nc.dram_tensor("in_" + n, v.shape, mybir.dt.from_np(v.dtype), kind="ExternalInput").ap() for n, v in arrays.items()]
    out = nc.dram_tensor("out_0", (B, T, D), F32, kind="ExternalOutput").ap()
    build(nc, *args, out)
    r = run_bass_kernel_spmd(nc, [{"in_" + n: v for n, v in arrays.items()}], core_ids=[0])
    return r.results[0]["out_0"]
```
